# Optimizing a Trainium2 kernel written in Bass

```python
import numpy as np
import jax
import jax.numpy as jnp

def _softmax(x, axis=-1):
    return jax.nn.softmax(x, axis=axis)

def _gelu(x):
    return jax.nn.gelu(x, approximate=True)

def _silu(x):
    return jax.nn.silu(x)

def _sigmoid(x):
    return jax.nn.sigmoid(x)

def _layernorm(x, axis=-1, eps=1e-05):
    m = jnp.mean(x, axis=axis, keepdims=True)
    v = jnp.var(x, axis=axis, keepdims=True)
    return (x - m) / jnp.sqrt(v + eps)

def _scatter_add(tgt, idx, src, axis=0):
    return tgt.at[idx].add(src)

def _segment_sum(src, seg, n):
    return jax.ops.segment_sum(src, seg, n)
kernel_name = 'mk_perceiver_d2_seqx_r8_5d47d2'

def setup_inputs(seed: int=0):
    np.random.seed(seed)
    _w = jnp.asarray

    def _rec_inputs():
        import jax
        import jax.numpy as jnp
        _rk = jax.random.key(seed)
        x = -0.0003929 + 0.9999 * jax.random.normal(jax.random.fold_in(_rk, 1), (2, 128, 256), jnp.float32)
        _lenS = 128 - jax.random.randint(jax.random.fold_in(_rk, 7), (2,), 0, max(1, 128 // 4) + 1, jnp.int32)
        _lenS2 = 2048 - jax.random.randint(jax.random.fold_in(_rk, 8), (2,), 0, max(1, 2048 // 4) + 1, jnp.int32)
        _ctx_2048P = jax.random.normal(jax.random.fold_in(_rk, 11), (2, 16, 256), jnp.float32)
        _ctx_2048c = jax.random.dirichlet(jax.random.fold_in(_rk, 511), 0.3 * jnp.ones((16,), jnp.float32), (2, 2048))
        _ctx_2048t = jnp.einsum('bsk,bkd->bsd', _ctx_2048c, _ctx_2048P)
        _ctx_2048t = _ctx_2048t * jax.lax.rsqrt(jnp.mean(jnp.square(_ctx_2048t)) + 1e-12) * 0.953939
        ctx_2048 = -1.39393e-06 + 0.999914 * (_ctx_2048t + 0.3 * jax.random.normal(jax.random.fold_in(_rk, 611), (2, 2048, 256), jnp.float32))
        itok_BxS_0_1023 = jax.random.randint(jax.random.fold_in(_rk, 12), (2, 128), 0, 128, jnp.int32)
        return (x, ctx_2048, itok_BxS_0_1023)
    x, ctx_2048, itok_BxS_0_1023 = _rec_inputs()

    def _L0_xattn_setup():
        import jax, jax.numpy as jnp
        import numpy as np
        B, Lq, Lk = (2, 512, 128)
        Q_DIM, KV_DIM = (256, 256)
        H, HD = (16, 128)
        KVC, QC, R = (64, 96, 64)
        LOOKBACK = 8
        NEG = -1e+30

        def _rope(x, L):
            half = x.shape[-1] // 2
            inv_freq = 1.0 / 10000.0 ** (jnp.arange(half, dtype=jnp.float32) / half)
            ang = jnp.arange(L, dtype=jnp.float32)[:, None] * inv_freq
            cos, sin = (jnp.cos(ang), jnp.sin(ang))
            x1, x2 = (x[..., :half], x[..., half:])
            return jnp.concatenate([x1 * cos - x2 * sin, x1 * sin + x2 * cos], axis=-1)
        key = jax.random.key(seed)
        ks = jax.random.split(key, 11)

        def w(k, shape, fan_in):
            return jax.random.normal(k, shape, jnp.float32) / np.sqrt(fan_in).astype(np.float32)
        return {'q': jax.random.normal(ks[0], (B, Lq, Q_DIM), jnp.float32), 'kv': jax.random.normal(ks[1], (B, Lk, KV_DIM), jnp.float32), 'seg_id': jnp.sort(jax.random.randint(ks[2], (B, Lq), 0, Lk), axis=-1), 'W_kvc': w(ks[3], (KV_DIM, KVC), KV_DIM), 'W_dq': w(ks[4], (Q_DIM, QC), Q_DIM), 'W_uq': w(ks[5], (QC, H * HD), QC), 'W_qr': w(ks[6], (QC, H * R), QC), 'W_uk': w(ks[7], (KVC, H * HD), KVC), 'W_kr': w(ks[8], (KVC, R), KVC), 'W_uv': w(ks[9], (KVC, H * HD), KVC), 'W_o': w(ks[10], (H * HD, Q_DIM), H * HD)}
    _L0_xattn_all = _L0_xattn_setup()
    _L0_xattn_in = {k: v for k, v in _L0_xattn_all.items() if k in ('W_kvc', 'W_dq', 'W_uq', 'W_qr', 'W_uk', 'W_kr', 'W_uv', 'W_o')}
    del _L0_xattn_all

    def _L0_attn_setup():
        import jax, jax.numpy as jnp
        from jax import lax
        import numpy as np
        D_MODEL, D_INNER, D_STATE, D_CONV, DT_RANK = (256, 512, 16, 4, 128)
        B, L = (2, 128)
        key = jax.random.key(seed)
        ks = jax.random.split(key, 10)
        s = 0.02
        x = jax.random.normal(ks[0], (B, L, D_MODEL), jnp.float32)
        W_in = jax.random.normal(ks[1], (2 * D_INNER, D_MODEL), jnp.float32) * s
        conv_w = jax.random.normal(ks[2], (D_INNER, D_CONV), jnp.float32) * s
        conv_b = jax.random.normal(ks[3], (D_INNER,), jnp.float32) * s
        W_x = jax.random.normal(ks[4], (DT_RANK + 2 * D_STATE, D_INNER), jnp.float32) * s
        W_dt = jax.random.normal(ks[5], (D_INNER, DT_RANK), jnp.float32) * s
        b_dt = jax.random.normal(ks[6], (D_INNER,), jnp.float32) * s
        A_log = jnp.log(jnp.broadcast_to(jnp.arange(1, D_STATE + 1, dtype=jnp.float32), (D_INNER, D_STATE)))
        Dp = jnp.ones((D_INNER,), jnp.float32)
        W_out = jax.random.normal(ks[7], (D_MODEL, D_INNER), jnp.float32) * s
        return {'x': x, 'W_in': W_in, 'conv_w': conv_w, 'conv_b': conv_b, 'W_x': W_x, 'W_dt': W_dt, 'b_dt': b_dt, 'A_log': A_log, 'Dp': Dp, 'W_out': W_out}
    _L0_attn_all = _L0_attn_setup()
    _L0_attn_in = {k: v for k, v in _L0_attn_all.items() if k in ('W_in', 'conv_w', 'conv_b', 'W_x', 'W_dt', 'b_dt', 'A_log', 'Dp', 'W_out')}
    del _L0_attn_all

    def _L0_ffn_setup():
        import jax, jax.numpy as jnp
        import numpy as np
        D_MODEL = 256
        D_FF = 1024
        BATCH = 4
        SEQ = 256
        MAX_EXP = 4
        NUM_BITS = 8
        C_CHUNKS = 2
        SCALE = 0.1

        def _pow2_ternary(key, out_dim, in_dim, max_exp):
            k1, k2 = jax.random.split(key)
            t = jax.random.randint(k1, (out_dim, in_dim), -1, 2).astype(jnp.float32)
            e = jax.random.randint(k2, (out_dim, in_dim), 0, max_exp + 1).astype(jnp.float32)
            return t * jnp.exp2(-e)

        def _lookup_act(h):
            total_bits = NUM_BITS * C_CHUNKS
            qmax = 2 ** (total_bits - 1) - 1
            qmin = -2 ** (total_bits - 1)
            q = jnp.clip(jnp.round(h / SCALE), qmin, qmax)
            return jax.nn.gelu(q * SCALE)
        key = jax.random.key(seed)
        kx, k1, k2 = jax.random.split(key, 3)
        x = jax.random.normal(kx, (BATCH, SEQ, D_MODEL), dtype=jnp.float32)
        W1 = _pow2_ternary(k1, D_FF, D_MODEL, MAX_EXP)
        W2 = _pow2_ternary(k2, D_MODEL, D_FF, MAX_EXP)
        return {'x': x, 'W1': W1, 'W2': W2}
    _L0_ffn_all = _L0_ffn_setup()
    _L0_ffn_in = {k: v for k, v in _L0_ffn_all.items() if k in ('W1', 'W2')}
    del _L0_ffn_all

    def _L1_xattn_setup():
        import jax, jax.numpy as jnp
        import numpy as np
        D_MODEL = 256
        NUM_HEADS = 16
        HEAD_DIM = D_MODEL // NUM_HEADS

        def _fq_sym(x, axis):
            s = jnp.max(jnp.abs(x), axis=axis, keepdims=True) / 127.0
            s = jnp.maximum(s, 1e-08)
            q = jnp.clip(jnp.round(x / s), -127.0, 127.0) * s
            return x + jax.lax.stop_gradient(q - x)

        def _fq_unsigned(x, axis):
            s = jnp.max(x, axis=axis, keepdims=True) / 255.0
            s = jnp.maximum(s, 1e-08)
            q = jnp.clip(jnp.round(x / s), 0.0, 255.0) * s
            return x + jax.lax.stop_gradient(q - x)
        key = jax.random.key(seed)
        ks = jax.random.split(key, 8)
        B, N, M, C = (2, 256, 64, D_MODEL)
        return {'x': jax.random.normal(ks[0], (B, N, C), jnp.float32), 'cond': jax.random.normal(ks[1], (B, M, C), jnp.float32), 'Wq': jax.random.normal(ks[2], (C, C), jnp.float32) * 0.02, 'bq': jnp.zeros((C,), jnp.float32), 'Wkv': jax.random.normal(ks[3], (C, 2 * C), jnp.float32) * 0.02, 'bkv': jnp.zeros((2 * C,), jnp.float32), 'Wp': jax.random.normal(ks[4], (C, C), jnp.float32) * 0.02, 'bp': jnp.zeros((C,), jnp.float32)}
    _L1_xattn_all = _L1_xattn_setup()
    _L1_xattn_in = {k: v for k, v in _L1_xattn_all.items() if k in ('Wq', 'bq', 'Wkv', 'bkv', 'Wp', 'bp')}
    del _L1_xattn_all

    def _L1_attn_setup():
        import jax, jax.numpy as jnp
        import numpy as np
        L, N, E, H = (256, 2, 256, 16)
        DH = E // H
        SCALE = DH ** (-0.5)
        key = jax.random.key(seed)
        k1, k2, k3 = jax.random.split(key, 3)
        x = jax.random.normal(k1, (L, N, E), dtype=jnp.float32)
        weight_qkv = jax.random.normal(k2, (3 * E, E), dtype=jnp.float32) * 0.02
        weight_out = jax.random.normal(k3, (E, E), dtype=jnp.float32) * 0.02
        return {'x': x, 'weight_qkv': weight_qkv, 'weight_out': weight_out}
    _L1_attn_all = _L1_attn_setup()
    _L1_attn_in = {k: v for k, v in _L1_attn_all.items() if k in ('weight_qkv', 'weight_out')}
    del _L1_attn_all

    def _L1_ffn_setup():
        import jax, jax.numpy as jnp
        import numpy as np
        HIDDEN = 256
        INTER = 1024
        MOE_INTER = 128
        N_ROUTED = 8
        NUM_LOCAL = 8
        TOP_K = 2
        B, S = (4, 256)

        def _mlp(x, gw, uw, dw):
            g = x @ gw.T
            u = x @ uw.T
            return g * jax.nn.sigmoid(g) * u @ dw.T
        key = jax.random.key(seed)
        ks = jax.random.split(key, 8)
        std = 0.02
        return {'hidden_states': jax.random.normal(ks[0], (B, S, HIDDEN), jnp.float32), 'router_weight': jax.random.normal(ks[1], (N_ROUTED, HIDDEN), jnp.float32) * std, 'sh_gate': jax.random.normal(ks[2], (INTER, HIDDEN), jnp.float32) * std, 'sh_up': jax.random.normal(ks[3], (INTER, HIDDEN), jnp.float32) * std, 'sh_down': jax.random.normal(ks[4], (HIDDEN, INTER), jnp.float32) * std, 'r_gate': jax.random.normal(ks[5], (MOE_INTER, HIDDEN), jnp.float32) * std, 'r_up': jax.random.normal(ks[6], (MOE_INTER, HIDDEN), jnp.float32) * std, 'r_down': jax.random.normal(ks[7], (HIDDEN, MOE_INTER), jnp.float32) * std}
    _L1_ffn_all = _L1_ffn_setup()
    _L1_ffn_in = {k: v for k, v in _L1_ffn_all.items() if k in ('router_weight', 'sh_gate', 'sh_up', 'sh_down', 'r_gate', 'r_up', 'r_down')}
    del _L1_ffn_all
    return {'x': x, 'ctx_2048': ctx_2048, 'itok_BxS_0_1023': itok_BxS_0_1023, 'L0_xattn_W_kvc': _L0_xattn_in['W_kvc'], 'L0_xattn_W_dq': _L0_xattn_in['W_dq'], 'L0_xattn_W_uq': _L0_xattn_in['W_uq'], 'L0_xattn_W_qr': _L0_xattn_in['W_qr'], 'L0_xattn_W_uk': _L0_xattn_in['W_uk'], 'L0_xattn_W_kr': _L0_xattn_in['W_kr'], 'L0_xattn_W_uv': _L0_xattn_in['W_uv'], 'L0_xattn_W_o': _L0_xattn_in['W_o'], 'L0_attn_W_in': _L0_attn_in['W_in'], 'L0_attn_conv_w': _L0_attn_in['conv_w'], 'L0_attn_conv_b': _L0_attn_in['conv_b'], 'L0_attn_W_x': _L0_attn_in['W_x'], 'L0_attn_W_dt': _L0_attn_in['W_dt'], 'L0_attn_b_dt': _L0_attn_in['b_dt'], 'L0_attn_A_log': _L0_attn_in['A_log'], 'L0_attn_Dp': _L0_attn_in['Dp'], 'L0_attn_W_out': _L0_attn_in['W_out'], 'L0_ffn_W1': _L0_ffn_in['W1'], 'L0_ffn_W2': _L0_ffn_in['W2'], 'L1_xattn_Wq': _L1_xattn_in['Wq'], 'L1_xattn_bq': _L1_xattn_in['bq'], 'L1_xattn_Wkv': _L1_xattn_in['Wkv'], 'L1_xattn_bkv': _L1_xattn_in['bkv'], 'L1_xattn_Wp': _L1_xattn_in['Wp'], 'L1_xattn_bp': _L1_xattn_in['bp'], 'L1_attn_weight_qkv': _L1_attn_in['weight_qkv'], 'L1_attn_weight_out': _L1_attn_in['weight_out'], 'L1_ffn_router_weight': _L1_ffn_in['router_weight'], 'L1_ffn_sh_gate': _L1_ffn_in['sh_gate'], 'L1_ffn_sh_up': _L1_ffn_in['sh_up'], 'L1_ffn_sh_down': _L1_ffn_in['sh_down'], 'L1_ffn_r_gate': _L1_ffn_in['r_gate'], 'L1_ffn_r_up': _L1_ffn_in['r_up'], 'L1_ffn_r_down': _L1_ffn_in['r_down']}

def reference(x, ctx_2048, itok_BxS_0_1023, L0_xattn_W_kvc, L0_xattn_W_dq, L0_xattn_W_uq, L0_xattn_W_qr, L0_xattn_W_uk, L0_xattn_W_kr, L0_xattn_W_uv, L0_xattn_W_o, L0_attn_W_in, L0_attn_conv_w, L0_attn_conv_b, L0_attn_W_x, L0_attn_W_dt, L0_attn_b_dt, L0_attn_A_log, L0_attn_Dp, L0_attn_W_out, L0_ffn_W1, L0_ffn_W2, L1_xattn_Wq, L1_xattn_bq, L1_xattn_Wkv, L1_xattn_bkv, L1_xattn_Wp, L1_xattn_bp, L1_attn_weight_qkv, L1_attn_weight_out, L1_ffn_router_weight, L1_ffn_sh_gate, L1_ffn_sh_up, L1_ffn_sh_down, L1_ffn_r_gate, L1_ffn_r_up, L1_ffn_r_down):
    import jax
    import jax.numpy as jnp

    def _L0_xattn_ref(q, kv, seg_id, W_kvc, W_dq, W_uq, W_qr, W_uk, W_kr, W_uv, W_o):
        import jax, jax.numpy as jnp
        import numpy as np
        B, Lq, Lk = (2, 512, 128)
        Q_DIM, KV_DIM = (256, 256)
        H, HD = (16, 128)
        KVC, QC, R = (64, 96, 64)
        LOOKBACK = 8
        NEG = -1e+30

        def _rope(x, L):
            half = x.shape[-1] // 2
            inv_freq = 1.0 / 10000.0 ** (jnp.arange(half, dtype=jnp.float32) / half)
            ang = jnp.arange(L, dtype=jnp.float32)[:, None] * inv_freq
            cos, sin = (jnp.cos(ang), jnp.sin(ang))
            x1, x2 = (x[..., :half], x[..., half:])
            return jnp.concatenate([x1 * cos - x2 * sin, x1 * sin + x2 * cos], axis=-1)
        b, lq, _ = q.shape
        lk = kv.shape[1]
        kv_c = kv @ W_kvc
        q_c = q @ W_dq
        q_nope = (q_c @ W_uq).reshape(b, lq, H, HD).transpose(0, 2, 1, 3)
        q_rope = (q_c @ W_qr).reshape(b, lq, H, R).transpose(0, 2, 1, 3)
        k_nope = (kv_c @ W_uk).reshape(b, lk, H, HD)
        v = (kv_c @ W_uv).reshape(b, lk, H, HD)
        k_rope = kv_c @ W_kr
        q_rope = _rope(q_rope, lq)
        k_rope = _rope(k_rope, lk)
        scale = 1.0 / np.sqrt(HD + R).astype(np.float32)
        scores = (jnp.einsum('bhqd,bkhd->bhqk', q_nope, k_nope) + jnp.einsum('bhqr,bkr->bhqk', q_rope, k_rope)) * scale
        k_ids = jnp.arange(lk)[None, None, :]
        qs = seg_id[:, :, None]
        good = (k_ids <= qs) & (k_ids >= qs - LOOKBACK)
        scores = jnp.where(good[:, None, :, :], scores, NEG)
        attn = jax.nn.softmax(scores, axis=-1)
        out = jnp.einsum('bhqk,bkhd->bqhd', attn, v).reshape(b, lq, H * HD)
        return out @ W_o

    def _L0_attn_ref(x, W_in, conv_w, conv_b, W_x, W_dt, b_dt, A_log, Dp, W_out):
        import jax, jax.numpy as jnp
        from jax import lax
        import numpy as np
        D_MODEL, D_INNER, D_STATE, D_CONV, DT_RANK = (256, 512, 16, 4, 128)
        B, L = (2, 128)
        b, l, _ = x.shape
        d_inner, d_state = A_log.shape
        dt_rank = W_dt.shape[1]
        d_conv = conv_w.shape[1]
        xz = jnp.einsum('bld,ed->ble', x, W_in)
        xp, z = jnp.split(xz, 2, axis=-1)
        xpad = jnp.pad(xp, ((0, 0), (d_conv - 1, 0), (0, 0)))
        xc = conv_b + sum((xpad[:, k:k + l, :] * conv_w[:, k] for k in range(d_conv)))
        xc = jax.nn.silu(xc)
        dbc = jnp.einsum('ble,fe->blf', xc, W_x)
        dt = dbc[..., :dt_rank]
        Bm = dbc[..., dt_rank:dt_rank + d_state]
        Cm = dbc[..., dt_rank + d_state:]
        delta = jax.nn.softplus(jnp.einsum('blr,er->ble', dt, W_dt) + b_dt)
        A = -jnp.exp(A_log)
        dA = jnp.exp(delta[..., None] * A)
        dBx = delta[..., None] * Bm[:, :, None, :] * xc[..., None]

        def step(h, inp):
            dA_t, dBx_t = inp
            h = dA_t * h + dBx_t
            return (h, h)
        h0 = jnp.zeros((b, d_inner, d_state), x.dtype)
        _, hs = lax.scan(step, h0, (jnp.swapaxes(dA, 0, 1), jnp.swapaxes(dBx, 0, 1)))
        hs = jnp.swapaxes(hs, 0, 1)
        y = jnp.einsum('bles,bls->ble', hs, Cm) + xc * Dp
        y = y * jax.nn.silu(z)
        return jnp.einsum('ble,de->bld', y, W_out)

    def _L0_ffn_ref(x, W1, W2):
        import jax, jax.numpy as jnp
        import numpy as np
        D_MODEL = 256
        D_FF = 1024
        BATCH = 4
        SEQ = 256
        MAX_EXP = 4
        NUM_BITS = 8
        C_CHUNKS = 2
        SCALE = 0.1

        def _pow2_ternary(key, out_dim, in_dim, max_exp):
            k1, k2 = jax.random.split(key)
            t = jax.random.randint(k1, (out_dim, in_dim), -1, 2).astype(jnp.float32)
            e = jax.random.randint(k2, (out_dim, in_dim), 0, max_exp + 1).astype(jnp.float32)
            return t * jnp.exp2(-e)

        def _lookup_act(h):
            total_bits = NUM_BITS * C_CHUNKS
            qmax = 2 ** (total_bits - 1) - 1
            qmin = -2 ** (total_bits - 1)
            q = jnp.clip(jnp.round(h / SCALE), qmin, qmax)
            return jax.nn.gelu(q * SCALE)
        h = jnp.einsum('bsd,fd->bsf', x, W1)
        a = _lookup_act(h)
        return jnp.einsum('bsf,df->bsd', a, W2)

    def _L1_xattn_ref(x, cond, Wq, bq, Wkv, bkv, Wp, bp):
        import jax, jax.numpy as jnp
        import numpy as np
        D_MODEL = 256
        NUM_HEADS = 16
        HEAD_DIM = D_MODEL // NUM_HEADS

        def _fq_sym(x, axis):
            s = jnp.max(jnp.abs(x), axis=axis, keepdims=True) / 127.0
            s = jnp.maximum(s, 1e-08)
            q = jnp.clip(jnp.round(x / s), -127.0, 127.0) * s
            return x + jax.lax.stop_gradient(q - x)

        def _fq_unsigned(x, axis):
            s = jnp.max(x, axis=axis, keepdims=True) / 255.0
            s = jnp.maximum(s, 1e-08)
            q = jnp.clip(jnp.round(x / s), 0.0, 255.0) * s
            return x + jax.lax.stop_gradient(q - x)
        B, N, C = x.shape
        H, hd = (NUM_HEADS, HEAD_DIM)
        q = (x @ Wq + bq).reshape(1, B * N, H, hd)
        kv = (cond @ Wkv + bkv).reshape(1, -1, 2, H, hd)
        k, v = (kv[:, :, 0], kv[:, :, 1])
        scale = 1.0 / np.sqrt(hd).astype(np.float32)
        q = jnp.transpose(q * scale, (0, 2, 1, 3))
        k = jnp.transpose(k, (0, 2, 1, 3))
        v = jnp.transpose(v, (0, 2, 1, 3))
        q = _fq_sym(q, axis=-1)
        k = _fq_sym(k, axis=-1)
        v = _fq_sym(v, axis=2)
        attn = jnp.einsum('bhqd,bhkd->bhqk', q, k)
        attn = jax.nn.softmax(attn.astype(jnp.float32), axis=-1)
        attn = _fq_unsigned(attn, axis=-1)
        out = jnp.einsum('bhqk,bhkd->bhqd', attn, v)
        out = jnp.transpose(out, (0, 2, 1, 3)).reshape(B, N, C)
        return out @ Wp + bp

    def _L1_attn_ref(x, weight_qkv, weight_out):
        import jax, jax.numpy as jnp
        import numpy as np
        L, N, E, H = (256, 2, 256, 16)
        DH = E // H
        SCALE = DH ** (-0.5)
        l, n, e = x.shape
        h, dh = (H, DH)
        qkv = jnp.einsum('lne,fe->lnf', x, weight_qkv)
        q, k, v = jnp.split(qkv, 3, axis=-1)
        q = q.reshape(l, n, h, dh) * jnp.asarray(SCALE, x.dtype)
        k = k.reshape(l, n, h, dh)
        v = v.reshape(l, n, h, dh)
        attn = jnp.einsum('lnhd,mnhd->nhlm', q, k)
        causal = jnp.tril(jnp.ones((l, l), dtype=bool))
        attn = jnp.where(causal, attn, jnp.asarray(-jnp.inf, attn.dtype))
        attn = jax.nn.softmax(attn, axis=-1)
        out = jnp.einsum('nhlm,mnhd->lnhd', attn, v).reshape(l, n, e)
        return jnp.einsum('lne,fe->lnf', out, weight_out)

    def _L1_ffn_ref(hidden_states, router_weight, sh_gate, sh_up, sh_down, r_gate, r_up, r_down):
        import jax, jax.numpy as jnp
        import numpy as np
        HIDDEN = 256
        INTER = 1024
        MOE_INTER = 128
        N_ROUTED = 8
        NUM_LOCAL = 8
        TOP_K = 2
        B, S = (4, 256)

        def _mlp(x, gw, uw, dw):
            g = x @ gw.T
            u = x @ uw.T
            return g * jax.nn.sigmoid(g) * u @ dw.T
        Bsz, Seq, H = hidden_states.shape
        x = hidden_states.reshape(-1, H)
        logits = x.astype(jnp.float32) @ router_weight.astype(jnp.float32).T
        topk_vals, topk_idx = jax.lax.top_k(logits, TOP_K)
        topk_w = jax.nn.softmax(topk_vals, axis=-1)
        slot_mask = (topk_idx < NUM_LOCAL).astype(topk_w.dtype)
        comb_w = jnp.sum(topk_w * slot_mask, axis=-1).astype(x.dtype)
        shared = _mlp(x, sh_gate, sh_up, sh_down)
        routed = _mlp(x, r_gate, r_up, r_down) * comb_w[:, None]
        return (shared + routed).reshape(Bsz, Seq, H)
    x = x + _L0_xattn_ref(_layernorm(x, axis=-1), ctx_2048, itok_BxS_0_1023, L0_xattn_W_kvc, L0_xattn_W_dq, L0_xattn_W_uq, L0_xattn_W_qr, L0_xattn_W_uk, L0_xattn_W_kr, L0_xattn_W_uv, L0_xattn_W_o)
    x = x + _L0_attn_ref(_layernorm(x, axis=-1), L0_attn_W_in, L0_attn_conv_w, L0_attn_conv_b, L0_attn_W_x, L0_attn_W_dt, L0_attn_b_dt, L0_attn_A_log, L0_attn_Dp, L0_attn_W_out)
    x = x + _L0_ffn_ref(_layernorm(x, axis=-1), L0_ffn_W1, L0_ffn_W2)
    x = x + _L1_xattn_ref(_layernorm(x, axis=-1), ctx_2048, L1_xattn_Wq, L1_xattn_bq, L1_xattn_Wkv, L1_xattn_bkv, L1_xattn_Wp, L1_xattn_bp)
    x = x + _L1_attn_ref(_layernorm(x, axis=-1), L1_attn_weight_qkv, L1_attn_weight_out)
    x = x + _L1_ffn_ref(_layernorm(x, axis=-1), L1_ffn_router_weight, L1_ffn_sh_gate, L1_ffn_sh_up, L1_ffn_sh_down, L1_ffn_r_gate, L1_ffn_r_up, L1_ffn_r_down)
    return x

_drawn_inputs = setup_inputs


def setup_inputs(seed=0):
    import zlib

    import numpy as np

    out = dict(_drawn_inputs(seed))
    spreads = {'L0_attn_Dp': (1.0, 0.6),
     'L1_xattn_bq': (0.0, 0.8),
     'L1_xattn_bkv': (0.0, 2.0),
     'L1_xattn_bp': (0.0, 2.0)}
    factors = {'L0_attn_W_in': 8.0,
     'L0_attn_conv_w': 8.0,
     'L0_attn_conv_b': 8.0,
     'L0_attn_W_x': 8.0,
     'L0_attn_b_dt': 8.0,
     'L0_attn_A_log': 8.0,
     'L0_attn_W_out': 8.0,
     'L1_xattn_Wq': 8.0,
     'L1_xattn_Wkv': 8.0,
     'L1_xattn_Wp': 8.0,
     'L1_attn_weight_qkv': 8.0,
     'L1_attn_weight_out': 8.0,
     'L1_ffn_sh_gate': 8.0,
     'L1_ffn_sh_up': 8.0,
     'L1_ffn_sh_down': 8.0,
     'L1_ffn_r_gate': 8.0,
     'L1_ffn_r_up': 8.0,
     'L1_ffn_r_down': 8.0,
     'L1_ffn_router_weight': 8.0}
    for name, (base, spread) in spreads.items():
        noise = np.random.default_rng([zlib.crc32(name.encode()), seed]).standard_normal(out[name].shape)
        drawn = base * np.exp(spread * noise) if base else spread * noise
        out[name] = jnp.asarray(drawn.astype(out[name].dtype))
    for name, factor in factors.items():
        out[name] = (out[name] * factor).astype(out[name].dtype)
    return out
```

```python
from contextlib import ExitStack

import concourse.bass as bass
from concourse import mybir

ALU = mybir.AluOpType
ACT = mybir.ActivationFunctionType
AX = mybir.AxisListType
F32 = mybir.dt.float32
BF16 = mybir.dt.bfloat16
F16 = mybir.dt.float16
U8 = mybir.dt.uint8
I32 = mybir.dt.int32

P = 128
B, L, D = 2, 128, 256
T = B * L
CH = D // P
NKEY = 2048
KEYS = B * NKEY
EPS = 1e-5
NEG = -1e30
MAGIC = 12582912.0

H = 16
HD, KVC, QC, R = 128, 64, 96, 64
LOOKBACK = 8
WIN = LOOKBACK + 1
GQ = P // H
NG = T // GQ
GB = NG // B
GK = GQ * WIN
GK1 = GK + 1
MLA_SCALE = float((HD + R) ** -0.5)
DI, DS, DC, DR = 512, 16, 4, 128
ET = DI // P
LP = L + DC - 1
FF = 1024
FT = FF // P
HW = D // H
PAIRS = H // 2
PR = 2 * 3 * HW
CK = 512
CT = CK // P
NC = KEYS // CK
KT = KEYS // P
QMAX = 127.0
LN255 = 5.541263545158426
E = 8
CST = 530
W0A = CH * QC + H * QC + H * KVC + H * 2 * R + H * R + CH * 2 * R + D + R
W0B = H * KVC + H * D
W1 = CH * 2 * DI + ET * (DR + 2 * DS) + DI + ET * D + ET * (DC + 3 + DS) + CH * 2 * D + D + CH
W2 = CH * FF + FT * D
W3 = 2 * (CH * D + D) + CH * 3 * D + CH * D + 2 * CH * (FF + P) + (FT + 1) * D + CH * E
ARENA = 40400


class Chain:

    def __init__(self, engine, semaphore):
        self.engine, self.semaphore, self.n, self.off = engine, semaphore, 0, 0

    def __call__(self, ins):
        self.n += 1
        ins.then_inc(self.semaphore, 1)
        self.engine.wait_ge(self.semaphore, self.off + self.n)


def perceiver_kernel(nc, x_d, seg_d, segrep_d, ctx_d, rope_d, cst_d, w0a_d, w0b_d, w1_d, w2_d, w3_d, out_d):
    with ExitStack() as ctx:
        def sb(name, shape, dt=F32):
            return ctx.enter_context(nc.sbuf_tensor(name, shape, dt))

        def sem(name):
            return ctx.enter_context(nc.semaphore(name))

        def dram(name, shape, dt):
            return nc.dram_tensor(name, shape, dt).ap()

        ps = ctx.enter_context(nc.psum_tensor("ps", [P, 8, 512], F32))

        cst = sb("cst", [P, CST])
        ident, qcos, qsin = cst[:, 0:128], cst[:, 128:256], cst[:, 256:384]
        ones, negdiag, jidx = cst[:, 384:512], cst[:, 512:520], cst[:, 520:529]
        identb = sb("identb", [P, P], BF16)
        xres = sb("xres", [P, B, D])
        xn = sb("xn", [P, B, D])
        xnT = sb("xnT", [P, CH, T])
        ln_st = sb("ln_st", [P, B, 6])
        ln_mv = sb("ln_mv", [P, B, 2])
        ln_ve = sb("ln_ve", [P, B])
        ln_rs = sb("ln_rs", [P, B])
        neghalf = sb("neghalf", [P, B])
        w1 = sb("w1", [P, W1])
        vrow = sb("vrow", [P, PAIRS, KT * 2 * HW], F16)

        arena = sb("arena", [P, ARENA])
        at = [0]

        def phase(start=0):
            at[0] = start

        def take(shape, dt=F32, rows=P):
            n = 1
            for s in shape:
                n *= s
            words = n if dt in (F32, I32) else (n + 1) // 2 if dt in (BF16, F16) else n // 4
            a = arena[0:rows, at[0]:at[0] + words]
            at[0] += words
            assert at[0] <= ARENA, (at[0], ARENA)
            if dt != F32:
                a = a.bitcast(dt)
            if len(shape) > 1:
                names = "abcd"[:len(shape)]
                a = a.rearrange(f"p ({' '.join(names)}) -> p {' '.join(names)}",
                                **{k: s for k, s in zip(names[1:], shape[1:])})
            return a

        phase()
        w0a = take([W0A])
        at[0] = 0
        w_dq = take([CH, QC])
        w_uqT = take([H, QC])
        w_ukT = take([H, KVC])
        w_qall = take([H, 2 * R])
        w_qrs = take([H, R])
        w_kcat = take([CH, 2 * R])
        w_kvcT = take([D])
        w_kr = take([R])
        assert at[0] == W0A
        w0b = take([W0B])
        at[0] -= W0B
        w_uvT = take([H, KVC])
        w_o = take([H, D])
        w_vo = take([PAIRS, D])
        g_at = at[0]
        grow = take([B, WIN * D])
        r_at = at[0]
        rrow = take([B, WIN * 2 * R])
        gT_at = at[0]
        gT = take([CH, WIN, P])
        krow = take([B, WIN, 2 * KVC])
        kcat = take([B, WIN, P])
        qT = take([NG, H, GQ])
        q_cT = take([T])
        rq = take([2, 2, 2, T])
        rk = take([2, 2, 3, R])
        seg_i = take([B], I32)
        segg_i = take([NG], I32)
        segf = take([B])
        base = take([B])
        idx = take([2 * B], I32)
        segh = take([NG])
        low = take([NG])
        baseg = take([NG])
        kid = take([NG, WIN])
        ge = take([NG, WIN])
        anyg = take([NG])
        mask = take([NG, GK1])
        sc = take([NG, GK1])
        mx = take([NG])
        mT = take([B * CH])
        phase(g_at)
        pT = take([NG, P])
        phase(r_at)
        oT = take([PAIRS, T])
        phase(gT_at)
        kvg = take([NG, KVC])
        phase(CH * QC)
        cs = take([2, CT, D])
        msum = take([B, D], rows=1)
        phase(CH * QC)
        kvm = take([NG, KVC], rows=1)

        taken = [0]

        def part(n):
            taken[0] += n
            return w1[:, taken[0] - n:taken[0]]

        w_in = part(CH * 2 * DI).rearrange("p (c n) -> p c n", c=CH)
        w_x = part(ET * (DR + 2 * DS)).rearrange("p (c n) -> p c n", c=ET)
        w_dt = part(DI)
        w_out = part(ET * D).rearrange("p (c n) -> p c n", c=ET)
        conv_w = part(ET * DC).rearrange("p (t k) -> p t k", t=ET)
        conv_b, b_dt, dskip = part(ET), part(ET), part(ET)
        a_log = part(ET * DS).rearrange("p (t s) -> p t s", t=ET)
        w_kv = part(CH * 2 * D).rearrange("p (c n) -> p c n", c=CH)
        b_k, b_v = part(D), part(CH)
        assert taken[0] == W1
        phase()
        xpad = take([ET, B, LP])
        zT = take([ET * T])
        acc = take([ET, T])
        th = take([ET * T])
        xc = take([ET * T])
        dtT = take([T])
        bcT = take([T], rows=2 * DS)
        delta = take([ET, T])
        u = take([ET, T])
        aneg = take([ET, DS])
        dA = take([2, ET, T])
        dbx = take([2, ET, T])
        hst = take([2, ET * T])
        hc = take([2, ET, T])
        bc = take([2, 2, T])
        w2_at = at[0]
        w2 = take([W2])
        cx = take([CT, D])
        cT = take([CH, CK])
        kmx = take([CT * H])
        ksc = take([CT * H])
        krs = take([CT * H])
        vq_at = at[0]
        kb = take([CT, D])
        tq = take([CT * H, HW])
        kq = take([CT * H, HW])
        r1 = take([CT * H, HW])
        k3 = take([CT, H, 3, HW], BF16)
        ktc = take([PAIRS, CK], BF16, rows=PR)
        vT = take([CH, KEYS])
        vmx = take([CH])
        vsc = sb("vsc", [P, CH])
        vrs = take([CH])
        phase(vq_at)
        vqb = take([CH, KEYS], BF16)

        w_f1 = w2[:, 0:CH * FF].rearrange("p (c n) -> p c n", c=CH)
        w_f2 = w2[:, CH * FF:CH * FF + FT * D].rearrange("p (c n) -> p c n", c=FT)
        phase()
        hq = take([FT, T])
        aT = take([FT, T])
        assert at[0] <= w2_at

        phase()
        kqs = take([2, KEYS + 2 * T], BF16, rows=PR)
        vss = take([2, KT * 2 * HW], F16)
        sqs = take([2, 8])
        s_sb = take([2, KEYS])
        p8 = take([2, KEYS * 2], U8)
        ptr = take([4, 1024], F16)
        oall = take([PAIRS, 4, HW])
        zall = take([PAIRS, 4])
        mxs = take([2, 4])
        mx1 = take([2])
        nb = take([2])
        zs = take([2, 4])
        tail_at = at[0]
        qz = take([PAIRS, 2, T], BF16, rows=PR)
        sqa = take([PAIRS, 8])
        hmask = take([2], rows=PR)
        qb = take([B * H, HW])
        qmx = take([B * H])
        qsc = take([B * H])
        qrs = take([B * H])
        q3 = take([B * H, 3, HW], BF16)
        phase(tail_at)
        onrm = take([B, D])
        rz = take([PAIRS * 4])
        onT = take([CH, T])
        q1 = take([D])
        prod = take([2, D])
        s2 = take([2, H])
        m2 = take([H])
        e2 = take([2, H])
        z2 = take([H])
        orow = take([B, D])
        pv2 = take([2, D])
        oaT = take([CH, T])
        lg = take([B, E])
        top = take([B, E])
        te = take([B, 2])
        tz = take([B])
        comb = take([B])
        tg = take([2, T])
        ga = take([2, T])
        hT = take([FT + 1, T])
        w3_at = max(at[0], tail_at + 3100)
        phase(w3_at)
        w_q = take([CH, D])
        b_q = take([D])
        w_p = take([CH, D])
        b_p = take([D])
        w3a = at[0] - w3_at
        w_qkv = take([CH, 3 * D])
        w_ao = take([CH, D])
        w_sg = take([CH, FF + P])
        w_su = take([CH, FF + P])
        w_sd = take([FT + 1, D])
        w_rt = take([CH, E])
        assert at[0] == w3_at + W3, (at[0] - w3_at, W3)
        w3 = arena[:, w3_at:w3_at + W3]

        pe_step = sem("pe_step")
        (WABS, WVO, QLAT, MTR, MLAT, MLA_OUT, DBC, DLIN, Y_DONE, MIX_OUT, FF_OUT, Q_PS, Q_TR, ON_TR, X_OUT,
         QKV, OA_TR, SA_OUT, LOGITS) = range(1, 20)
        ld_seg = sem("ld_seg")
        ld_x = sem("ld_x")
        ld_cst = sem("ld_cst")
        ld_segg = sem("ld_segg")
        ld_w0a = sem("ld_w0a")
        ld_w0b = sem("ld_w0b")
        csum = sem("csum")
        ld_cs = [sem(f"ld_cs{k}") for k in range(2)]
        ld_w1 = sem("ld_w1")
        kc_sb = sem("kc_sb")
        st_kv = sem("st_kv")
        ld_kvg = sem("ld_kvg")
        kvm_ready = sem("kvm_ready")
        dt_sb = sem("dt_sb")
        st_bc = sem("st_bc")
        mla_done = sem("mla_done")
        ld_w2 = sem("ld_w2")
        cx_tr = sem("cx_tr")
        ld_cx = sem("ld_cx")
        hc_made = sem("hc_made")
        ld_bc = [sem(f"ld_bc{k}") for k in range(2)]
        vr_sb = sem("vr_sb")
        kt_stored = sem("kt_stored")
        ld_w3a = sem("ld_w3a")
        ld_w3b = sem("ld_w3b")
        qz_ready = sem("qz_ready")
        sqa_ready = sem("sqa_ready")
        ld_kqs = [sem(f"ld_kqs{k}") for k in range(2)]
        ld_sqs = [sem(f"ld_sqs{k}") for k in range(2)]
        ld_vss = [sem(f"ld_vss{k}") for k in range(2)]
        s_ps = sem("s_ps")
        ptr_used = sem("ptr_used")
        y_ready = sem("y_ready")
        st_out = sem("st_out")
        half = sem("half")
        ln_var = sem("ln_var")
        ln_rstd = sem("ln_rstd")
        idx_ready = sem("idx_ready")
        got_rows = [sem(f"got_rows{k}") for k in range(2)]
        got_rope = [sem(f"got_rope{k}") for k in range(2)]
        u_ready = sem("u_ready")
        h_ready = sem("h_ready")
        dbx_ready = sem("dbx_ready")
        kq_ready = sem("kq_ready")
        krs_ready = sem("krs_ready")
        tq_ready = sem("tq_ready")
        k_int = sem("k_int")
        hmask_set = sem("hmask_set")
        hmask_ready = sem("hmask_ready")
        p8_set = sem("p8_set")
        ln_tr = sem("ln_tr")
        ln_cols = sem("ln_cols")
        identb_ready = sem("identb_ready")
        wabs_sb = sem("wabs_sb")
        wvo_sb = sem("wvo_sb")
        qlat_sb = sem("qlat_sb")
        qpair = sem("qpair")
        qa_sb = sem("qa_sb")
        kpr = sem("kpr")
        gt_tr = sem("gt_tr")
        gt_sb = sem("gt_sb")
        kt_tr = sem("kt_tr")
        kt_sb = sem("kt_sb")
        mtr_sb = sem("mtr_sb")
        sc_ready = sem("sc_ready")
        sc_exp = sem("sc_exp")
        pt_tr = sem("pt_tr")
        pt_sb = sem("pt_sb")
        xz = sem("xz")
        xz_sb = sem("xz_sb")
        aneg_ready = sem("aneg_ready")
        conv = sem("conv")
        xc_tanh = sem("xc_tanh")
        dlin_ps = sem("dlin_ps")
        sp_ln = sem("sp_ln")
        delta_ready = sem("delta_ready")
        dA_ready = sem("dA_ready")
        v_sb = sem("v_sb")
        ktc_sb = [sem(f"ktc_sb{k}") for k in range(2)]
        v_ps = sem("v_ps")
        cT_sb = sem("cT_sb")
        ktc_tr = sem("ktc_tr")
        k_hi = sem("k_hi")
        r1_ready = sem("r1_ready")
        vsc_ready = sem("vsc_ready")
        v_round = sem("v_round")
        z_tanh = sem("z_tanh")
        vr_tr = sem("vr_tr")
        ff_q = sem("ff_q")
        ff_a = sem("ff_a")
        nb_ready = sem("nb_ready")
        t_ps = sem("t_ps")
        o_read = sem("o_read")
        p_ready = sem("p_ready")
        ptr_sb = [sem(f"ptr_sb{k}") for k in range(2)]
        on_cols = sem("on_cols")
        q1_sb = sem("q1_sb")
        oa_rows = sem("oa_rows")
        e2_arg = sem("e2_arg")
        e2_ready = sem("e2_ready")
        oa_cols = sem("oa_cols")
        te_arg = sem("te_arg")
        te_ready = sem("te_ready")
        moe_gu = sem("moe_gu")
        moe_h = sem("moe_h")
        moe_t = sem("moe_t")
        dve_chain = sem("dve_chain")
        ln_rows = sem("ln_rows")
        qr_sb = sem("qr_sb")
        kr_sb = sem("kr_sb")
        kr_ps = sem("kr_ps")
        scored = sem("scored")
        sc_ps = sem("sc_ps")
        msum_sb = sem("msum_sb")
        probs = sem("probs")
        pv0 = sem("pv0")
        ot_sb = sem("ot_sb")
        xc_ready = sem("xc_ready")
        skip = sem("skip")
        kb_sb = sem("kb_sb")
        hc_used = sem("hc_used")
        k_ps = sem("k_ps")
        k3_ready = sem("k3_ready")
        gated = sem("gated")
        vq_ready = sem("vq_ready")
        mix_add = sem("mix_add")
        ff_h = sem("ff_h")
        q3_ready = sem("q3_ready")
        s_read = sem("s_read")
        mx_ready = sem("mx_ready")
        on_rows = sem("on_rows")
        qkv_used = sem("qkv_used")
        moe_out = sem("moe_out")
        act_chain = sem("act_chain")

        kt_scr = dram("kt_scr", (PR, PAIRS, KEYS), BF16)
        kv_scr = dram("kv_scr", (T, WIN, KVC), F32)
        bc_scr = dram("bc_scr", (DS, 2, T), F32)

        def bank(k, at_, n, row=0, rows=P):
            return ps[row:row + rows, k, at_:at_ + n]

        block = ctx.enter_context(nc.Block())

        @block.sync
        def _(sp):
            sp.dma_start(seg_i[:, :], seg_d).then_inc(ld_seg, 16)
            sp.dma_start(xres[:, :, :], x_d).then_inc(ld_x, 16)
            sp.dma_start(cst[:, :], cst_d).then_inc(ld_cst, 16)
            sp.dma_start(segg_i[:, :], segrep_d).then_inc(ld_segg, 16)
            sp.dma_start(w0a[:, :], w0a_d).then_inc(ld_w0a, 16)
            sp.dma_start(w0b[:, :], w0b_d).then_inc(ld_w0b, 16)
            sp.wait_ge(pe_step, WABS)
            for c in range(NC):
                if c >= 2:
                    sp.wait_ge(csum, c - 1)
                sp.dma_start(cs[:, c % 2], ctx_d[c * CK:(c + 1) * CK, :].rearrange("(p t) d -> p t d", t=CT))\
                  .then_inc(ld_cs[c % 2], 16)
                if c == 1:
                    sp.dma_start(w1[:, :], w1_d).then_inc(ld_w1, 16)
            for b in range(B):
                sp.wait_ge(kc_sb, 3 * b + 3)
                sp.dma_start(kv_scr[b * L:(b + 1) * L, :, :], krow[:, b, :, 0:KVC]).then_inc(st_kv, 16)
            sp.wait_ge(st_kv, 32)
            for j in range(WIN):
                sp.dma_start(kvg[j * GQ:(j + 1) * GQ, :, :], kv_scr[:, j, :].rearrange("(g i) k -> i g k", i=GQ))\
                  .then_inc(ld_kvg, 16)
            sp.wait_ge(kvm_ready, 1)
            sp.dma_start(kvg[GK:GK1, :, :], kvm[:, :, :]).then_inc(ld_kvg, 16)

            sp.wait_ge(dt_sb, 2)
            sp.dma_start(bc_scr.rearrange("s a t -> a s t"), bcT[0:2 * DS, :]).then_inc(st_bc, 16)
            sp.wait_ge(st_bc, 16)
            sp.wait_ge(mla_done, 1)
            sp.dma_start(w2[:, :], w2_d).then_inc(ld_w2, 16)
            with sp.Fori(0, NC) as i:
                key0, states = sp.snap(i * CK), [sp.snap(2 * i + s) for s in range(2)]
                sp.wait_ge(cx_tr, i + 1)
                sp.dma_start(cx[:, :, :], ctx_d[bass.ds(key0, CK), :].rearrange("(p t) d -> p t d", t=CT)).then_inc(ld_cx, 16)
                for s in range(2):
                    sp.wait_ge(hc_made, 2 * i + s + 1)
                    sp.dma_start(bc[:, s], bc_scr[bass.ds(states[s], 1), :, :].partition_broadcast(P)
                                 .rearrange("p o a t -> p (o a) t")).then_inc(ld_bc[s], 16)
            sp.wait_ge(vr_sb, 8)
            sp.wait_ge(kt_stored, 16 * NC + 16)
            sp.dma_start(w3[:, 0:w3a], w3_d[:, 0:w3a]).then_inc(ld_w3a, 16)
            sp.dma_start(w3[:, w3a:W3], w3_d[:, w3a:W3]).then_inc(ld_w3b, 16)

            sp.wait_ge(qz_ready, 2)
            sp.wait_ge(sqa_ready, 1)

            def pair(it, kk, n):
                sp.dma_start(kqs[:, kk, 0:KEYS], kt_scr[:, bass.ds(n, 1), :].rearrange("r o k -> r (o k)")).then_inc(ld_kqs[kk], 16)
                sp.dma_start(kqs[:, kk, KEYS:KEYS + 2 * T], qz[:, bass.ds(n, 1), :, :].rearrange("r o h t -> r (o h t)"))\
                  .then_inc(ld_kqs[kk], 16)

            def pair_values(it, kk, n):
                sp.dma_start(sqs[:, kk, :], sqa[:, bass.ds(n, 1), :].rearrange("q o n -> q (o n)")).then_inc(ld_sqs[kk], 16)
                sp.dma_start(vss[:, kk, :], vrow[:, bass.ds(n, 1), :].rearrange("k o n -> k (o n)")).then_inc(ld_vss[kk], 16)

            for kk in range(2):
                pair(0, kk, kk)
                pair_values(0, kk, kk)
            with sp.Fori(0, 3) as it:
                nxt = [sp.snap(2 * it + 2 + kk) for kk in range(2)]
                for kk in range(2):
                    sp.wait_ge(s_ps, 4 * (8 * it + 4 * kk + 4))
                    pair(it, kk, nxt[kk])
                    sp.wait_ge(ptr_used, 4 * (8 * it + 4 * kk + 4) + 4)
                    pair_values(it, kk, nxt[kk])
            sp.wait_ge(y_ready, 2)
            sp.dma_start(out_d, xres[:, :, :]).then_inc(st_out, 16)
            sp.wait_ge(st_out, 16)

        @block.gpsimd
        def _(pool):
            pool.memset(neghalf[:, :], -0.5).then_inc(half, 1)
            pool.wait_ge(half, 1)

            def root(k):
                pool.wait_ge(ln_var, k + 1)
                pool.tensor_tensor(ln_rs[:, :], ln_ve[:, :], neghalf[:, :], ALU.pow).then_inc(ln_rstd, 1)

            root(0)
            pool.wait_ge(idx_ready, 1)
            for b in range(B):
                pool.indirect_dma_start(grow[:, b, :], None, ctx_d, bass.IndirectOffsetOnAxis(ap=idx[:, b:b + 1], axis=0))\
                    .then_inc(got_rows[b], 16)
            for b in range(B):
                pool.indirect_dma_start(rrow[:, b, :], None, rope_d, bass.IndirectOffsetOnAxis(ap=idx[:, B + b:B + b + 1], axis=0))\
                    .then_inc(got_rope[b], 16)
            root(1)

            pool.wait_ge(u_ready, 1)

            def input_of(i, s):
                pool.wait_ge(ld_bc[s], 16 * i + 16)
                pool.wait_ge(h_ready, 2 * i + s + 1)
                pool.tensor_tensor(dbx[:, s], u[:, :, :], bc[:, s, 0, :].unsqueeze(1).broadcast_to([P, ET, T]), ALU.mult)\
                    .then_inc(dbx_ready, 1)

            pool.nop().then_inc(kq_ready, 1)
            with pool.Fori(0, NC) as i:
                input_of(i, 0)
                wide = [P, CT * H, HW]
                pool.wait_ge(krs_ready, i + 1)
                pool.tensor_tensor(tq[:, :, :], kb.rearrange("p t (h d) -> p (t h) d", h=H),
                                   krs.unsqueeze(2).broadcast_to(wide), ALU.mult).then_inc(tq_ready, 1)
                input_of(i, 1)
                pool.wait_ge(k_int, i + 1)
                pool.tensor_tensor(kq[:, :, :], tq[:, :, :], ksc.unsqueeze(2).broadcast_to(wide), ALU.mult).then_inc(kq_ready, 1)
            root(2)
            root(3)
            pool.wait_ge(pe_step, FF_OUT)
            pool.memset(hmask[0:PR, :], 1.0).then_inc(hmask_set, 1)
            pool.wait_ge(hmask_set, 1)
            pool.affine_select(out=hmask[0:PR, 0:1], in_=hmask[0:PR, 0:1], compare_op=ALU.is_ge, fill=0.0, base=PR // 2 - 1,
                               pattern=[[0, 1]], channel_multiplier=-1).then_inc(hmask_set, 1)
            pool.affine_select(out=hmask[0:PR, 1:2], in_=hmask[0:PR, 1:2], compare_op=ALU.is_ge, fill=0.0, base=-(PR // 2),
                               pattern=[[0, 1]], channel_multiplier=1).then_inc(hmask_set, 1)
            pool.wait_ge(hmask_set, 3)
            pool.nop().then_inc(hmask_ready, 1)
            pool.memset(p8.rearrange("p a n -> p (a n)").bitcast(F16), 1024.0).then_inc(p8_set, 1)
            root(4)
            root(5)

        @block.scalar
        def _(act):
            link = Chain(act, act_chain)

            def columns(k):
                act.wait_ge(ln_tr, k + 1)
                act.activation(xnT.rearrange("p c t -> p (c t)"), bank(7, 0, 512), ACT.Copy).then_inc(ln_cols, 1)

            act.wait_ge(ld_cst, 16)
            act.activation(identb[:, :], ident, ACT.Copy).then_inc(identb_ready, 1)
            act.wait_ge(pe_step, WABS)
            for n in range(2):
                act.activation(w_qall[0:QC, 8 * n:8 * n + 8, 0:KVC],
                               bank(n, 0, 512, 0, QC).rearrange("p (h k) -> p h k", h=8), ACT.Copy).then_inc(wabs_sb, 1)
            act.activation(w_kcat[:, :, KVC:2 * KVC], bank(2, 0, CH * R).rearrange("p (c r) -> p c r", c=CH), ACT.Copy)\
               .then_inc(wabs_sb, 1)
            columns(0)
            act.wait_ge(pe_step, WVO)
            for n in range(4):
                act.activation(w_vo[:, 2 * n:2 * n + 2, :], bank(3 + n, 0, 512).rearrange("p (a n) -> p a n", a=2), ACT.Copy)\
                   .then_inc(wvo_sb, 1)
            act.wait_ge(pe_step, QLAT)
            act.activation(q_cT[0:QC, :], bank(7, 0, T, 0, QC), ACT.Copy).then_inc(qlat_sb, 1)
            for p in range(PAIRS):
                act.wait_ge(qpair, p + 1)
                act.activation(qT[0:KVC, :, 2 * p:2 * p + 2, :],
                               bank(p % 2, 0, 512, 0, KVC).rearrange("p (o g i) -> p g o i", o=2, i=GQ),
                               ACT.Copy).then_inc(qa_sb, 1)
            fill = 0
            for b in range(B):
                if b == 1:
                    act.wait_ge(kpr, 3)
                flat = gT.rearrange("p c j q -> p j c q")
                for f in range(5):
                    act.wait_ge(gt_tr, fill + 1)
                    nj = 2 if f < 4 else 1
                    act.activation(flat[:, 2 * f:2 * f + nj], bank(4 + fill % 2, 0, nj * 2 * P)
                                   .rearrange("p (j c q) -> p j c q", j=nj, c=CH), ACT.Copy).then_inc(gt_sb, 1)
                    fill += 1
                for f in range(3):
                    n = 3 * b + f
                    act.wait_ge(kpr, n + 1)
                    act.activation(krow[:, b, 3 * f:3 * f + 3, 0:KVC],
                                   bank(6 + n % 2, 0, 3 * P).rearrange("p (j k) -> p j k", j=3)[:, :, 0:KVC], ACT.Copy)\
                       .then_inc(kc_sb, 1)
            for n in range(6):
                act.wait_ge(kt_tr, n + 1)
                act.activation(kcat[:, n // 3, 3 * (n % 3):3 * (n % 3) + 3, :],
                               bank(4 + n % 2, 0, 3 * P).rearrange("p (j k) -> p j k", j=3), ACT.Copy).then_inc(kt_sb, 1)
            act.wait_ge(pe_step, MTR)
            act.activation(mT[:, :], bank(6, 8, B * CH), ACT.Copy, scale=1.0 / NKEY).then_inc(mtr_sb, 1)
            act.wait_ge(pe_step, MLAT)
            act.activation(kvm.rearrange("p (b g) k -> p b g k", b=B),
                           bank(6, 64, B * KVC, 0, 1).rearrange("p (b k) -> p b k", b=B).unsqueeze(2)
                           .broadcast_to([1, B, GB, KVC]), ACT.Copy).then_inc(kvm_ready, 1)
            for b in range(B):
                act.wait_ge(sc_ready, b + 1)
                act.activation(sc[:, b * GB:(b + 1) * GB, :], sc[:, b * GB:(b + 1) * GB, :], ACT.Exp, scale=MLA_SCALE)\
                   .then_inc(sc_exp, 1)
            for n in range(8):
                act.wait_ge(pt_tr, n + 1)
                act.activation(pT[0:GK1, 4 * n:4 * n + 4, :], bank(2 + n % 2, 0, 512, 0, GK1)
                               .rearrange("p (g r) -> p g r", g=4), ACT.Copy).then_inc(pt_sb, 1)

            columns(1)
            for m in range(4):
                act.wait_ge(xz, m + 1)
                if m < 2:
                    act.activation(xpad[:, 2 * m:2 * m + 2, :, DC - 1:LP], bank(m, 0, 512)
                                   .rearrange("p (t b l) -> p t b l", t=2, b=B), ACT.Copy).then_inc(xz_sb, 1)
                else:
                    act.activation(zT[:, (m - 2) * 512:(m - 1) * 512], bank(m, 0, 512), ACT.Copy).then_inc(xz_sb, 1)
            act.wait_ge(ld_w1, 16)
            link(act.activation(aneg[:, :, :], a_log, ACT.Exp))
            act.activation(aneg[:, :, :], aneg[:, :, :], ACT.Copy, scale=-1.0).then_inc(aneg_ready, 1)
            act.wait_ge(conv, 1)
            act.activation(th[:, :], acc.rearrange("p t n -> p (t n)"), ACT.Tanh, scale=0.5).then_inc(xc_tanh, 1)
            act.wait_ge(pe_step, DBC)
            act.activation(dtT[:, :], bank(4, 0, T), ACT.Copy).then_inc(dt_sb, 1)
            act.activation(bcT[0:2 * DS, :], bank(4, T, T, 0, 2 * DS), ACT.Copy).then_inc(dt_sb, 1)
            act.wait_ge(dlin_ps, 1)
            link(act.activation(th[:, :], acc.rearrange("p t n -> p (t n)"), ACT.Abs))
            link(act.activation(th[:, :], th[:, :], ACT.Exp, scale=-1.0))
            act.activation(th[:, :], th[:, :], ACT.Ln, bias=1.0).then_inc(sp_ln, 1)
            act.wait_ge(aneg_ready, 1)
            act.wait_ge(delta_ready, 1)

            def decay(i, s):
                act.wait_ge(h_ready, 2 * i + s + 1)
                for t in range(ET):
                    ins = act.activation(dA[:, s, t, :].rearrange("p (b l) -> p b l", b=B)[:, :, 1:L],
                                         delta[:, t, :].rearrange("p (b l) -> p b l", b=B)[:, :, 1:L], ACT.Exp,
                                         scale=aneg[:, t, bass.ds(2 * i + s, 1)])
                ins.then_inc(dA_ready, 1)

            act.nop().then_inc(v_sb, 2)
            act.nop().then_inc(ktc_sb[0], 1)
            act.nop().then_inc(kt_stored, 16)
            with act.Fori(0, NC) as i:
                decay(i, 0)
                act.wait_ge(cx_tr, i + 2)
                act.wait_ge(v_ps, 2 * i + 2)
                for c in range(CH):
                    act.activation(cT[:, c, :], bank(c, 0, CK), ACT.Copy).then_inc(cT_sb, 1)
                decay(i, 1)
                for m in range(CH):
                    act.wait_ge(v_ps, 2 * i + m + 3)
                    act.activation(vT[:, m, bass.ds(CK * i, CK)], bank(m, 0, CK), ACT.Identity, bias=b_v[:, m:m + 1])\
                       .then_inc(v_sb, 1)
                act.wait_ge(kq_ready, i + 2)
                act.wait_ge(ktc_tr, 4 * i + 1)
                act.activation(k3.rearrange("k t h a d -> k (t h) a d")[:, :, 0, :], kq[:, :, :], ACT.Copy).then_inc(k_hi, 1)
                act.wait_ge(r1_ready, i + 1)
                act.activation(k3.rearrange("k t h a d -> k (t h) a d")[:, :, 1, :], r1[:, :, :], ACT.Copy).then_inc(k_hi, 1)
                for n in (0, 2):
                    act.wait_ge(ktc_tr, 4 * i + n + 2)
                    if n == 0:
                        act.wait_ge(kt_stored, 16 * i + 16)
                    act.activation(ktc[:, 2 * n:2 * n + 2, :].rearrange("p a k -> p (a k)"),
                                   bank(4 + n % 2, 0, 512, 0, PR).bitcast(BF16), ACT.Copy).then_inc(ktc_sb[0], 1)
                act.wait_ge(ktc_sb[0], 2 * i + 3)
                act.wait_ge(ktc_sb[1], 2 * i + 3)
                act.dma_start(kt_scr[:, :, bass.ds(i * CK, CK)], ktc[:, :, :]).then_inc(kt_stored, 16)
            act.wait_ge(vsc_ready, 1)
            for m in range(CH):
                act.activation(vT[:, m, :], vT[:, m, :], ACT.Identity, bias=cst[:, 529:530], scale=vrs[:, m:m + 1]).then_inc(v_round, 1)
            act.activation(th[:, :], zT[:, :], ACT.Tanh, scale=0.5).then_inc(z_tanh, 1)
            for n in range(8):
                m, q = n // 4, n % 4
                act.wait_ge(vr_tr, n + 1)
                act.activation(vrow.rearrange("k p (t n) -> k t p n", n=2 * HW)[:, 8 * q:8 * q + 8, 4 * m:4 * m + 4, :],
                               bank(n % 2, 0, 512).bitcast(BF16).rearrange("k (t p n) -> k t p n", t=8, p=4), ACT.Copy)\
                   .then_inc(vr_sb, 1)

            columns(2)
            for n in range(4):
                act.wait_ge(ff_q, n + 1)
                act.activation(aT[:, 2 * n:2 * n + 2, :], hq[:, 2 * n:2 * n + 2, :], ACT.Gelu_apprx_tanh, scale=0.1)\
                   .then_inc(ff_a, 1)

            columns(3)

            def probabilities(it, j):
                u, kk = 8 * it + j, j // 4
                act.wait_ge(nb_ready, u + 1)
                act.wait_ge(t_ps, 4 * u + 4)
                if j % 4 == 0:
                    act.wait_ge(ld_sqs[kk], 16 * it + 16)
                    act.wait_ge(o_read, 2 * it + j // 4 + 1)
                out8 = p8[:, j % 2].rearrange("q (n w a e) -> q n a w e", w=P, a=2, e=2)[:, :, :, :, 0]
                act.activation(out8, s_sb[:, j % 2].rearrange("q (n a w) -> q n a w", a=2, w=P), ACT.Exp,
                               bias=nb[:, j % 2:j % 2 + 1], scale=sqs[:, kk, j % 4:j % 4 + 1],
                               accum_out=zs[:, kk, j % 4:j % 4 + 1]).then_inc(p_ready, 1)

            def columns16(it, j):
                u = 8 * it + j
                for c in (2, 3):
                    act.wait_ge(t_ps, 4 * u + c + 9)
                    act.wait_ge(ptr_used, 4 * u + c + 1)
                    act.activation(ptr[:, c, :], bank(4 + c % 3, 0, 512).bitcast(F16), ACT.Copy, bias=-1024.0)\
                       .then_inc(ptr_sb[1], 1)

            act.nop().then_inc(ptr_sb[1], 2)
            act.nop().then_inc(p_ready, 2)
            act.wait_ge(p8_set, 1)
            probabilities(0, 0)
            with act.Fori(0, 3) as it:
                for j in range(8):
                    probabilities(it + (j + 1) // 8, (j + 1) % 8)
                    columns16(it, j)
            for j in range(8):
                if j < 7:
                    probabilities(3, j + 1)
                columns16(3, j)
            act.wait_ge(pe_step, ON_TR)
            for c in range(CH):
                act.activation(onT[:, c, :], bank(4, c * T, T), ACT.Copy, scale=vsc[:, c:c + 1]).then_inc(on_cols, 1)

            columns(4)
            act.wait_ge(pe_step, QKV)
            act.activation(q1[:, :], bank(2, 0, D), ACT.Copy, scale=HW ** -0.5).then_inc(q1_sb, 1)
            act.activation(orow[:, 0, :], bank(0, D, D), ACT.Copy).then_inc(oa_rows, 1)
            act.wait_ge(e2_arg, 1)
            act.activation(e2[:, :, :], s2[:, :, :], ACT.Exp).then_inc(e2_ready, 1)
            act.wait_ge(pe_step, OA_TR)
            act.activation(oaT.rearrange("p c t -> p (c t)"), bank(3, 0, 512), ACT.Copy).then_inc(oa_cols, 1)

            columns(5)
            act.wait_ge(te_arg, 1)
            act.activation(te[:, :, :], te[:, :, :], ACT.Exp).then_inc(te_ready, 1)
            for m in range(FT + 1):
                act.wait_ge(moe_gu, m + 1)
                if m >= 2:
                    act.wait_ge(moe_h, m - 1)
                act.activation(tg[:, m % 2, :], bank(m % 4, 0, T), ACT.Tanh, scale=0.5).then_inc(moe_t, 1)

        @block.vector
        def _(dve):
            link = Chain(dve, dve_chain)

            def normalise(k):
                for b in range(B):
                    dve.bn_stats(ln_st[:, b, :], xres[:, b, :]).then_inc(dve_chain, 1)
                    link.n += 1
                dve.wait_ge(dve_chain, link.n)
                for b in range(B):
                    dve.bn_aggr(ln_mv[:, b, :], ln_st[:, b, :]).then_inc(dve_chain, 1)
                    link.n += 1
                dve.wait_ge(dve_chain, link.n)
                dve.tensor_scalar(ln_ve[:, :], ln_mv[:, :, 1], EPS, None, ALU.add).then_inc(ln_var, 1)
                dve.wait_ge(ln_rstd, k + 1)
                for b in range(B):
                    dve.tensor_scalar(xn[:, b, :], xres[:, b, :], ln_mv[:, b, 0:1], ln_rs[:, b:b + 1], ALU.subtract, ALU.mult)\
                       .then_inc(ln_rows, 1)

            dve.wait_ge(ld_x, 16)
            normalise(0)
            dve.wait_ge(ld_seg, 16)
            link(dve.tensor_copy(segf[:, :], seg_i[:, :]))
            link(dve.tensor_scalar(base[:, :], segf[:, :], float(-LOOKBACK), float(NKEY - WIN), ALU.add, ALU.min))
            link(dve.tensor_scalar(base[:, :], base[:, :], 0.0, None, ALU.max))
            dve.tensor_copy(idx[:, B:2 * B], base[:, :])
            for b in range(B):
                ins = dve.tensor_scalar(idx[:, b:b + 1], base[:, b:b + 1], float(b * NKEY), None, ALU.add)
            ins.then_inc(idx_ready, 1)
            dve.wait_ge(ld_segg, 16)
            dve.wait_ge(ld_cst, 16)
            link(dve.tensor_copy(segh[:, :], segg_i[:, :]))
            link(dve.tensor_scalar(low[:, :], segh[:, :], float(-LOOKBACK), None, ALU.add))
            link(dve.tensor_scalar(baseg[:, :], low[:, :], float(NKEY - WIN), 0.0, ALU.min, ALU.max))
            wide = [P, NG, WIN]
            link(dve.tensor_tensor(kid, baseg.unsqueeze(2).broadcast_to(wide), jidx.unsqueeze(1).broadcast_to(wide), ALU.add))
            link(dve.tensor_tensor(ge, kid, low.unsqueeze(2).broadcast_to(wide), ALU.is_ge))
            link(dve.tensor_tensor(kid, kid, segh.unsqueeze(2).broadcast_to(wide), ALU.is_le))
            link(dve.tensor_tensor(ge, ge, kid, ALU.mult))
            link(dve.tensor_reduce(anyg[:, :], ge, AX.X, ALU.max))
            dve.tensor_scalar(mask[:, :, GK:GK1].rearrange("p g o -> p (g o)"), anyg[:, :], NEG, None, ALU.mult)
            link(dve.tensor_scalar(ge, ge, -1.0, -NEG, ALU.add, ALU.mult))
            full = [P, NG, WIN, GQ]
            link(dve.tensor_tensor(mask[:, :, 0:GK].rearrange("p g (j i) -> p g j i", j=WIN),
                                   ge.unsqueeze(3).broadcast_to(full),
                                   negdiag.unsqueeze(1).unsqueeze(1).broadcast_to(full), ALU.add))
            dve.tensor_copy(sc[:, :, GK:GK1], mask[:, :, GK:GK1])
            for p in range(PAIRS):
                dve.wait_ge(qpair, p + 1)
                four = [R, 2, B, L]
                cosb = qcos[R:2 * R, :].unsqueeze(1).unsqueeze(1).broadcast_to(four)
                sinb = qsin[R:2 * R, :].unsqueeze(1).unsqueeze(1).broadcast_to(four)
                r = rq[R:2 * R, p % 2]
                if p >= 2:
                    dve.wait_ge(qr_sb, p - 1)
                split = "p (o b l) -> p o b l"
                dve.tensor_tensor(r[:, 0].rearrange("p o (b l) -> p o b l", b=B),
                                  bank(p % 2, 0, 512, R, R).rearrange(split, o=2, b=B), cosb, ALU.mult)
                link(dve.tensor_tensor(r[:, 1].rearrange("p o (b l) -> p o b l", b=B),
                                       bank(2 + p % 2, 0, 512, R, R).rearrange(split, o=2, b=B), sinb, ALU.mult))
                dve.tensor_tensor(qT[R:2 * R, :, 2 * p:2 * p + 2, :], r[:, 0].rearrange("p o (g i) -> p g o i", i=GQ),
                                  r[:, 1].rearrange("p o (g i) -> p g o i", i=GQ), ALU.add).then_inc(qr_sb, 1)
            for n in range(6):
                b, f = n // 3, n % 3
                if f == 0:
                    dve.wait_ge(got_rope[b], 16)
                dve.wait_ge(kc_sb, n + 1)
                if n >= 2:
                    dve.wait_ge(kr_sb, n - 1)
                r = rk[:, n % 2]
                raw = bank(6 + n % 2, 0, 3 * P).rearrange("p (j k) -> p j k", j=3)[:, :, KVC:2 * KVC]
                cs_ = rrow[:, b, :].rearrange("p (j k) -> p j k", j=WIN)[:, 3 * f:3 * f + 3, :]
                dve.tensor_tensor(r[:, 0], raw, cs_[:, :, 0:R], ALU.mult)
                dve.tensor_tensor(r[:, 1, :, 0:R // 2], raw[:, :, R // 2:R], cs_[:, :, R:R + R // 2], ALU.mult)
                ins = dve.tensor_tensor(r[:, 1, :, R // 2:R], raw[:, :, 0:R // 2], cs_[:, :, R + R // 2:2 * R], ALU.mult)
                ins.then_inc(kr_ps, 1)
                dve.wait_ge(kr_ps, n + 1)
                dve.tensor_tensor(krow[:, b, 3 * f:3 * f + 3, KVC:2 * KVC], r[:, 0], r[:, 1], ALU.add).then_inc(kr_sb, 1)
            for n in range(8):
                dve.wait_ge(scored, n + 1)
                dve.tensor_tensor(sc[:, 4 * n:4 * n + 4, 0:GK], bank(n % 2, 0, 4 * GK).rearrange("p (g k) -> p g k", g=4),
                                  mask[:, 4 * n:4 * n + 4, 0:GK], ALU.add).then_inc(sc_ps, 1)
                if n % 4 == 3:
                    b = n // 4
                    s = sc[:, b * GB:(b + 1) * GB, :]
                    dve.wait_ge(sc_ps, n + 1)
                    link(dve.tensor_reduce(mx[:, b * GB:(b + 1) * GB], s, AX.X, ALU.max))
                    dve.tensor_tensor(s, s, mx[:, b * GB:(b + 1) * GB].unsqueeze(2).broadcast_to([P, GB, GK1]), ALU.subtract)\
                       .then_inc(sc_ready, 1)
            for b in range(B):
                dve.wait_ge(csum, 4 * b + 4)
                link(dve.tensor_copy(msum[0:1, b, :], bank(6 + b, 0, D, 0, 1)))
                dve.tensor_tensor(msum[0:1, b, :], bank(6 + b, D, D, 0, 1), msum[0:1, b, :], ALU.add).then_inc(msum_sb, 1)
            for b in range(B):
                s, m = sc[:, b * GB:(b + 1) * GB, :], mx[:, b * GB:(b + 1) * GB]
                dve.wait_ge(sc_exp, b + 1)
                link(dve.tensor_reduce(m, s, AX.X, ALU.add))
                link(dve.reciprocal(m, m))
                dve.tensor_tensor(s, s, m.unsqueeze(2).broadcast_to([P, GB, GK1]), ALU.mult).then_inc(probs, 1)
            for n in range(4):
                dve.wait_ge(pv0, n + 1)
                dve.tensor_copy(oT.rearrange("k p (g i) -> k g p i", i=GQ)[:, 8 * n:8 * n + 8],
                                bank(4 + n % 2, 0, 512).rearrange("k (g p i) -> k g p i", g=8, p=PAIRS)).then_inc(ot_sb, 1)
            dve.wait_ge(pe_step, MLA_OUT)
            dve.tensor_tensor(xres[:, :, :], bank(0, 0, 512).rearrange("p (b d) -> p b d", b=B), xres[:, :, :], ALU.add)\
               .then_inc(mla_done, 1)
            dve.wait_ge(mla_done, 1)

            normalise(1)
            link(dve.memset(xpad[:, :, :, 0:DC - 1], 0.0))
            dve.memset(dA[:, :, :, :], 0.0)
            dve.wait_ge(ld_w1, 16)
            for k in range(DC):
                for t in range(ET):
                    if k == 0 and t % 2 == 0:
                        dve.wait_ge(xz_sb, t // 2 + 1)
                    a, src = acc[:, t, :].rearrange("p (b l) -> p b l", b=B), xpad[:, t, :, k:k + L]
                    if k == 0:
                        ins = dve.tensor_scalar(a, src, conv_w[:, t, 0:1], conv_b[:, t:t + 1], ALU.mult, ALU.add)
                    else:
                        ins = dve.scalar_tensor_tensor(out=a, in0=src, scalar=conv_w[:, t, k:k + 1], in1=a,
                                                       op0=ALU.mult, op1=ALU.add)
                if k < DC - 1:
                    link(ins)
            ins.then_inc(conv, 1)
            acc_f = acc.rearrange("p t n -> p (t n)")
            dve.wait_ge(xc_tanh, 1)
            link(dve.scalar_tensor_tensor(out=xc[:, :], in0=th[:, :], scalar=1.0, in1=acc_f, op0=ALU.add, op1=ALU.mult))
            dve.tensor_scalar(xc[:, :], xc[:, :], 0.5, None, ALU.mult).then_inc(xc_ready, 1)
            dve.wait_ge(xc_ready, 1)
            tq_f = tq.rearrange("p a b -> p (a b)")
            dve.wait_ge(pe_step, DLIN)
            for t in range(ET):
                ins = dve.tensor_scalar(acc[:, t, :], bank(5 + t // 2, (t % 2) * T, T), b_dt[:, t:t + 1], None, ALU.add)
            ins.then_inc(dlin_ps, 1)
            dve.wait_ge(sp_ln, 1)
            delta_f, u_f = delta.rearrange("p t n -> p (t n)"), u.rearrange("p t n -> p (t n)")
            dve.scalar_tensor_tensor(out=delta_f, in0=acc_f, scalar=0.0, in1=th[:, :], op0=ALU.max, op1=ALU.add)\
               .then_inc(delta_ready, 1)
            dve.wait_ge(delta_ready, 1)
            dve.tensor_tensor(u_f, delta_f, xc[:, :], ALU.mult).then_inc(u_ready, 1)
            for t in range(ET):
                ins = dve.tensor_scalar(acc_f[:, t * T:(t + 1) * T], xc[:, t * T:(t + 1) * T], dskip[:, t:t + 1], None, ALU.mult)
            ins.then_inc(skip, 1)
            dve.nop().then_inc(h_ready, 2)
            dve.nop().then_inc(hc_made, 2)
            dve.nop().then_inc(kb_sb, 2)
            dve.nop().then_inc(ktc_sb[1], 1)

            def state(i, s):
                dve.wait_ge(dA_ready, 2 * i + s + 1)
                dve.wait_ge(dbx_ready, 2 * i + s + 1)
                dve.tensor_tensor_scan(hst[:, s, :], dA[:, s].rearrange("p t n -> p (t n)"),
                                       dbx[:, s].rearrange("p t n -> p (t n)"), 0.0, ALU.mult, ALU.add).then_inc(h_ready, 1)
                dve.wait_ge(h_ready, 2 * i + s + 3)
                dve.wait_ge(hc_used, 2 * i + s + 1)
                dve.tensor_tensor(hc[:, s], hst[:, s, :].rearrange("p (t n) -> p t n", t=ET),
                                  bc[:, s, 1, :].unsqueeze(1).broadcast_to([P, ET, T]), ALU.mult).then_inc(hc_made, 1)

            KV_LINKS = 3
            start = link.n
            with dve.Fori(0, NC) as i:
                link.n, link.off = start, KV_LINKS * i
                state(i, 0)
                dve.wait_ge(kq_ready, i + 1)
                for n in range(2):
                    dve.wait_ge(k_ps, 2 * i + n + 1)
                    dve.tensor_tensor(kb[:, 2 * n:2 * n + 2, :], bank(2 + n, 0, 512).rearrange("p (t d) -> p t d", t=2),
                                      b_k.unsqueeze(1).broadcast_to([P, 2, D]), ALU.add).then_inc(kb_sb, 1)
                dve.wait_ge(kb_sb, 2 * i + 4)
                link(dve.tensor_reduce(kmx[:, :], kb.rearrange("p t (h d) -> p (t h) d", h=H), AX.X, ALU.max,
                                       apply_absolute_value=True))
                link(dve.tensor_scalar(ksc[:, :], kmx[:, :], 1.0 / QMAX, 1e-8, ALU.mult, ALU.max))
                dve.reciprocal(krs[:, :], ksc[:, :]).then_inc(krs_ready, 1)
                state(i, 1)
                dve.wait_ge(tq_ready, i + 1)
                link(dve.tensor_scalar(tq_f, tq_f, MAGIC, MAGIC + QMAX, ALU.add, ALU.min))
                dve.tensor_scalar(tq_f, tq_f, MAGIC - QMAX, MAGIC, ALU.max, ALU.subtract).then_inc(k_int, 1)
                dve.wait_ge(k_hi, 2 * i + 1)
                k3v = k3.rearrange("k t h a d -> k (t h) a d")
                dve.tensor_tensor(r1[:, :, :], kq[:, :, :], k3v[:, :, 0, :], ALU.subtract).then_inc(r1_ready, 1)
                dve.wait_ge(r1_ready, i + 1)
                dve.wait_ge(k_hi, 2 * i + 2)
                dve.tensor_tensor(k3v[:, :, 2, :], r1[:, :, :], k3v[:, :, 1, :], ALU.subtract).then_inc(k3_ready, 1)
                for n in (1, 3):
                    dve.wait_ge(ktc_tr, 4 * i + n + 2)
                    if n == 1:
                        dve.wait_ge(kt_stored, 16 * i + 16)
                    dve.tensor_copy(ktc[:, 2 * n:2 * n + 2, :].rearrange("p a k -> p (a k)"),
                                    bank(4 + n % 2, 0, 512, 0, PR).bitcast(BF16)).then_inc(ktc_sb[1], 1)
            assert link.n == start + KV_LINKS, link.n - start
            link.n, link.off = start + KV_LINKS * NC, 0
            dve.wait_ge(v_sb, 2 * NC + 2)
            link(dve.tensor_reduce(vmx[:, :], vT[:, :, :], AX.X, ALU.max, apply_absolute_value=True))
            link(dve.tensor_scalar(vsc[:, :], vmx[:, :], 1.0 / QMAX, 1e-8, ALU.mult, ALU.max))
            dve.reciprocal(vrs[:, :], vsc[:, :]).then_inc(vsc_ready, 1)
            dve.wait_ge(pe_step, Y_DONE)
            dve.wait_ge(z_tanh, 1)
            link(dve.scalar_tensor_tensor(out=zT[:, :], in0=th[:, :], scalar=1.0, in1=zT[:, :], op0=ALU.add, op1=ALU.mult))
            for n in range(2):
                ins = dve.scalar_tensor_tensor(out=acc_f[:, n * 512:(n + 1) * 512], in0=bank(6 + n, 0, 512), scalar=0.5,
                                               in1=zT[:, n * 512:(n + 1) * 512], op0=ALU.mult, op1=ALU.mult)
            ins.then_inc(gated, 1)
            dve.wait_ge(v_round, 2)
            v_f = vT.rearrange("p c k -> p (c k)")
            link(dve.tensor_scalar(v_f, v_f, MAGIC + QMAX, MAGIC - QMAX, ALU.min, ALU.max))
            dve.tensor_scalar(vqb.rearrange("p c k -> p (c k)"), v_f, MAGIC, None, ALU.subtract).then_inc(vq_ready, 1)
            dve.wait_ge(pe_step, MIX_OUT)
            dve.tensor_tensor(xres[:, :, :], bank(2, 0, 512).rearrange("p (b d) -> p b d", b=B), xres[:, :, :], ALU.add)\
               .then_inc(mix_add, 1)
            dve.wait_ge(mix_add, 1)

            normalise(2)
            for n in range(4):
                h2 = hq[:, 2 * n:2 * n + 2, :].rearrange("p m t -> p (m t)")
                dve.wait_ge(ff_h, n + 1)
                link(dve.tensor_scalar(h2, bank(n, 0, 512), 10.0, 32767.0, ALU.mult, ALU.min))
                link(dve.tensor_scalar(h2, h2, -32768.0, MAGIC, ALU.max, ALU.add))
                dve.tensor_scalar(h2, h2, MAGIC, None, ALU.subtract).then_inc(ff_q, 1)
            dve.wait_ge(pe_step, FF_OUT)
            link(dve.tensor_tensor(xres[:, :, :], bank(4, 0, 512).rearrange("p (b d) -> p b d", b=B), xres[:, :, :], ALU.add))

            normalise(3)
            dve.wait_ge(ld_w3a, 16)
            dve.wait_ge(pe_step, Q_PS)
            link(dve.tensor_tensor(qb.rearrange("p (b h) d -> p b (h d)", b=B), bank(0, 0, 512).rearrange("p (b d) -> p b d", b=B),
                                   b_q.unsqueeze(1).broadcast_to([P, B, D]), ALU.add))
            link(dve.tensor_reduce(qmx[:, :], qb, AX.X, ALU.max, apply_absolute_value=True))
            link(dve.tensor_scalar(qsc[:, :], qmx[:, :], HW ** -0.5 / QMAX, 1e-8, ALU.mult, ALU.max))
            link(dve.reciprocal(qrs[:, :], qsc[:, :]))
            link(dve.scalar_tensor_tensor(out=qb, in0=qb, scalar=HW ** -0.5, in1=qrs.unsqueeze(2).broadcast_to([P, B * H, HW]),
                                          op0=ALU.mult, op1=ALU.mult))
            link(dve.tensor_scalar(qb, qb, MAGIC, MAGIC + QMAX, ALU.add, ALU.min))
            dve.tensor_scalar(q3, qb.unsqueeze(2).broadcast_to([P, B * H, 3, HW]), MAGIC - QMAX, MAGIC, ALU.max, ALU.subtract)\
               .then_inc(q3_ready, 1)
            for sgn, o in ((1.0, 0), (-1.0, 4)):
                ins = dve.tensor_scalar(sqa[:, :, o:o + 4].rearrange("q p (o b) -> q p o b", o=2),
                                        qsc.rearrange("q (b p o) -> q p o b", b=B, o=2), sgn, None, ALU.mult)
            ins.then_inc(sqa_ready, 1)
            dve.wait_ge(pe_step, Q_TR)
            dve.wait_ge(hmask_ready, 1)
            for o in range(2):
                dve.tensor_scalar(qz[:, :, o, :].rearrange("r p (b q) -> r b p q", b=B),
                                  ps[0:PR, 1:3, :].rearrange("r b n -> r (b n)").bitcast(BF16)
                                  .rearrange("r (b p q) -> r b p q", b=B, q=P),
                                  hmask[0:PR, o:o + 1], None, ALU.mult).then_inc(qz_ready, 1)
            link(dve.tensor_tensor(xres[:, :, :], xres[:, :, :], b_p.unsqueeze(1).broadcast_to([P, B, D]), ALU.add))
            dve.nop().then_inc(ptr_sb[0], 2)
            dve.nop().then_inc(s_read, 2)
            dve.nop().then_inc(o_read, 2)

            def maxima(it, j, c):
                u = 8 * it + j
                if c == 0:
                    dve.wait_ge(p_ready, u + 1)
                dve.wait_ge(s_ps, 4 * u + c + 1)
                dve.tensor_scalar(s_sb[:, j % 2, c * 1024:(c + 1) * 1024], ps[:, 2 * (c % 2):2 * (c % 2) + 2, :]
                                  .rearrange("p a n -> p (a n)"), 1.0, None, ALU.mult, ALU.max,
                                  accum_out=mxs[:, j % 2, c:c + 1]).then_inc(s_read, 1)
                if c == 3:
                    kk = j // 4
                    if j % 4 == 0:
                        dve.wait_ge(ld_sqs[kk], 16 * it + 16)
                    dve.wait_ge(s_read, 4 * u + 6)
                    dve.tensor_reduce(mx1[:, j % 2:j % 2 + 1], mxs[:, j % 2, :], AX.X, ALU.max).then_inc(mx_ready, 1)
                    dve.wait_ge(mx_ready, u + 1)
                    dve.tensor_scalar(nb[:, j % 2:j % 2 + 1], mx1[:, j % 2:j % 2 + 1], sqs[:, kk, 4 + j % 4:5 + j % 4], LN255,
                                      ALU.mult, ALU.add).then_inc(nb_ready, 1)

            def columns16(it, j, c):
                u = 8 * it + j
                dve.wait_ge(t_ps, 4 * u + c + 9)
                dve.wait_ge(ptr_used, 4 * u + c + 1)
                dve.tensor_scalar(ptr[:, c, :], bank(4 + c % 3, 0, 512).bitcast(F16), -1024.0, None, ALU.add)\
                   .then_inc(ptr_sb[0], 1)

            def sums(it, g):
                n = 2 * it + g
                dve.wait_ge(ptr_used, 4 * (8 * it + 4 * g + 4) + 4)
                dve.tensor_copy(zall[:, bass.ds(n, 1), :].rearrange("q o u -> q (o u)"), zs[:, g, :])
                dve.tensor_copy(oall[:, bass.ds(n, 1), :, :].rearrange("q o u d -> q (o u d)"), bank(7, 0, 4 * HW)).then_inc(o_read, 1)

            def turn(it, j, last):
                for c in range(4):
                    if not (last and j >= 6):
                        maxima(it + (j + 2) // 8, (j + 2) % 8, c)
                    if c < 2:
                        columns16(it, j, c)
                if j % 4 == 3:
                    sums(it, j // 4)

            for j in range(2):
                for c in range(4):
                    maxima(0, j, c)
            with dve.Fori(0, 3) as it:
                for j in range(8):
                    turn(it, j, False)
            for j in range(8):
                turn(3, j, True)
            dve.wait_ge(o_read, 2 + PAIRS)
            link(dve.reciprocal(rz[:, :], zall.rearrange("q p u -> q (p u)")))
            for b in range(B):
                ins = dve.tensor_tensor(onrm[:, b, :].rearrange("q (p o d) -> q p o d", p=PAIRS, o=2),
                                        oall.rearrange("q p (o b) d -> q b p o d", b=B)[:, b],
                                        rz.rearrange("q (p o b) -> q b p o", o=2, b=B)[:, b].unsqueeze(3)
                                        .broadcast_to([P, PAIRS, 2, HW]), ALU.mult)
            ins.then_inc(on_rows, 1)
            dve.wait_ge(pe_step, X_OUT)
            link(dve.tensor_tensor(xres[:, :, :], bank(5, 0, 512).rearrange("p (b d) -> p b d", b=B), xres[:, :, :], ALU.add))

            normalise(4)
            dve.wait_ge(oa_rows, 1)
            dve.tensor_tensor(prod[:, 0, :], bank(0, 0, D), q1[:, :], ALU.mult)
            link(dve.tensor_tensor(prod[:, 1, :], bank(1, 0, D), q1[:, :], ALU.mult))
            link(dve.tensor_reduce(s2[:, :, :].rearrange("p m h -> p (m h)"), prod.rearrange("p m (h d) -> p (m h) d", d=HW),
                                   AX.X, ALU.add))
            link(dve.tensor_tensor(m2[:, :], s2[:, 0, :], s2[:, 1, :], ALU.max))
            dve.tensor_tensor(s2[:, :, :], s2[:, :, :], m2.unsqueeze(1).broadcast_to([P, 2, H]), ALU.subtract).then_inc(e2_arg, 1)
            dve.wait_ge(e2_ready, 1)
            link(dve.tensor_tensor(z2[:, :], e2[:, 0, :], e2[:, 1, :], ALU.add))
            link(dve.reciprocal(z2[:, :], z2[:, :]))
            link(dve.tensor_tensor(e2[:, :, :], e2[:, :, :], z2.unsqueeze(1).broadcast_to([P, 2, H]), ALU.mult))
            for m in range(2):
                ins = dve.tensor_tensor(pv2[:, m, :].rearrange("p (h d) -> p h d", d=HW),
                                        bank(m, D, D).rearrange("p (h d) -> p h d", d=HW),
                                        e2[:, m, :].unsqueeze(2).broadcast_to([P, H, HW]), ALU.mult)
            link(ins)
            dve.nop().then_inc(qkv_used, 1)
            dve.tensor_tensor(orow[:, 1, :], pv2[:, 0, :], pv2[:, 1, :], ALU.add).then_inc(oa_rows, 1)
            dve.wait_ge(pe_step, SA_OUT)
            link(dve.tensor_tensor(xres[:, :, :], bank(4, 0, 512).rearrange("p (b d) -> p b d", b=B), xres[:, :, :], ALU.add))

            normalise(5)
            dve.wait_ge(pe_step, LOGITS)
            for b in range(B):
                ins = dve.max(top[:, b, :], bank(7, b * E, E))
            link(ins)
            dve.tensor_tensor(te[:, :, :], top[:, :, 0:2], top[:, :, 0:1].broadcast_to([P, B, 2]), ALU.subtract).then_inc(te_arg, 1)
            dve.wait_ge(te_ready, 1)
            link(dve.tensor_tensor(tz[:, :], te[:, :, 0], te[:, :, 1], ALU.add))
            link(dve.reciprocal(tz[:, :], tz[:, :]))
            link(dve.tensor_tensor(te[:, :, :], te[:, :, :], tz.unsqueeze(2).broadcast_to([P, B, 2]), ALU.mult))
            link(dve.tensor_tensor(comb[:, :], te[:, :, 0], te[:, :, 1], ALU.add))
            for m in range(FT + 1):
                dve.wait_ge(moe_t, m + 1)
                link(dve.scalar_tensor_tensor(out=ga[:, m % 2, :], in0=tg[:, m % 2, :], scalar=1.0, in1=bank(m % 4, 0, T),
                                              op0=ALU.add, op1=ALU.mult))
                dve.scalar_tensor_tensor(out=hT[:, m, :], in0=ga[:, m % 2, :], scalar=0.5, in1=bank(m % 4, T, T),
                                         op0=ALU.mult, op1=ALU.mult).then_inc(moe_h, 1)
            dve.wait_ge(moe_out, 1)
            link(dve.tensor_tensor(xres[:, :, :], bank(5, 0, 512).rearrange("p (b d) -> p b d", b=B), xres[:, :, :], ALU.add))
            dve.wait_ge(moe_out, 2)
            for b in range(B):
                dve.scalar_tensor_tensor(out=xres[:, b, :], in0=bank(6, b * D, D), scalar=comb[:, b:b + 1], in1=xres[:, b, :],
                                         op0=ALU.mult, op1=ALU.add).then_inc(y_ready, 1)

        @block.tensor
        def _(pe):
            def columns(k):
                pe.wait_ge(ln_rows, 2 * (k + 1))
                for c in range(CH):
                    for b in range(B):
                        mm = pe.transpose(bank(7, c * T + b * L, P), xn[:, b, c * P:(c + 1) * P], ident)
                mm.then_inc(ln_tr, 1)

            pe.wait_ge(ld_cst, 16)
            pe.wait_ge(ld_w0a, 16)
            for h in range(H):
                pe.matmul(bank(h // 8, (h % 8) * KVC, KVC, 0, QC), w_uqT[:, h, :], w_ukT[:, h, :], start=True, stop=True)
            for c in range(CH):
                mm = pe.matmul(bank(2, c * R, R), w_kvcT[0:KVC, c * P:(c + 1) * P], w_kr[0:KVC, :], start=True, stop=True)
            mm.then_inc(pe_step, 1)
            columns(0)
            pe.wait_ge(ld_w0b, 16)
            for p in range(PAIRS):
                for o in range(2):
                    mm = pe.matmul(bank(3 + p // 2, (p % 2) * D, D, o * KVC, KVC), w_uvT[:, 2 * p + o, :], w_o[:, 2 * p + o, :],
                                   start=True, stop=True)
            mm.then_inc(pe_step, 1)
            pe.wait_ge(ln_cols, 1)
            for c in range(CH):
                mm = pe.matmul(bank(7, 0, T, 0, QC), w_dq[:, c, :], xnT[:, c, :], start=(c == 0), stop=(c == CH - 1))
            mm.then_inc(pe_step, 1)
            pe.wait_ge(qlat_sb, 1)
            pe.wait_ge(wabs_sb, 3)
            for p in range(PAIRS):
                if p >= 2:
                    pe.wait_ge(qa_sb, p - 1)
                    pe.wait_ge(qr_sb, p - 1)
                else:
                    pe.wait_ge(wvo_sb, 1)
                for o in range(2):
                    pe.matmul(bank(p % 2, o * T, T), w_qall[0:QC, 2 * p + o, :], q_cT[0:QC, :], start=True, stop=True)
                for o in range(2):
                    mm = pe.matmul(bank(2 + p % 2, o * T, T, R, R), w_qrs[0:QC, 2 * p + o, :], q_cT[0:QC, :],
                                   start=True, stop=True)
                mm.then_inc(qpair, 1)
            fill = 0
            for b in range(B):
                pe.wait_ge(got_rows[b], 16)
                for n in range(CH * WIN):
                    if n % 4 == 0:
                        if fill == 0:
                            pe.wait_ge(wvo_sb, 4)
                        if fill >= 2:
                            pe.wait_ge(gt_sb, fill - 1)
                    j, c = n // CH, n % CH
                    mm = pe.transpose(bank(4 + fill % 2, (n % 4) * P, P), grow[:, b, j * D + c * P:j * D + (c + 1) * P], ident)
                    if n % 4 == 3 or n == CH * WIN - 1:
                        mm.then_inc(gt_tr, 1)
                        fill += 1
                for f in range(3):
                    pe.wait_ge(gt_sb, fill)
                    n = 3 * b + f
                    if n == 0:
                        pe.wait_ge(qlat_sb, 1)
                    if n >= 2:
                        pe.wait_ge(kc_sb, n - 1)
                        pe.wait_ge(kr_ps, n - 1)
                    for j in range(3):
                        for c in range(CH):
                            mm = pe.matmul(bank(6 + n % 2, j * P, P), gT[:, c, 3 * f + j, :], w_kcat[:, c, :],
                                           start=(c == 0), stop=(c == CH - 1))
                    mm.then_inc(kpr, 1)
            for n in range(6):
                b, f = n // 3, n % 3
                pe.wait_ge(kc_sb, n + 1)
                pe.wait_ge(kr_sb, n + 1)
                pe.wait_ge(gt_sb, 10) if n < 2 else pe.wait_ge(kt_sb, n - 1)
                for j in range(3):
                    mm = pe.transpose(bank(4 + n % 2, j * P, P), krow[:, b, 3 * f + j, :], ident)
                mm.then_inc(kt_tr, 1)
            for c in range(NC):
                pe.wait_ge(ld_cs[c % 2], 16 * (c // 2 + 1))
                for t in range(CT // 2):
                    mm = pe.matmul(bank(6 + c // 4, 0, 512, 0, 1), ones[:, 0:1], cs[:, c % 2, 2 * t:2 * t + 2, :],
                                   start=(c % 4 == 0 and t == 0), stop=(c % 4 == 3 and t == CT // 2 - 1))
                mm.then_inc(csum, 1)
            pe.wait_ge(qa_sb, PAIRS)
            pe.wait_ge(qr_sb, PAIRS)
            for n in range(8):
                pe.wait_ge(kt_sb, 3 if n < 4 else 6)
                if n >= 2:
                    pe.wait_ge(sc_ps, n - 1)
                for i in range(4):
                    g = 4 * n + i
                    q, b = g * GQ, g // GB
                    mm = pe.matmul(bank(n % 2, i * GK, GK), qT[:, g].rearrange("k h i -> k (h i)"), kcat[:, b, :, q % L:q % L + GQ],
                                   start=True, stop=True)
                mm.then_inc(scored, 1)
            pe.wait_ge(msum_sb, B)
            for b in range(B):
                for c in range(CH):
                    mm = pe.matmul(bank(6, 8 + CH * b + c, 1), msum[0:1, b, c * P:(c + 1) * P], ones[0:1, 0:1],
                                   start=True, stop=True)
            mm.then_inc(pe_step, 1)
            pe.wait_ge(mtr_sb, 1)
            for b in range(B):
                for c in range(CH):
                    mm = pe.matmul(bank(6, 64 + KVC * b, KVC, 0, 1), mT[:, CH * b + c:CH * b + c + 1], w_kcat[:, c, 0:KVC],
                                   start=(c == 0), stop=(c == CH - 1))
            mm.then_inc(pe_step, 1)
            for n in range(8):
                pe.wait_ge(probs, 1 if n < 4 else 2)
                if n < 2:
                    pe.wait_ge(qr_sb, PAIRS)
                else:
                    pe.wait_ge(pt_sb, n - 1)
                for i in range(4):
                    mm = pe.transpose(bank(2 + n % 2, i * P, P, 0, GK1), sc[:, 4 * n + i, :], ident)
                mm.then_inc(pt_tr, 1)
            pe.wait_ge(ld_kvg, 16 * (WIN + 1))
            for n in range(4):
                pe.wait_ge(pt_sb, 2 * n + 2)
                pe.wait_ge(kt_sb, 6) if n < 2 else pe.wait_ge(ot_sb, n - 1)
                for i in range(8):
                    g = 8 * n + i
                    for o in range(2):
                        pr = pT[0:GK1, g, :].rearrange("k (p o i) -> k o p i", o=2, i=GQ)[:, o]
                        mm = pe.matmul(bank(4 + n % 2, i * 64, 64, o * KVC, KVC), kvg[0:GK1, g, :], pr, start=True, stop=True)
                mm.then_inc(pv0, 1)
            pe.wait_ge(ot_sb, 4)
            pe.wait_ge(wvo_sb, 4)
            for b in range(B):
                for p in range(PAIRS):
                    mm = pe.matmul(bank(0, b * D, D), oT[:, p, b * L:(b + 1) * L], w_vo[:, p, :],
                                   start=(p == 0), stop=(p == PAIRS - 1))
            mm.then_inc(pe_step, 1)

            columns(1)
            pe.wait_ge(ld_w1, 16)
            pe.wait_ge(ln_cols, 2)
            for m in range(2 * ET):
                for c in range(CH):
                    mm = pe.matmul(bank(m // 2, (m % 2) * T, T), w_in[:, c, m * P:(m + 1) * P], xnT[:, c, :],
                                   start=(c == 0), stop=(c == CH - 1))
                if m % 2:
                    mm.then_inc(xz, 1)
            pe.wait_ge(xc_ready, 1)
            for c in range(ET):
                pe.matmul(bank(4, 0, T), w_x[:, c, 0:DR], xc[:, c * T:(c + 1) * T], start=(c == 0), stop=(c == ET - 1))
            for c in range(ET):
                mm = pe.matmul(bank(4, T, T, 0, 2 * DS), w_x[:, c, DR:DR + 2 * DS], xc[:, c * T:(c + 1) * T],
                               start=(c == 0), stop=(c == ET - 1))
            mm.then_inc(pe_step, 1)
            pe.wait_ge(dt_sb, 1)
            for t in range(ET):
                mm = pe.matmul(bank(5 + t // 2, (t % 2) * T, T), w_dt[:, t * P:(t + 1) * P], dtT[:, :], start=True, stop=True)
            mm.then_inc(pe_step, 1)
            pe.wait_ge(skip, 1)
            for n in range(2):
                pe.matmul(bank(6 + n, 0, 512), ident, acc.rearrange("p t n -> p (t n)")[:, n * 512:(n + 1) * 512],
                          start=True, stop=True)
            pe.wait_ge(xz_sb, 4)
            pe.wait_ge(dt_sb, 2)

            def state(i, s):
                pe.wait_ge(hc_made, 2 * i + s + 3)
                for n in range(2):
                    mm = pe.matmul(bank(6 + n, 0, 512), ident, hc[:, s].rearrange("p t n -> p (t n)")[:, n * 512:(n + 1) * 512],
                                   start=False, stop=True, skip_group_check=True)
                mm.then_inc(hc_used, 1)

            pe.nop().then_inc(cx_tr, 1)
            pe.nop().then_inc(v_ps, 2)
            pe.nop().then_inc(ktc_tr, 1)
            pe.nop().then_inc(hc_used, 2)
            with pe.Fori(0, NC) as i:
                pe.wait_ge(ld_cx, 16 * i + 16)
                pe.wait_ge(v_sb, 2 * i + 2)
                for t in range(CT):
                    for c in range(CH):
                        mm = pe.transpose(bank(c, t * P, P), cx[:, t, c * P:(c + 1) * P], ident)
                mm.then_inc(cx_tr, 1)
                pe.wait_ge(cT_sb, 2 * i + 2)
                pe.wait_ge(kb_sb, 2 * i + 2)
                for t in range(CT):
                    for c in range(CH):
                        mm = pe.matmul(bank(2 + t // 2, (t % 2) * D, D), cT[:, c, t * P:(t + 1) * P], w_kv[:, c, 0:D],
                                       start=(c == 0), stop=(c == CH - 1))
                    if t % 2:
                        mm.then_inc(k_ps, 1)
                state(i, 0)
                for m in range(CH):
                    for c in range(CH):
                        mm = pe.matmul(bank(m, 0, CK), w_kv[:, c, D + m * P:D + (m + 1) * P], cT[:, c, :],
                                       start=(c == 0), stop=(c == CH - 1))
                    mm.then_inc(v_ps, 1)
                state(i, 1)
                pe.wait_ge(k3_ready, i + 1)
                for n in range(4):
                    pe.wait_ge(ktc_sb[n % 2], 2 * i + n // 2 + 1)
                    for o in range(2):
                        p = 2 * n + o
                        for t in range(CT):
                            dst = bank(4 + n % 2, 0, 512, 0, PR).bitcast(BF16)[:, (o * CT + t) * P:(o * CT + t + 1) * P]
                            mm = pe.transpose(dst, k3[:, t, 2 * p:2 * p + 2].rearrange("k h a d -> k (h a d)"), identb[:, :])
                    mm.then_inc(ktc_tr, 1)
            pe.nop().then_inc(pe_step, 1)
            for n in range(8):
                m, q = n // 4, n % 4
                pe.wait_ge(vq_ready, 1)
                if n >= 2:
                    pe.wait_ge(vr_sb, n - 1)
                else:
                    pe.wait_ge(v_sb, 2 * NC + 2)
                for t in range(8):
                    k = (8 * q + t) * P
                    mm = pe.transpose(bank(n % 2, 0, 512).bitcast(BF16)[:, t * P:(t + 1) * P], vqb[:, m, k:k + P], identb[:, :])
                mm.then_inc(vr_tr, 1)
            pe.wait_ge(gated, 1)
            pe.wait_ge(kb_sb, 2 * NC + 2)
            for b in range(B):
                for t in range(ET):
                    mm = pe.matmul(bank(2, b * D, D), acc[:, t, b * L:(b + 1) * L], w_out[:, t, :],
                                   start=(t == 0), stop=(t == ET - 1))
            mm.then_inc(pe_step, 1)

            columns(2)
            pe.wait_ge(ln_cols, 3)
            pe.wait_ge(ld_w2, 16)
            pe.wait_ge(vr_sb, 8)
            pe.wait_ge(mix_add, 1)
            for m in range(FT):
                for c in range(CH):
                    mm = pe.matmul(bank(m // 2, (m % 2) * T, T), w_f1[:, c, m * P:(m + 1) * P], xnT[:, c, :],
                                   start=(c == 0), stop=(c == CH - 1))
                if m % 2:
                    mm.then_inc(ff_h, 1)
            pe.wait_ge(ff_a, 4)
            for b in range(B):
                for m in range(FT):
                    mm = pe.matmul(bank(4, b * D, D), aT[:, m, b * L:(b + 1) * L], w_f2[:, m, :],
                                   start=(m == 0), stop=(m == FT - 1))
            mm.then_inc(pe_step, 1)

            columns(3)
            pe.wait_ge(ln_cols, 4)
            pe.wait_ge(ld_w3a, 16)
            for b in range(B):
                for c in range(CH):
                    mm = pe.matmul(bank(0, b * D, D), xnT[:, c, b * L:(b + 1) * L], w_q[:, c, :],
                                   start=(c == 0), stop=(c == CH - 1))
            mm.then_inc(pe_step, 1)
            pe.wait_ge(q3_ready, 1)
            for b in range(B):
                for p in range(PAIRS):
                    dst = bank(1 + b, 0, 512, 0, PR).bitcast(BF16)[:, p * P:(p + 1) * P]
                    mm = pe.transpose(dst, q3[:, b * H + 2 * p:b * H + 2 * p + 2].rearrange("q h a d -> q (h a d)"), identb[:, :])
            mm.then_inc(pe_step, 1)
            pe.wait_ge(qz_ready, 2)
            pe.nop().then_inc(ptr_used, 4)
            pe.nop().then_inc(t_ps, 8)

            def scores(it, j):
                u, kk = 8 * it + j, j // 4
                if j % 4 == 0:
                    pe.wait_ge(ld_kqs[kk], 32 * it + 32)
                for c in range(4):
                    n = 4 * u + c
                    pe.wait_ge(s_read, n + 1)
                    q = KEYS + (j // 2 % 2) * T + (j % 2) * L
                    for m in range(2):
                        k = c * 1024 + m * 512
                        mm = pe.matmul(bank(2 * (c % 2) + m, 0, 512), kqs[:, kk, q:q + L], kqs[:, kk, k:k + 512],
                                       start=True, stop=True)
                    mm.then_inc(s_ps, 1)
                    yield

            def weighted(it, j):
                u, kk = 8 * it + j, j // 4
                pe.wait_ge(p_ready, u + 3)
                words = p8[:, j % 2].bitcast(F32)
                if j % 4 == 0:
                    pe.wait_ge(ld_vss[kk], 16 * it + 16)

                def values(c):
                    pe.wait_ge(ptr_sb[c // 2], 2 * u + c % 2 + 3)
                    if j % 4 == 0 and c == 0:
                        pe.wait_ge(o_read, 2 * it + j // 4 + 2)
                    for n in range(4):
                        for par in range(2):
                            t = 2 * (4 * c + n) + par
                            v = t * 2 * HW + (j // 2 % 2) * HW
                            mm = pe.matmul(bank(7, (j % 4) * HW, HW), ptr[:, c, n * 2 * P + par:(n + 1) * 2 * P:2],
                                           vss[:, kk, v:v + HW], start=(t == 0), stop=(t == KT - 1))
                    mm.then_inc(ptr_used, 1)

                for c in range(4):
                    who, count = ((1, 2), (0, 2), (1, 1), (0, 3))[c]
                    pe.wait_ge(ptr_sb[who], 2 * u + count)
                    for n in range(4):
                        w = (4 * c + n) * P
                        mm = pe.transpose(bank(4 + c % 3, n * P, P), words[:, w:w + P], ident)
                    mm.then_inc(t_ps, 1)
                    if c >= 1:
                        values(c - 1)
                    yield
                values(3)
                yield

            def both(a, b):
                for step in zip(a, b):
                    pass
                for step in b:
                    pass
                for step in a:
                    pass

            for j in range(2):
                for step in scores(0, j):
                    pass
            with pe.Fori(0, 3) as it:
                for j in range(8):
                    both(scores(it + (j + 2) // 8, (j + 2) % 8), weighted(it, j))
            for j in range(8):
                both(scores(3, j + 2) if j < 6 else iter(()), weighted(3, j))

            pe.wait_ge(on_rows, 1)
            for c in range(CH):
                for b in range(B):
                    mm = pe.transpose(bank(4, c * T + b * L, P), onrm[:, b, c * P:(c + 1) * P], ident)
            mm.then_inc(pe_step, 1)
            pe.wait_ge(on_cols, CH)
            for b in range(B):
                for c in range(CH):
                    mm = pe.matmul(bank(5, b * D, D), onT[:, c, b * L:(b + 1) * L], w_p[:, c, :],
                                   start=(c == 0), stop=(c == CH - 1))
            mm.then_inc(pe_step, 1)

            columns(4)
            pe.wait_ge(ln_cols, 5)
            pe.wait_ge(ld_w3b, 16)
            for b, n0, bk in ((0, D, 0), (1, D, 1), (1, 0, 2)):
                n1 = 3 * D if n0 else D
                for c in range(CH):
                    mm = pe.matmul(bank(bk, 0, n1 - n0), xnT[:, c, b * L:(b + 1) * L], w_qkv[:, c, n0:n1],
                                   start=(c == 0), stop=(c == CH - 1))
            mm.then_inc(pe_step, 1)
            pe.wait_ge(oa_rows, B)
            for c in range(CH):
                for b in range(B):
                    mm = pe.transpose(bank(3, c * T + b * L, P), orow[:, b, c * P:(c + 1) * P], ident)
            mm.then_inc(pe_step, 1)
            pe.wait_ge(oa_cols, 1)
            for b in range(B):
                for c in range(CH):
                    mm = pe.matmul(bank(4, b * D, D), oaT[:, c, b * L:(b + 1) * L], w_ao[:, c, :],
                                   start=(c == 0), stop=(c == CH - 1))
            mm.then_inc(pe_step, 1)

            columns(5)
            pe.wait_ge(ln_cols, 6)
            pe.wait_ge(qkv_used, 1)
            for b in range(B):
                for c in range(CH):
                    mm = pe.matmul(bank(7, b * E, E), xnT[:, c, b * L:(b + 1) * L], w_rt[:, c, :],
                                   start=(c == 0), stop=(c == CH - 1))
            mm.then_inc(pe_step, 1)
            for m in range(FT + 1):
                if m >= 4:
                    pe.wait_ge(moe_h, m - 3)
                for n, w in ((0, w_sg), (1, w_su)):
                    for c in range(CH):
                        mm = pe.matmul(bank(m % 4, n * T, T), w[:, c, m * P:(m + 1) * P], xnT[:, c, :],
                                       start=(c == 0), stop=(c == CH - 1))
                mm.then_inc(moe_gu, 1)
            pe.wait_ge(moe_h, FT)
            for b in range(B):
                for m in range(FT):
                    mm = pe.matmul(bank(5, b * D, D), hT[:, m, b * L:(b + 1) * L], w_sd[:, m, :],
                                   start=(m == 0), stop=(m == FT - 1))
            mm.then_inc(moe_out, 1)
            pe.wait_ge(moe_h, FT + 1)
            for b in range(B):
                mm = pe.matmul(bank(6, b * D, D), hT[:, FT, b * L:(b + 1) * L], w_sd[:, FT, :], start=True, stop=True)
            mm.then_inc(moe_out, 1)


_CONST = {}


def constants():
    import numpy as np

    half = R // 2
    inv = (1.0 / 10000.0 ** (np.arange(half, dtype=np.float32) / np.float32(half))).astype(np.float32)
    ang = np.arange(NKEY, dtype=np.float32)[:, None] * inv
    cos, sin = np.cos(ang).astype(np.float32), np.sin(ang).astype(np.float32)
    rope = np.concatenate([cos, cos, -sin, sin], 1)
    cst = np.zeros((P, CST), np.float32)
    cst[:, 0:128] = np.eye(P)
    cst[R:, 128:256] = rope[:L, 0:R].T
    cst[R:, 256:384] = rope[:L, R:].T
    cst[:, 384:512] = 1.0
    cst[:, 512:520] = np.where(np.arange(P)[:, None] % GQ == np.arange(GQ), 0.0, NEG)
    cst[:, 520:529] = np.arange(WIN)
    cst[:, 529] = MAGIC
    return cst, rope


def kernel(**inputs):
    import numpy as np
    import concourse.bacc as bacc
    from concourse.bass_utils import run_bass_kernel_spmd

    a = {k: np.asarray(v) for k, v in inputs.items()}

    def rows(w, n=P):
        return w.reshape(-1, n, w.shape[-1]).transpose(1, 0, 2).reshape(n, -1)

    def full(w):
        out = np.zeros((P, w.shape[1]), w.dtype)
        out[:w.shape[0]] = w
        return out

    def over(v):
        return np.broadcast_to(v, (P, v.shape[-1]))

    def swap(w):
        return np.concatenate([w[..., R // 2:], w[..., :R // 2]], -1)

    uq = a["L0_xattn_W_uq"].reshape(QC, H, HD)
    uk = a["L0_xattn_W_uk"].reshape(KVC, H, HD)
    uv = a["L0_xattn_W_uv"].reshape(KVC, H, HD)
    qr = a["L0_xattn_W_qr"].reshape(QC, H, R)
    kvc = rows(a["L0_xattn_W_kvc"]).reshape(P, CH, KVC)
    w0a = np.concatenate([
        rows(a["L0_xattn_W_dq"]),
        uq.transpose(2, 1, 0).reshape(P, -1),
        uk.transpose(2, 1, 0).reshape(P, -1),
        full(np.concatenate([np.zeros_like(qr), qr], 2).reshape(QC, -1)),
        full(swap(qr).reshape(QC, -1)),
        np.concatenate([kvc, np.zeros_like(kvc)], 2).reshape(P, -1),
        full(a["L0_xattn_W_kvc"].T),
        full(a["L0_xattn_W_kr"]),
    ], 1)
    w0b = np.concatenate([uv.transpose(2, 1, 0).reshape(P, -1), rows(a["L0_xattn_W_o"])], 1)
    w1 = np.concatenate([
        rows(a["L0_attn_W_in"].T), rows(a["L0_attn_W_x"].T), a["L0_attn_W_dt"].T, rows(a["L0_attn_W_out"].T),
        rows(a["L0_attn_conv_w"]), rows(a["L0_attn_conv_b"][:, None]), rows(a["L0_attn_b_dt"][:, None]),
        rows(a["L0_attn_Dp"][:, None]), rows(a["L0_attn_A_log"]), rows(a["L1_xattn_Wkv"]),
        over(a["L1_xattn_bkv"][:D]), rows(a["L1_xattn_bkv"][D:, None]),
    ], 1)
    w2 = np.concatenate([rows(a["L0_ffn_W1"].T), rows(a["L0_ffn_W2"].T)], 1)

    def beside(s, r):
        return np.concatenate([rows(s).reshape(P, CH, -1), rows(r).reshape(P, CH, -1)], 2).reshape(P, -1)

    w3 = np.concatenate([
        rows(a["L1_xattn_Wq"]), over(a["L1_xattn_bq"]), rows(a["L1_xattn_Wp"]), over(a["L1_xattn_bp"]),
        rows(a["L1_attn_weight_qkv"].T), rows(a["L1_attn_weight_out"].T),
        beside(a["L1_ffn_sh_gate"].T, a["L1_ffn_r_gate"].T), beside(a["L1_ffn_sh_up"].T, a["L1_ffn_r_up"].T),
        rows(a["L1_ffn_sh_down"].T), rows(a["L1_ffn_r_down"].T), rows(a["L1_ffn_router_weight"].T),
    ], 1)
    seg = a["itok_BxS_0_1023"].reshape(NG, GQ)
    cst, rope = constants()
    arrays = {
        "x": a["x"].transpose(1, 0, 2),
        "seg": a["itok_BxS_0_1023"].T,
        "segg": np.broadcast_to(seg.T[None], (H, GQ, NG)).reshape(P, NG),
        "context": a["ctx_2048"].reshape(KEYS, D),
        "rope": rope, "cst": cst, "w0a": w0a, "w0b": w0b, "w1": w1, "w2": w2, "w3": w3,
    }
    arrays = {f"in_{k}": np.ascontiguousarray(v) for k, v in arrays.items()}
    nc = bacc.Bacc("TRN2", target_bir_lowering=False, num_devices=1)
    args = [nc.dram_tensor(k, v.shape, mybir.dt.from_np(v.dtype), kind="ExternalInput").ap() for k, v in arrays.items()]
    out = nc.dram_tensor("out", (P, B, D), F32, kind="ExternalOutput").ap()
    perceiver_kernel(nc, *args, out)
    r = run_bass_kernel_spmd(nc, [arrays], core_ids=[0])
    return np.asarray(r.results[0]["out"]).transpose(1, 0, 2)
```

```python
from contextlib import ExitStack

import concourse.bass as bass
from concourse import mybir

ALU = mybir.AluOpType
ACT = mybir.ActivationFunctionType
AX = mybir.AxisListType
F32 = mybir.dt.float32
BF16 = mybir.dt.bfloat16
F16 = mybir.dt.float16
U8 = mybir.dt.uint8
I32 = mybir.dt.int32

P = 128
B, L, D = 2, 128, 256
T = B * L
CH = D // P
NKEY = 2048
KEYS = B * NKEY
EPS = 1e-5
NEG = -1e30
MAGIC = 12582912.0

H = 16
HD, KVC, QC, R = 128, 64, 96, 64
LOOKBACK = 8
WIN = LOOKBACK + 1
GQ = P // H
NG = T // GQ
GB = NG // B
GK = GQ * WIN
GK1 = GK + 1
MLA_SCALE = float((HD + R) ** -0.5)
DI, DS, DC, DR = 512, 16, 4, 128
ET = DI // P
LP = L + DC - 1
FF = 1024
FT = FF // P
HW = D // H
PAIRS = H // 2
PR = 2 * 3 * HW
CK = 512
CT = CK // P
NC = KEYS // CK
KT = KEYS // P
QMAX = 127.0
LN255 = 5.541263545158426
E = 8
CST = 530
W0A = H * QC + H * KVC + D + R
W0Q = CH * QC + CH * 2 * R + H * R
W0B = H * KVC + H * D
W1 = CH * 2 * DI + ET * (DR + 2 * DS) + DI + ET * D + ET * (DC + 3 + DS) + CH * 2 * D + D + CH
W2 = CH * FF + FT * D
W3 = 2 * (CH * D + D) + CH * 3 * D + CH * D + 2 * CH * (FF + P) + (FT + 1) * D + CH * E
ARENA = 40400
KV_LINKS = 3

UNITS = B * H


def unit(it, j):
    return it + j // 8, j % 8


def adds(c):
    per = NC // B
    return c // per * (per - 1) + max(c % per, 1)


class Chain:

    def __init__(self, engine, semaphore):
        self.engine, self.semaphore, self.n, self.off = engine, semaphore, 0, 0

    def __call__(self, ins):
        self.n += 1
        ins.then_inc(self.semaphore, 1)
        self.engine.wait_ge(self.semaphore, self.off + self.n)


def perceiver_kernel(nc, x_d, seg_d, segrep_d, ctx_d, rope_d, cst_d, w0a_d, w0q_d, w0b_d, w1_d, w2_d, w3_d, out_d):
    with ExitStack() as ctx:
        def sb(name, shape, dt=F32):
            return ctx.enter_context(nc.sbuf_tensor(name, shape, dt))

        def sem(name):
            return ctx.enter_context(nc.semaphore(name))

        def dram(name, shape, dt):
            return nc.dram_tensor(name, shape, dt).ap()

        ps = ctx.enter_context(nc.psum_tensor("ps", [P, 8, 512], F32))

        cst = sb("cst", [P, CST])
        ident, qcos, qsin = cst[:, 0:128], cst[:, 128:256], cst[:, 256:384]
        ones, negdiag, jidx = cst[:, 384:512], cst[:, 512:520], cst[:, 520:529]
        identb = sb("identb", [P, P], BF16)
        xres = sb("xres", [P, B, D])
        xn = sb("xn", [P, B, D])
        xnT = sb("xnT", [P, CH, T])
        ln_st = sb("ln_st", [P, B, 6])
        ln_mv = sb("ln_mv", [P, B, 2])
        ln_ve = sb("ln_ve", [P, B])
        ln_rs = sb("ln_rs", [P, B])
        neghalf = sb("neghalf", [P, B])
        w1 = sb("w1", [P, W1])
        vrow = sb("vrow", [P, PAIRS, KT * 2 * HW], F16)

        arena = sb("arena", [P, ARENA])
        at = [0]

        def phase(start=0):
            at[0] = start

        def take(shape, dt=F32, rows=P):
            n = 1
            for s in shape:
                n *= s
            words = n if dt in (F32, I32) else (n + 1) // 2 if dt in (BF16, F16) else n // 4
            a = arena[0:rows, at[0]:at[0] + words]
            at[0] += words
            assert at[0] <= ARENA, (at[0], ARENA)
            if dt != F32:
                a = a.bitcast(dt)
            if len(shape) > 1:
                names = "abcd"[:len(shape)]
                a = a.rearrange(f"p ({' '.join(names)}) -> p {' '.join(names)}",
                                **{k: s for k, s in zip(names[1:], shape[1:])})
            return a

        early = vrow.rearrange("k p n -> k (p n)").bitcast(F32)
        csums = early[:, 0:B * CT * D].rearrange("k (b t d) -> k b t d", b=B, t=CT)
        w0q = early[:, B * CT * D:B * CT * D + W0Q]
        w_dq = w0q[:, 0:CH * QC].rearrange("p (c n) -> p c n", c=CH)
        w_kcat = w0q[:, CH * QC:CH * (QC + 2 * R)].rearrange("p (c n) -> p c n", c=CH)
        w_qr = w0q[:, CH * (QC + 2 * R):W0Q].rearrange("p (h n) -> p h n", h=H)
        phase()
        w_uqT = take([H, QC])
        w_ukT = take([H, KVC])
        w_kvcT = take([D])
        w_kr = take([R])
        w0a = arena[:, 0:W0A]
        w_qall = take([H, 2 * R])
        w_qrs = take([H, R])
        w0b = take([W0B])
        at[0] -= W0B
        w_uvT = take([H, KVC])
        w_o = take([H, D])
        w_vo = take([PAIRS, D])
        g_at = at[0]
        grow = take([B, WIN * D])
        r_at = at[0]
        rrow = take([B, WIN * 2 * R])
        gT_at = at[0]
        gT = take([CH, WIN, P])
        krow = take([B, WIN, 2 * KVC])
        kcat = take([B, WIN, P])
        qT = take([NG, H, GQ])
        q_cT = take([T])
        rq = take([2, 2, 2, T])
        rk = take([2, 2, 3, R])
        seg_i = take([B], I32)
        segg_i = take([NG], I32)
        segf = take([B])
        base = take([B])
        idx = take([2 * B], I32)
        segh = take([NG])
        low = take([NG])
        baseg = take([NG])
        kid = take([NG, WIN])
        ge = take([NG, WIN])
        anyg = take([NG])
        mask = take([NG, GK1])
        sc = take([NG, GK1])
        mx = take([NG])
        mT = take([B * CH])
        phase(g_at)
        pT = take([NG, P])
        phase(r_at)
        oT = take([PAIRS, T])
        phase(gT_at)
        kvg = take([NG, KVC])
        phase()
        cs = take([2, CT, D])
        phase()
        kvm = take([NG, KVC], rows=1)
        taken = [0]

        def part(n):
            taken[0] += n
            return w1[:, taken[0] - n:taken[0]]

        w_in = part(CH * 2 * DI).rearrange("p (c n) -> p c n", c=CH)
        w_x = part(ET * (DR + 2 * DS)).rearrange("p (c n) -> p c n", c=ET)
        w_dt = part(DI)
        w_out = part(ET * D).rearrange("p (c n) -> p c n", c=ET)
        conv_w = part(ET * DC).rearrange("p (t k) -> p t k", t=ET)
        conv_b, b_dt, dskip = part(ET), part(ET), part(ET)
        a_log = part(ET * DS).rearrange("p (t s) -> p t s", t=ET)
        w_kv = part(CH * 2 * D).rearrange("p (c n) -> p c n", c=CH)
        b_k, b_v = part(D), part(CH)
        assert taken[0] == W1
        phase()
        xpad = take([ET, B, LP])
        zT = take([ET * T])
        acc = take([ET, T])
        th = take([ET * T])
        xc = take([ET * T])
        dtT = take([T])
        bcT = take([T], rows=2 * DS)
        delta = take([ET, T])
        u = take([ET, T])
        aneg = take([ET, DS])
        dA = take([2, ET, T])
        dbx = take([2, ET, T])
        hst = take([2, ET * T])
        hc = take([2, ET, T])
        bc = take([2, 2, T])
        w2_at = at[0]
        w2 = take([W2])
        cx = take([CT, D])
        cT = take([CH, CK])
        kmx = take([CT * H])
        ksc = take([CT * H])
        krs = take([CT * H])
        vq_at = at[0]
        kb = take([CT, D])
        tq = take([CT * H, HW])
        kq = take([CT * H, HW])
        r1 = take([CT * H, HW])
        k3_at = at[0]
        k3 = take([CT, H, 3, HW], BF16)
        ktc = take([PAIRS, CK], BF16, rows=PR)
        vT = take([CH, KEYS])
        vmx = take([CH, NC + 1])
        vsc = sb("vsc", [P, CH])
        vrs = take([CH])
        phase(vq_at)
        vqb = take([CH, KEYS], BF16)

        w_f1 = w2[:, 0:CH * FF].rearrange("p (c n) -> p c n", c=CH)
        w_f2 = w2[:, CH * FF:CH * FF + FT * D].rearrange("p (c n) -> p c n", c=FT)
        phase()
        hq = take([FT, T])
        aT = take([FT, T])
        assert at[0] <= w2_at

        phase()
        kqs = take([2, KEYS + 2 * T], BF16, rows=PR)
        vss = take([2, KT * 2 * HW], F16)
        sqs = take([2, 8])
        s_at = at[0]
        s_sb = take([2, KEYS])
        p8 = take([2, KEYS * 2], U8)
        ptr = take([4, 1024], F16)
        oall = take([PAIRS, 4, HW])
        zall = take([PAIRS, 4])
        mxs = take([2, 4])
        mx1 = take([2])
        scaled_mx = take([2])
        ln255 = take([1])
        nb = take([2])
        zs = take([2, 2, 4])
        tail_at = at[0]
        qz = take([PAIRS, 2, T], BF16, rows=PR)
        sqa = take([PAIRS, 8])
        hmask = take([2], rows=PR)
        phase(s_at)
        qb = take([B * H, HW])
        qmx = take([B * H])
        qsc = take([B * H])
        qrs = take([B * H])
        q3 = take([B * H, 3, HW], BF16)
        phase(tail_at)
        onrm = take([B, D])
        rz = take([PAIRS * 4])
        onT = take([CH, T])
        q1 = take([D])
        prod = take([2, D])
        s2 = take([2, H])
        m2 = take([H])
        e2 = take([2, H])
        z2 = take([H])
        orow = take([B, D])
        pv2 = take([2, D])
        oaT = take([CH, T])
        lg = take([B, E])
        top = take([B, E])
        te = take([B, 2])
        tz = take([B])
        comb = take([B])
        tg = take([2, T])
        ga = take([2, T])
        hT = take([FT + 1, T])
        assert at[0] <= k3_at
        w3_at = k3_at
        phase(w3_at)
        w_q = take([CH, D])
        b_q = take([D])
        w_p = take([CH, D])
        b_p = take([D])
        w3a = at[0] - w3_at
        w_qkv = take([CH, 3 * D])
        w_ao = take([CH, D])
        w_sg = take([CH, FF + P])
        w_su = take([CH, FF + P])
        w_sd = take([FT + 1, D])
        w_rt = take([CH, E])
        assert at[0] == w3_at + W3, (at[0] - w3_at, W3)
        w3 = arena[:, w3_at:w3_at + W3]

        pe_step = sem("pe_step")
        (WABS, QLAT, WVO, MTR, MLAT, MLA_OUT, DBC, DLIN, MIX_OUT, FF_OUT, Q_PS, Q_TR, ON_TR, X_OUT, QKV,
         OA_TR, SA_OUT, LOGITS) = range(1, 19)
        ld_seg = sem("ld_seg")
        ld_x = sem("ld_x")
        ld_cst = sem("ld_cst")
        ld_segg = sem("ld_segg")
        ld_w0a = sem("ld_w0a")
        ld_w0q = sem("ld_w0q")
        csum = sem("csum")
        ld_cs = [sem(f"ld_cs{k}") for k in range(2)]
        got_rope = [sem(f"got_rope{k}") for k in range(2)]
        ld_w0b = sem("ld_w0b")
        kc_sb = sem("kc_sb")
        st_kv = sem("st_kv")
        ld_kvg = sem("ld_kvg")
        ld_w1 = sem("ld_w1")
        kvm_ready = sem("kvm_ready")
        mla_done = sem("mla_done")
        cx_tr = sem("cx_tr")
        ld_cx = sem("ld_cx")
        dbx_ready = sem("dbx_ready")
        ld_b = [sem(f"ld_b{k}") for k in range(2)]
        hc_made = sem("hc_made")
        ld_c = [sem(f"ld_c{k}") for k in range(2)]
        ld_w2 = sem("ld_w2")
        dt_sb = sem("dt_sb")
        st_bc = sem("st_bc")
        ktc_tr = sem("ktc_tr")
        ld_w3a = sem("ld_w3a")
        vq_ready = sem("vq_ready")
        kt_stored = sem("kt_stored")
        ld_w3b = sem("ld_w3b")
        qz_ready = sem("qz_ready")
        sqa_ready = sem("sqa_ready")
        ld_kqs = [sem(f"ld_kqs{k}") for k in range(2)]
        ld_sqs = [sem(f"ld_sqs{k}") for k in range(2)]
        ld_vss = [sem(f"ld_vss{k}") for k in range(2)]
        vr_sb = sem("vr_sb")
        s_ps = sem("s_ps")
        ptr_used = sem("ptr_used")
        y_ready = sem("y_ready")
        st_out = sem("st_out")
        half = sem("half")
        ln_var = sem("ln_var")
        ln_rstd = sem("ln_rstd")
        idx_ready = sem("idx_ready")
        got_rows = [sem(f"got_rows{k}") for k in range(2)]
        rq_ready = sem("rq_ready")
        qr_sb = sem("qr_sb")
        h_ready = sem("h_ready")
        kq_ready = sem("kq_ready")
        krs_ready = sem("krs_ready")
        tq_ready = sem("tq_ready")
        k_int = sem("k_int")
        u_ready = sem("u_ready")
        hmask_set = sem("hmask_set")
        hmask_ready = sem("hmask_ready")
        ln255_set = sem("ln255_set")
        p8_set = sem("p8_set")
        mx_ready = sem("mx_ready")
        mx_scaled = sem("mx_scaled")
        nb_ready = sem("nb_ready")
        ln_tr = sem("ln_tr")
        ln_cols = sem("ln_cols")
        identb_ready = sem("identb_ready")
        wq_made = sem("wq_made")
        wabs_sb = sem("wabs_sb")
        qlat_sb = sem("qlat_sb")
        kpr = sem("kpr")
        gt_tr = sem("gt_tr")
        gt_sb = sem("gt_sb")
        qpair = sem("qpair")
        qa_sb = sem("qa_sb")
        kt_tr = sem("kt_tr")
        kt_sb = sem("kt_sb")
        wvo_sb = sem("wvo_sb")
        sc_ready = sem("sc_ready")
        sc_exp = sem("sc_exp")
        mtr_sb = sem("mtr_sb")
        pt_tr = sem("pt_tr")
        pt_sb = sem("pt_sb")
        xz = sem("xz")
        xz_sb = sem("xz_sb")
        aneg_ready = sem("aneg_ready")
        v_sb = sem("v_sb")
        ktc_sb = [sem(f"ktc_sb{k}") for k in range(2)]
        v_ps = sem("v_ps")
        cT_sb = sem("cT_sb")
        conv = sem("conv")
        xc_tanh = sem("xc_tanh")
        z_tanh = sem("z_tanh")
        dlin_ps = sem("dlin_ps")
        sp_ln = sem("sp_ln")
        delta_ready = sem("delta_ready")
        dA_ready = sem("dA_ready")
        k_hi = sem("k_hi")
        r1_ready = sem("r1_ready")
        v_round = sem("v_round")
        vsc_ready = sem("vsc_ready")
        ff_q = sem("ff_q")
        ff_a = sem("ff_a")
        vr_tr = sem("vr_tr")
        t_ps = sem("t_ps")
        o_read = sem("o_read")
        p_ready = sem("p_ready")
        ptr_sb = [sem(f"ptr_sb{k}") for k in range(2)]
        on_cols = sem("on_cols")
        q1_sb = sem("q1_sb")
        oa_rows = sem("oa_rows")
        e2_arg = sem("e2_arg")
        e2_ready = sem("e2_ready")
        oa_cols = sem("oa_cols")
        te_arg = sem("te_arg")
        te_ready = sem("te_ready")
        moe_gu = sem("moe_gu")
        moe_h = sem("moe_h")
        moe_t = sem("moe_t")
        dve_chain = sem("dve_chain")
        ln_rows = sem("ln_rows")
        kr_sb = sem("kr_sb")
        kr_ps = sem("kr_ps")
        scored = sem("scored")
        sc_ps = sem("sc_ps")
        probs = sem("probs")
        pv0 = sem("pv0")
        ot_sb = sem("ot_sb")
        xc_ready = sem("xc_ready")
        kb_sb = sem("kb_sb")
        k_ps = sem("k_ps")
        skip = sem("skip")
        hc_used = sem("hc_used")
        k3_ready = sem("k3_ready")
        vmx_made = sem("vmx_made")
        gated = sem("gated")
        mix_add = sem("mix_add")
        ff_h = sem("ff_h")
        vq_clip = sem("vq_clip")
        ff_add = sem("ff_add")
        q3_ready = sem("q3_ready")
        s_read = sem("s_read")
        on_rows = sem("on_rows")
        qkv_used = sem("qkv_used")
        moe_out = sem("moe_out")
        act_chain = sem("act_chain")

        kt_scr = dram("kt_scr", (PR, PAIRS, KEYS), BF16)
        kv_scr = dram("kv_scr", (T, WIN, KVC), F32)
        bc_scr = dram("bc_scr", (DS, 2, T), F32)

        def bank(k, at_, n, row=0, rows=P):
            return ps[row:row + rows, k, at_:at_ + n]

        block = ctx.enter_context(nc.Block())

        @block.sync
        def _(sp):
            sp.dma_start(seg_i[:, :], seg_d).then_inc(ld_seg, 16)
            sp.dma_start(xres[:, :, :], x_d).then_inc(ld_x, 16)
            sp.dma_start(cst[:, :], cst_d).then_inc(ld_cst, 16)
            sp.dma_start(segg_i[:, :], segrep_d).then_inc(ld_segg, 16)
            sp.dma_start(w0a[:, :], w0a_d).then_inc(ld_w0a, 16)
            sp.dma_start(w0q[:, :], w0q_d).then_inc(ld_w0q, 16)

            def chunk(c):
                if c >= 2:
                    sp.wait_ge(csum, adds(c - 2))
                sp.dma_start(cs[:, c % 2], ctx_d[c * CK:(c + 1) * CK, :].rearrange("(p t) d -> p t d", t=CT))\
                  .then_inc(ld_cs[c % 2], 16)

            sp.wait_ge(pe_step, WABS)
            sp.wait_ge(got_rope[1], 16)
            chunk(0)
            chunk(1)
            sp.dma_start(w0b[:, :], w0b_d).then_inc(ld_w0b, 16)
            for b in range(B):
                sp.wait_ge(kc_sb, 3 * b + 3)
                sp.dma_start(kv_scr[b * L:(b + 1) * L, :, :], krow[:, b, :, 0:KVC]).then_inc(st_kv, 16)
                chunk(2 * b + 2)
                chunk(2 * b + 3)
            sp.wait_ge(st_kv, 32)
            for j in range(WIN):
                sp.dma_start(kvg[j * GQ:(j + 1) * GQ, :, :], kv_scr[:, j, :].rearrange("(g i) k -> i g k", i=GQ))\
                  .then_inc(ld_kvg, 16)
            chunk(6)
            chunk(7)
            sp.dma_start(w1[:, :], w1_d).then_inc(ld_w1, 16)
            sp.wait_ge(kvm_ready, 1)
            sp.dma_start(kvg[GK:GK1, :, :], kvm[:, :, :]).then_inc(ld_kvg, 16)

            sp.wait_ge(mla_done, 1)

            def context(i, key0):
                sp.wait_ge(cx_tr, i + 1)
                sp.dma_start(cx[:, :, :], ctx_d[bass.ds(key0, CK), :].rearrange("(p t) d -> p t d", t=CT)).then_inc(ld_cx, 16)

            def inputs(i, states):
                for s in range(2):
                    sp.wait_ge(dbx_ready, 2 * i + s + 1)
                    sp.dma_start(bc[:, s, 0], bc_scr[bass.ds(states[s], 1), 0, :].partition_broadcast(P)
                                 .rearrange("p o t -> p (o t)")).then_inc(ld_b[s], 16)
                for s in range(2):
                    sp.wait_ge(hc_made, 2 * i + s + 1)
                    sp.dma_start(bc[:, s, 1], bc_scr[bass.ds(states[s], 1), 1, :].partition_broadcast(P)
                                 .rearrange("p o t -> p (o t)")).then_inc(ld_c[s], 16)

            context(0, 0)
            sp.dma_start(w2[:, :], w2_d).then_inc(ld_w2, 16)
            sp.wait_ge(dt_sb, 2)
            sp.dma_start(bc_scr.rearrange("s a t -> a s t"), bcT[0:2 * DS, :]).then_inc(st_bc, 16)
            sp.wait_ge(st_bc, 16)
            with sp.Fori(0, NC - 1) as i:
                key0, states = sp.snap(i * CK + CK), [sp.snap(2 * i + s) for s in range(2)]
                inputs(i, states)
                context(i + 1, key0)
            inputs(NC - 1, [2 * (NC - 1) + s for s in range(2)])
            sp.wait_ge(ktc_tr, 4 * NC + 1)
            sp.dma_start(w3[:, 0:w3a], w3_d[:, 0:w3a]).then_inc(ld_w3a, 16)
            sp.wait_ge(vq_ready, 4)
            sp.wait_ge(kt_stored, 16 * NC + 16)
            sp.dma_start(w3[:, w3a:W3], w3_d[:, w3a:W3]).then_inc(ld_w3b, 16)

            sp.wait_ge(qz_ready, 2)
            sp.wait_ge(sqa_ready, 1)

            def pair(it, kk, n):
                sp.dma_start(kqs[:, kk, 0:KEYS], kt_scr[:, bass.ds(n, 1), :].rearrange("r o k -> r (o k)")).then_inc(ld_kqs[kk], 16)
                sp.dma_start(kqs[:, kk, KEYS:KEYS + 2 * T], qz[:, bass.ds(n, 1), :, :].rearrange("r o h t -> r (o h t)"))\
                  .then_inc(ld_kqs[kk], 16)

            def pair_values(it, kk, n):
                sp.dma_start(sqs[:, kk, :], sqa[:, bass.ds(n, 1), :].rearrange("q o n -> q (o n)")).then_inc(ld_sqs[kk], 16)
                sp.dma_start(vss[:, kk, :], vrow[:, bass.ds(n, 1), :].rearrange("k o n -> k (o n)")).then_inc(ld_vss[kk], 16)

            for kk in range(2):
                pair(0, kk, kk)
            sp.wait_ge(vr_sb, 8)
            for kk in range(2):
                pair_values(0, kk, kk)
            with sp.Fori(0, 3) as it:
                nxt = [sp.snap(2 * it + 2 + kk) for kk in range(2)]
                for kk in range(2):
                    sp.wait_ge(s_ps, 4 * (8 * it + 4 * kk + 4))
                    pair(it, kk, nxt[kk])
                    sp.wait_ge(ptr_used, 4 * (8 * it + 4 * kk + 4) + 4)
                    pair_values(it, kk, nxt[kk])
            sp.wait_ge(y_ready, 2)
            sp.dma_start(out_d, xres[:, :, :]).then_inc(st_out, 16)
            sp.wait_ge(st_out, 16)

        @block.gpsimd
        def _(pool):
            pool.memset(neghalf[:, :], -0.5).then_inc(half, 1)
            pool.wait_ge(half, 1)

            def root(k):
                pool.wait_ge(ln_var, k + 1)
                pool.tensor_tensor(ln_rs[:, :], ln_ve[:, :], neghalf[:, :], ALU.pow).then_inc(ln_rstd, 1)

            root(0)
            pool.wait_ge(idx_ready, 1)
            for b in range(B):
                pool.indirect_dma_start(grow[:, b, :], None, ctx_d, bass.IndirectOffsetOnAxis(ap=idx[:, b:b + 1], axis=0))\
                    .then_inc(got_rows[b], 16)
            for b in range(B):
                pool.indirect_dma_start(rrow[:, b, :], None, rope_d, bass.IndirectOffsetOnAxis(ap=idx[:, B + b:B + b + 1], axis=0))\
                    .then_inc(got_rope[b], 16)
            for b in range(B):
                pool.wait_ge(got_rows[b], 16)
                pool.wait_ge(got_rope[b], 16)
            for p in range(PAIRS):
                pool.wait_ge(rq_ready, p + 1)
                r = rq[R:2 * R, p % 2]
                pool.tensor_tensor(qT[R:2 * R, :, 2 * p:2 * p + 2, :], r[:, 0].rearrange("p o (g i) -> p g o i", i=GQ),
                                   r[:, 1].rearrange("p o (g i) -> p g o i", i=GQ), ALU.add).then_inc(qr_sb, 1)
            pool.wait_ge(qr_sb, PAIRS)
            for c in range(NC):
                b, k = c * B // NC, c % (NC // B)
                pool.wait_ge(ld_cs[c % 2], 16 * (c // 2 + 1))
                if k == 0:
                    continue
                if k > 1:
                    pool.wait_ge(csum, adds(c) - 1)
                pool.tensor_tensor(csums[:, b], cs[:, 0] if k == 1 else csums[:, b], cs[:, c % 2], ALU.add).then_inc(csum, 1)
            root(1)


            def input_of(i, s):
                pool.wait_ge(ld_b[s], 16 * i + 16)
                pool.wait_ge(h_ready, 2 * i + s + 1)
                pool.tensor_tensor(dbx[:, s], u[:, :, :], bc[:, s, 0, :].unsqueeze(1).broadcast_to([P, ET, T]), ALU.mult)\
                    .then_inc(dbx_ready, 1)

            pool.nop().then_inc(dbx_ready, 2)
            pool.nop().then_inc(kq_ready, 1)
            wide = [P, CT * H, HW]

            def scaled(i):
                pool.wait_ge(krs_ready, i + 1)
                pool.tensor_tensor(tq[:, :, :], kb.rearrange("p t (h d) -> p (t h) d", h=H),
                                   krs.unsqueeze(2).broadcast_to(wide), ALU.mult).then_inc(tq_ready, 1)

            def quantised(i):
                pool.wait_ge(k_int, i + 1)
                pool.tensor_tensor(kq[:, :, :], tq[:, :, :], ksc.unsqueeze(2).broadcast_to(wide), ALU.mult).then_inc(kq_ready, 1)

            scaled(0)
            pool.wait_ge(u_ready, 1)
            input_of(0, 0)
            input_of(0, 1)
            with pool.Fori(0, NC - 1) as i:
                input_of(i + 1, 0)
                quantised(i)
                input_of(i + 1, 1)
                scaled(i + 1)
            quantised(NC - 1)
            root(2)
            root(3)
            pool.wait_ge(pe_step, FF_OUT)
            pool.memset(hmask[0:PR, :], 1.0).then_inc(hmask_set, 1)
            pool.wait_ge(hmask_set, 1)
            pool.affine_select(out=hmask[0:PR, 0:1], in_=hmask[0:PR, 0:1], compare_op=ALU.is_ge, fill=0.0, base=PR // 2 - 1,
                               pattern=[[0, 1]], channel_multiplier=-1).then_inc(hmask_set, 1)
            pool.affine_select(out=hmask[0:PR, 1:2], in_=hmask[0:PR, 1:2], compare_op=ALU.is_ge, fill=0.0, base=-(PR // 2),
                               pattern=[[0, 1]], channel_multiplier=1).then_inc(hmask_set, 1)
            pool.wait_ge(hmask_set, 3)
            pool.nop().then_inc(hmask_ready, 1)
            pool.memset(ln255[:, :], LN255).then_inc(ln255_set, 1)
            pool.wait_ge(ln255_set, 1)
            pool.memset(p8.rearrange("p a n -> p (a n)").bitcast(F16), 1024.0).then_inc(p8_set, 1)
            def exponent(it, j):
                u, kk = 8 * it + j, j // 4
                if j % 4 == 0:
                    pool.wait_ge(ld_sqs[kk], 16 * it + 16)
                pool.wait_ge(mx_ready, u + 1)
                pool.tensor_tensor(scaled_mx[:, j % 2:j % 2 + 1], mx1[:, j % 2:j % 2 + 1], sqs[:, kk, 4 + j % 4:5 + j % 4], ALU.mult)\
                    .then_inc(mx_scaled, 1)
                pool.wait_ge(mx_scaled, u + 1)
                pool.tensor_tensor(nb[:, j % 2:j % 2 + 1], scaled_mx[:, j % 2:j % 2 + 1], ln255[:, 0:1], ALU.add).then_inc(nb_ready, 1)

            with pool.Fori(0, UNITS // 8) as it:
                for j in range(8):
                    exponent(it, j)
            root(4)
            root(5)

        @block.scalar
        def _(act):
            link = Chain(act, act_chain)

            def columns(k):
                act.wait_ge(ln_tr, k + 1)
                act.activation(xnT.rearrange("p c t -> p (c t)"), bank(7, 0, 512), ACT.Copy).then_inc(ln_cols, 1)

            act.wait_ge(ld_cst, 16)
            act.activation(identb[:, :], ident, ACT.Copy).then_inc(identb_ready, 1)
            act.wait_ge(ld_w0q, 16)
            act.activation(w_qall[0:QC, :, KVC:2 * KVC], w_qr[0:QC, :, :], ACT.Copy).then_inc(wq_made, 1)
            half = R // 2
            for k in range(2):
                act.activation(w_qrs[0:QC, :, k * half:(k + 1) * half], w_qr[0:QC, :, (1 - k) * half:(2 - k) * half], ACT.Copy)\
                   .then_inc(wq_made, 1)
            act.wait_ge(pe_step, WABS)
            for n in range(2):
                act.activation(w_qall[0:QC, 8 * n:8 * n + 8, 0:KVC],
                               bank(n, 0, 512, 0, QC).rearrange("p (h k) -> p h k", h=8), ACT.Copy).then_inc(wabs_sb, 1)
            act.activation(w_kcat[:, :, KVC:2 * KVC], bank(2, 0, CH * R).rearrange("p (c r) -> p c r", c=CH), ACT.Copy)\
               .then_inc(wabs_sb, 1)
            columns(0)
            act.wait_ge(pe_step, QLAT)
            act.activation(q_cT[0:QC, :], bank(7, 0, T, 0, QC), ACT.Copy).then_inc(qlat_sb, 1)

            def window_columns(b, f):
                if b == 1 and f == 0:
                    act.wait_ge(kpr, 3)
                act.wait_ge(gt_tr, 5 * b + f + 1)
                nj = 2 if f < 4 else 1
                act.activation(gT.rearrange("p c j q -> p j c q")[:, 2 * f:2 * f + nj],
                               bank(4 + (5 * b + f) % 2, 0, nj * 2 * P).rearrange("p (j c q) -> p j c q", j=nj, c=CH), ACT.Copy)\
                   .then_inc(gt_sb, 1)

            for p in range(PAIRS):
                act.wait_ge(qpair, p + 1)
                act.activation(qT[0:KVC, :, 2 * p:2 * p + 2, :],
                               bank(p % 2, 0, 512, 0, KVC).rearrange("p (o g i) -> p g o i", o=2, i=GQ),
                               ACT.Copy).then_inc(qa_sb, 1)
                if p >= 3:
                    window_columns(0, p - 3)
            for b in range(B):
                if b == 1:
                    for f in range(5):
                        window_columns(1, f)
                for f in range(3):
                    n = 3 * b + f
                    act.wait_ge(kpr, n + 1)
                    act.activation(krow[:, b, 3 * f:3 * f + 3, 0:KVC],
                                   bank(6 + n % 2, 0, 3 * P).rearrange("p (j k) -> p j k", j=3)[:, :, 0:KVC], ACT.Copy)\
                       .then_inc(kc_sb, 1)
            for n in range(6):
                act.wait_ge(kt_tr, n + 1)
                act.activation(kcat[:, n // 3, 3 * (n % 3):3 * (n % 3) + 3, :],
                               bank(4 + n % 2, 0, 3 * P).rearrange("p (j k) -> p j k", j=3), ACT.Copy).then_inc(kt_sb, 1)
            act.wait_ge(pe_step, WVO)
            for n in range(4):
                act.activation(w_vo[:, 2 * n:2 * n + 2, :], bank(3 + n, 0, 512).rearrange("p (a n) -> p a n", a=2), ACT.Copy)\
                   .then_inc(wvo_sb, 1)
            for b in range(B):
                act.wait_ge(sc_ready, b + 1)
                act.activation(sc[:, b * GB:(b + 1) * GB, :], sc[:, b * GB:(b + 1) * GB, :], ACT.Exp, scale=MLA_SCALE)\
                   .then_inc(sc_exp, 1)
            act.wait_ge(pe_step, MTR)
            act.activation(mT[:, :], bank(7, 8, B * CH), ACT.Copy, scale=1.0 / NKEY).then_inc(mtr_sb, 1)
            act.wait_ge(pe_step, MLAT)
            act.activation(kvm.rearrange("p (b g) k -> p b g k", b=B),
                           bank(7, 64, B * KVC, 0, 1).rearrange("p (b k) -> p b k", b=B).unsqueeze(2)
                           .broadcast_to([1, B, GB, KVC]), ACT.Copy).then_inc(kvm_ready, 1)
            for n in range(8):
                act.wait_ge(pt_tr, n + 1)
                act.activation(pT[0:GK1, 4 * n:4 * n + 4, :], bank(2 + n % 2, 0, 512, 0, GK1)
                               .rearrange("p (g r) -> p g r", g=4), ACT.Copy).then_inc(pt_sb, 1)

            columns(1)
            for m in range(4):
                act.wait_ge(xz, m + 1)
                if m < 2:
                    act.activation(xpad[:, 2 * m:2 * m + 2, :, DC - 1:LP], bank(m, 0, 512)
                                   .rearrange("p (t b l) -> p t b l", t=2, b=B), ACT.Copy).then_inc(xz_sb, 1)
                else:
                    act.activation(zT[:, (m - 2) * 512:(m - 1) * 512], bank(m, 0, 512), ACT.Copy).then_inc(xz_sb, 1)
            act.wait_ge(ld_w1, 16)
            link(act.activation(aneg[:, :, :], a_log, ACT.Exp))
            act.activation(aneg[:, :, :], aneg[:, :, :], ACT.Copy, scale=-1.0).then_inc(aneg_ready, 1)
            act.nop().then_inc(v_sb, 2)
            act.nop().then_inc(ktc_sb[0], 1)
            act.nop().then_inc(kt_stored, 16)

            def context_columns(i):
                act.wait_ge(cx_tr, i + 2)
                act.wait_ge(v_ps, 2 * i + 2)
                for c in range(CH):
                    act.activation(cT[:, c, :], bank(c, 0, CK), ACT.Copy).then_inc(cT_sb, 1)

            context_columns(0)
            act.wait_ge(conv, 1)
            act.activation(th[:, :], acc.rearrange("p t n -> p (t n)"), ACT.Tanh, scale=0.5).then_inc(xc_tanh, 1)
            act.activation(hst[:, 0, :], zT[:, :], ACT.Tanh, scale=0.5).then_inc(z_tanh, 1)
            act.wait_ge(pe_step, DBC)
            act.activation(dtT[:, :], bank(4, 0, T), ACT.Copy).then_inc(dt_sb, 1)
            act.activation(bcT[0:2 * DS, :], bank(4, T, T, 0, 2 * DS), ACT.Copy).then_inc(dt_sb, 1)
            act.wait_ge(dlin_ps, 1)
            link(act.activation(th[:, :], acc.rearrange("p t n -> p (t n)"), ACT.Abs))
            link(act.activation(th[:, :], th[:, :], ACT.Exp, scale=-1.0))
            act.activation(th[:, :], th[:, :], ACT.Ln, bias=1.0).then_inc(sp_ln, 1)
            act.wait_ge(aneg_ready, 1)
            act.wait_ge(delta_ready, 1)

            def decay(i, s):
                act.wait_ge(h_ready, 2 * i + s + 1)
                for t in range(ET):
                    ins = act.activation(dA[:, s, t, :].rearrange("p (b l) -> p b l", b=B)[:, :, 1:L],
                                         delta[:, t, :].rearrange("p (b l) -> p b l", b=B)[:, :, 1:L], ACT.Exp,
                                         scale=aneg[:, t, bass.ds(2 * i + s, 1)])
                ins.then_inc(dA_ready, 1)


            def values_of(i):
                for m in range(CH):
                    act.wait_ge(v_ps, 2 * i + m + 3)
                    act.activation(vT[:, m, bass.ds(CK * i, CK)], bank(m, 0, CK), ACT.Identity, bias=b_v[:, m:m + 1])\
                       .then_inc(v_sb, 1)

            def first_part(i):
                act.wait_ge(kq_ready, i + 2)
                act.wait_ge(ktc_tr, 4 * i + 1)
                act.activation(k3.rearrange("k t h a d -> k (t h) a d")[:, :, 0, :], kq[:, :, :], ACT.Copy).then_inc(k_hi, 1)

            def second_part(i):
                act.wait_ge(r1_ready, i + 1)
                act.activation(k3.rearrange("k t h a d -> k (t h) a d")[:, :, 1, :], r1[:, :, :], ACT.Copy).then_inc(k_hi, 1)

            def key_columns(i):
                for n in (0, 2):
                    act.wait_ge(ktc_tr, 4 * i + n + 2)
                    if n == 0:
                        act.wait_ge(kt_stored, 16 * i + 16)
                    act.activation(ktc[:, 2 * n:2 * n + 2, :].rearrange("p a k -> p (a k)"),
                                   bank(4 + n % 2, 0, 512, 0, PR).bitcast(BF16), ACT.Copy).then_inc(ktc_sb[0], 1)

            def keys_out(i):
                act.wait_ge(ktc_sb[0], 2 * i + 3)
                act.wait_ge(ktc_sb[1], 2 * i + 3)
                act.dma_start(kt_scr[:, :, bass.ds(i * CK, CK)], ktc[:, :, :]).then_inc(kt_stored, 16)

            decay(0, 0)
            decay(0, 1)
            values_of(0)
            with act.Fori(0, NC - 1) as i:
                decay(i + 1, 0)
                context_columns(i + 1)
                first_part(i)
                decay(i + 1, 1)
                second_part(i)
                key_columns(i)
                values_of(i + 1)
                keys_out(i)

            def rounded(n):
                v = vT[:, n // 2, (n % 2) * KEYS // 2:(n % 2 + 1) * KEYS // 2]
                act.activation(v, v, ACT.Identity, bias=cst[:, 529:530], scale=vrs[:, n // 2:n // 2 + 1]).then_inc(v_round, 1)

            first_part(NC - 1)
            second_part(NC - 1)
            act.wait_ge(vsc_ready, 1)
            rounded(0)
            key_columns(NC - 1)
            rounded(1)

            columns(2)
            keys_out(NC - 1)
            rounded(2)
            rounded(3)
            for n in range(4):
                act.wait_ge(ff_q, n + 1)
                act.activation(aT[:, 2 * n:2 * n + 2, :], hq[:, 2 * n:2 * n + 2, :], ACT.Gelu_apprx_tanh, scale=0.1)\
                   .then_inc(ff_a, 1)

            columns(3)
            for n in range(8):
                m, q = n // 4, n % 4
                act.wait_ge(vr_tr, n + 1)
                act.activation(vrow.rearrange("k p (t n) -> k t p n", n=2 * HW)[:, 8 * q:8 * q + 8, 4 * m:4 * m + 4, :],
                               bank(5 + n % 2, 0, 512).bitcast(BF16).rearrange("k (t p n) -> k t p n", t=8, p=4), ACT.Copy)\
                   .then_inc(vr_sb, 1)

            def probabilities(it, j, half):
                u, kk = 8 * it + j, j // 4
                if half == 0:
                    act.wait_ge(nb_ready, u + 1)
                    act.wait_ge(t_ps, 4 * u + 4)
                    if j % 4 == 0:
                        act.wait_ge(ld_sqs[kk], 16 * it + 16)
                        act.wait_ge(o_read, 2 * it + j // 4 + 1)
                keys = slice(half * KEYS // 2, (half + 1) * KEYS // 2)
                out8 = p8[:, j % 2, half * KEYS:(half + 1) * KEYS].rearrange("q (n w a e) -> q n a w e", w=P, a=2, e=2)
                act.activation(out8[:, :, :, :, 0], s_sb[:, j % 2, keys].rearrange("q (n a w) -> q n a w", a=2, w=P), ACT.Exp,
                               bias=nb[:, j % 2:j % 2 + 1], scale=sqs[:, kk, j % 4:j % 4 + 1],
                               accum_out=zs[:, kk, half, j % 4:j % 4 + 1]).then_inc(p_ready, 1)

            def columns16(it, j, c):
                u = 8 * it + j
                act.wait_ge(t_ps, 4 * u + c + 9)
                act.wait_ge(ptr_used, 4 * u + c + 1)
                act.activation(ptr[:, c, :], bank((4, 5, 6, 5)[c], 0, 512).bitcast(F16), ACT.Copy, bias=-1024.0)\
                   .then_inc(ptr_sb[1], 1)

            def turn(it, j, ahead=True):
                for half in range(2):
                    if ahead:
                        probabilities(*unit(it, j + 1), half)
                    columns16(*unit(it, j), 2 * half + 1)

            act.nop().then_inc(ptr_sb[1], 2)
            act.nop().then_inc(p_ready, 4)
            act.wait_ge(p8_set, 1)
            for half in range(2):
                probabilities(0, 0, half)
            turn(0, 0)
            with act.Fori(0, UNITS // 8 - 1) as it:
                for j in range(1, 9):
                    turn(it, j)
            for j in range(1, 8):
                turn(UNITS // 8 - 1, j, ahead=j < 7)
            act.wait_ge(pe_step, ON_TR)
            for c in range(CH):
                act.activation(onT[:, c, :], bank(4, c * T, T), ACT.Copy, scale=vsc[:, c:c + 1]).then_inc(on_cols, 1)

            columns(4)
            act.wait_ge(pe_step, QKV)
            act.activation(q1[:, :], bank(2, 0, D), ACT.Copy, scale=HW ** -0.5).then_inc(q1_sb, 1)
            act.activation(orow[:, 0, :], bank(0, D, D), ACT.Copy).then_inc(oa_rows, 1)
            act.wait_ge(e2_arg, 1)
            act.activation(e2[:, :, :], s2[:, :, :], ACT.Exp).then_inc(e2_ready, 1)
            act.wait_ge(pe_step, OA_TR)
            act.activation(oaT.rearrange("p c t -> p (c t)"), bank(3, 0, 512), ACT.Copy).then_inc(oa_cols, 1)

            columns(5)
            act.wait_ge(te_arg, 1)
            act.activation(te[:, :, :], te[:, :, :], ACT.Exp).then_inc(te_ready, 1)
            for m in range(FT + 1):
                act.wait_ge(moe_gu, m + 1)
                if m >= 2:
                    act.wait_ge(moe_h, m - 1)
                act.activation(tg[:, m % 2, :], bank(m % 4, 0, T), ACT.Tanh, scale=0.5).then_inc(moe_t, 1)

        @block.vector
        def _(dve):
            link = Chain(dve, dve_chain)

            def normalise(k):
                for b in range(B):
                    dve.bn_stats(ln_st[:, b, :], xres[:, b, :]).then_inc(dve_chain, 1)
                    link.n += 1
                dve.wait_ge(dve_chain, link.n)
                for b in range(B):
                    dve.bn_aggr(ln_mv[:, b, :], ln_st[:, b, :]).then_inc(dve_chain, 1)
                    link.n += 1
                dve.wait_ge(dve_chain, link.n)
                dve.tensor_scalar(ln_ve[:, :], ln_mv[:, :, 1], EPS, None, ALU.add).then_inc(ln_var, 1)
                dve.wait_ge(ln_rstd, k + 1)
                for b in range(B):
                    dve.tensor_scalar(xn[:, b, :], xres[:, b, :], ln_mv[:, b, 0:1], ln_rs[:, b:b + 1], ALU.subtract, ALU.mult)\
                       .then_inc(ln_rows, 1)

            dve.wait_ge(ld_x, 16)
            normalise(0)
            dve.wait_ge(ld_seg, 16)
            link(dve.tensor_copy(segf[:, :], seg_i[:, :]))
            link(dve.tensor_scalar(base[:, :], segf[:, :], float(-LOOKBACK), float(NKEY - WIN), ALU.add, ALU.min))
            link(dve.tensor_scalar(base[:, :], base[:, :], 0.0, None, ALU.max))
            dve.tensor_copy(idx[:, B:2 * B], base[:, :])
            for b in range(B):
                ins = dve.tensor_scalar(idx[:, b:b + 1], base[:, b:b + 1], float(b * NKEY), None, ALU.add)
            ins.then_inc(idx_ready, 1)
            dve.wait_ge(ld_segg, 16)
            dve.wait_ge(ld_cst, 16)
            link(dve.tensor_copy(segh[:, :], segg_i[:, :]))
            link(dve.tensor_scalar(low[:, :], segh[:, :], float(-LOOKBACK), None, ALU.add))
            link(dve.tensor_scalar(baseg[:, :], low[:, :], float(NKEY - WIN), 0.0, ALU.min, ALU.max))
            wide = [P, NG, WIN]
            link(dve.tensor_tensor(kid, baseg.unsqueeze(2).broadcast_to(wide), jidx.unsqueeze(1).broadcast_to(wide), ALU.add))
            link(dve.tensor_tensor(ge, kid, low.unsqueeze(2).broadcast_to(wide), ALU.is_ge))
            link(dve.tensor_tensor(kid, kid, segh.unsqueeze(2).broadcast_to(wide), ALU.is_le))
            link(dve.tensor_tensor(ge, ge, kid, ALU.mult))
            link(dve.tensor_reduce(anyg[:, :], ge, AX.X, ALU.max))
            dve.tensor_scalar(mask[:, :, GK:GK1].rearrange("p g o -> p (g o)"), anyg[:, :], NEG, None, ALU.mult)
            link(dve.tensor_scalar(ge, ge, -1.0, -NEG, ALU.add, ALU.mult))
            full = [P, NG, WIN, GQ]
            link(dve.tensor_tensor(mask[:, :, 0:GK].rearrange("p g (j i) -> p g j i", j=WIN),
                                   ge.unsqueeze(3).broadcast_to(full),
                                   negdiag.unsqueeze(1).unsqueeze(1).broadcast_to(full), ALU.add))
            dve.tensor_copy(sc[:, :, GK:GK1], mask[:, :, GK:GK1])
            for p in range(PAIRS):
                dve.wait_ge(qpair, p + 1)
                four = [R, 2, B, L]
                cosb = qcos[R:2 * R, :].unsqueeze(1).unsqueeze(1).broadcast_to(four)
                sinb = qsin[R:2 * R, :].unsqueeze(1).unsqueeze(1).broadcast_to(four)
                r = rq[R:2 * R, p % 2]
                if p >= 2:
                    dve.wait_ge(qr_sb, p - 1)
                split = "p (o b l) -> p o b l"
                dve.tensor_tensor(r[:, 0].rearrange("p o (b l) -> p o b l", b=B),
                                  bank(p % 2, 0, 512, R, R).rearrange(split, o=2, b=B), cosb, ALU.mult)
                dve.tensor_tensor(r[:, 1].rearrange("p o (b l) -> p o b l", b=B),
                                  bank(2 + p % 2, 0, 512, R, R).rearrange(split, o=2, b=B), sinb, ALU.mult).then_inc(rq_ready, 1)
            for n in range(6):
                b, f = n // 3, n % 3
                if f == 0:
                    dve.wait_ge(got_rope[b], 16)
                dve.wait_ge(kc_sb, n + 1)
                if n >= 2:
                    dve.wait_ge(kr_sb, n - 1)
                r = rk[:, n % 2]
                raw = bank(6 + n % 2, 0, 3 * P).rearrange("p (j k) -> p j k", j=3)[:, :, KVC:2 * KVC]
                cs_ = rrow[:, b, :].rearrange("p (j k) -> p j k", j=WIN)[:, 3 * f:3 * f + 3, :]
                dve.tensor_tensor(r[:, 0], raw, cs_[:, :, 0:R], ALU.mult)
                dve.tensor_tensor(r[:, 1, :, 0:R // 2], raw[:, :, R // 2:R], cs_[:, :, R:R + R // 2], ALU.mult)
                ins = dve.tensor_tensor(r[:, 1, :, R // 2:R], raw[:, :, 0:R // 2], cs_[:, :, R + R // 2:2 * R], ALU.mult)
                ins.then_inc(kr_ps, 1)
                dve.wait_ge(kr_ps, n + 1)
                dve.tensor_tensor(krow[:, b, 3 * f:3 * f + 3, KVC:2 * KVC], r[:, 0], r[:, 1], ALU.add).then_inc(kr_sb, 1)
            for n in range(8):
                dve.wait_ge(scored, n + 1)
                dve.tensor_tensor(sc[:, 4 * n:4 * n + 4, 0:GK], bank(n % 2, 0, 4 * GK).rearrange("p (g k) -> p g k", g=4),
                                  mask[:, 4 * n:4 * n + 4, 0:GK], ALU.add).then_inc(sc_ps, 1)
                if n % 4 == 3:
                    b = n // 4
                    s = sc[:, b * GB:(b + 1) * GB, :]
                    dve.wait_ge(sc_ps, n + 1)
                    link(dve.tensor_reduce(mx[:, b * GB:(b + 1) * GB], s, AX.X, ALU.max))
                    dve.tensor_tensor(s, s, mx[:, b * GB:(b + 1) * GB].unsqueeze(2).broadcast_to([P, GB, GK1]), ALU.subtract)\
                       .then_inc(sc_ready, 1)
            for b in range(B):
                s, m = sc[:, b * GB:(b + 1) * GB, :], mx[:, b * GB:(b + 1) * GB]
                dve.wait_ge(sc_exp, b + 1)
                link(dve.tensor_reduce(m, s, AX.X, ALU.add))
                link(dve.reciprocal(m, m))
                dve.tensor_tensor(s, s, m.unsqueeze(2).broadcast_to([P, GB, GK1]), ALU.mult).then_inc(probs, 1)
            for n in range(4):
                dve.wait_ge(pv0, n + 1)
                dve.tensor_copy(oT.rearrange("k p (g i) -> k g p i", i=GQ)[:, 8 * n:8 * n + 8],
                                bank(4 + n % 2, 0, 512).rearrange("k (g p i) -> k g p i", g=8, p=PAIRS)).then_inc(ot_sb, 1)
            dve.wait_ge(pe_step, MLA_OUT)
            dve.tensor_tensor(xres[:, :, :], bank(0, 0, 512).rearrange("p (b d) -> p b d", b=B), xres[:, :, :], ALU.add)\
               .then_inc(mla_done, 1)
            dve.wait_ge(mla_done, 1)

            normalise(1)
            link(dve.memset(xpad[:, :, :, 0:DC - 1], 0.0))
            dve.memset(dA[:, :, :, :], 0.0)
            dve.wait_ge(ld_w1, 16)
            for k in range(DC):
                for t in range(ET):
                    if k == 0 and t % 2 == 0:
                        dve.wait_ge(xz_sb, t // 2 + 1)
                    a, src = acc[:, t, :].rearrange("p (b l) -> p b l", b=B), xpad[:, t, :, k:k + L]
                    if k == 0:
                        ins = dve.tensor_scalar(a, src, conv_w[:, t, 0:1], conv_b[:, t:t + 1], ALU.mult, ALU.add)
                    else:
                        ins = dve.scalar_tensor_tensor(out=a, in0=src, scalar=conv_w[:, t, k:k + 1], in1=a,
                                                       op0=ALU.mult, op1=ALU.add)
                if k < DC - 1:
                    link(ins)
            ins.then_inc(conv, 1)
            acc_f = acc.rearrange("p t n -> p (t n)")
            dve.wait_ge(xc_tanh, 1)
            link(dve.scalar_tensor_tensor(out=xc[:, :], in0=th[:, :], scalar=1.0, in1=acc_f, op0=ALU.add, op1=ALU.mult))
            dve.tensor_scalar(xc[:, :], xc[:, :], 0.5, None, ALU.mult).then_inc(xc_ready, 1)
            dve.wait_ge(xc_ready, 1)
            tq_f = tq.rearrange("p a b -> p (a b)")
            dve.nop().then_inc(h_ready, 2)
            dve.nop().then_inc(hc_made, 2)
            dve.nop().then_inc(kb_sb, 2)
            dve.nop().then_inc(ktc_sb[1], 1)

            def scale_of(i):
                dve.wait_ge(kq_ready, i + 1)
                for n in range(2):
                    dve.wait_ge(k_ps, 2 * i + n + 1)
                    dve.tensor_tensor(kb[:, 2 * n:2 * n + 2, :], bank(2 + n, 0, 512).rearrange("p (t d) -> p t d", t=2),
                                      b_k.unsqueeze(1).broadcast_to([P, 2, D]), ALU.add).then_inc(kb_sb, 1)
                dve.wait_ge(kb_sb, 2 * i + 4)
                link(dve.tensor_reduce(kmx[:, :], kb.rearrange("p t (h d) -> p (t h) d", h=H), AX.X, ALU.max,
                                       apply_absolute_value=True))
                link(dve.tensor_scalar(ksc[:, :], kmx[:, :], 1.0 / QMAX, 1e-8, ALU.mult, ALU.max))
                dve.reciprocal(krs[:, :], ksc[:, :]).then_inc(krs_ready, 1)

            scale_of(0)
            dve.wait_ge(z_tanh, 1)
            link(dve.scalar_tensor_tensor(out=zT[:, :], in0=hst[:, 0, :], scalar=1.0, in1=zT[:, :], op0=ALU.add, op1=ALU.mult))
            dve.wait_ge(pe_step, DLIN)
            for t in range(ET):
                ins = dve.tensor_scalar(acc[:, t, :], bank(5 + t // 2, (t % 2) * T, T), b_dt[:, t:t + 1], None, ALU.add)
            ins.then_inc(dlin_ps, 1)
            dve.wait_ge(sp_ln, 1)
            delta_f, u_f = delta.rearrange("p t n -> p (t n)"), u.rearrange("p t n -> p (t n)")
            dve.scalar_tensor_tensor(out=delta_f, in0=acc_f, scalar=0.0, in1=th[:, :], op0=ALU.max, op1=ALU.add)\
               .then_inc(delta_ready, 1)
            dve.wait_ge(delta_ready, 1)
            dve.tensor_tensor(u_f, delta_f, xc[:, :], ALU.mult).then_inc(u_ready, 1)
            for t in range(ET):
                ins = dve.tensor_scalar(acc_f[:, t * T:(t + 1) * T], xc[:, t * T:(t + 1) * T], dskip[:, t:t + 1], None, ALU.mult)
            ins.then_inc(skip, 1)

            def state(i, s):
                dve.wait_ge(dA_ready, 2 * i + s + 1)
                dve.wait_ge(dbx_ready, 2 * i + s + 3)
                dve.tensor_tensor_scan(hst[:, s, :], dA[:, s].rearrange("p t n -> p (t n)"),
                                       dbx[:, s].rearrange("p t n -> p (t n)"), 0.0, ALU.mult, ALU.add).then_inc(h_ready, 1)
                dve.wait_ge(h_ready, 2 * i + s + 3)
                dve.wait_ge(hc_used, 2 * i + s + 1)
                dve.wait_ge(ld_c[s], 16 * i + 16)
                dve.tensor_tensor(hc[:, s], hst[:, s, :].rearrange("p (t n) -> p t n", t=ET),
                                  bc[:, s, 1, :].unsqueeze(1).broadcast_to([P, ET, T]), ALU.mult).then_inc(hc_made, 1)

            k3v = k3.rearrange("k t h a d -> k (t h) a d")

            def integers(i):
                dve.wait_ge(tq_ready, i + 1)
                link(dve.tensor_scalar(tq_f, tq_f, MAGIC, MAGIC + QMAX, ALU.add, ALU.min))
                dve.tensor_scalar(tq_f, tq_f, MAGIC - QMAX, MAGIC, ALU.max, ALU.subtract).then_inc(k_int, 1)

            def second_part(i):
                dve.wait_ge(k_hi, 2 * i + 1)
                dve.tensor_tensor(r1[:, :, :], kq[:, :, :], k3v[:, :, 0, :], ALU.subtract).then_inc(r1_ready, 1)

            def third_part(i):
                dve.wait_ge(r1_ready, i + 1)
                dve.wait_ge(k_hi, 2 * i + 2)
                dve.tensor_tensor(k3v[:, :, 2, :], r1[:, :, :], k3v[:, :, 1, :], ALU.subtract).then_inc(k3_ready, 1)

            def largest(i):
                dve.wait_ge(v_sb, 2 * i + 4)
                dve.tensor_reduce(vmx[:, :, bass.ds(i, 1)], vT[:, :, bass.ds(CK * i, CK)], AX.X, ALU.max,
                                  apply_absolute_value=True).then_inc(vmx_made, 1)

            def key_columns(i):
                for n in (1, 3):
                    dve.wait_ge(ktc_tr, 4 * i + n + 2)
                    if n == 1:
                        dve.wait_ge(kt_stored, 16 * i + 16)
                    dve.tensor_copy(ktc[:, 2 * n:2 * n + 2, :].rearrange("p a k -> p (a k)"),
                                    bank(4 + n % 2, 0, 512, 0, PR).bitcast(BF16)).then_inc(ktc_sb[1], 1)

            state(0, 0)
            start = link.n
            with dve.Fori(0, NC - 1) as i:
                link.n, link.off = start, KV_LINKS * i
                integers(i)
                state(i, 1)
                second_part(i)
                third_part(i)
                largest(i)
                scale_of(i + 1)
                key_columns(i)
                state(i + 1, 0)
            assert link.n == start + KV_LINKS
            link.n, link.off = start + KV_LINKS * (NC - 1), 0
            integers(NC - 1)
            state(NC - 1, 1)
            largest(NC - 1)
            dve.wait_ge(vmx_made, NC)
            link(dve.tensor_reduce(vmx[:, :, NC:NC + 1], vmx[:, :, 0:NC], AX.X, ALU.max))
            link(dve.tensor_scalar(vsc[:, :], vmx[:, :, NC], 1.0 / QMAX, 1e-8, ALU.mult, ALU.max))
            dve.reciprocal(vrs[:, :], vsc[:, :]).then_inc(vsc_ready, 1)
            second_part(NC - 1)
            dve.wait_ge(hc_used, 2 * NC + 2)
            for n in range(2):
                ins = dve.scalar_tensor_tensor(out=acc_f[:, n * 512:(n + 1) * 512], in0=bank(6 + n, 0, 512), scalar=0.5,
                                               in1=zT[:, n * 512:(n + 1) * 512], op0=ALU.mult, op1=ALU.mult)
            ins.then_inc(gated, 1)
            third_part(NC - 1)
            dve.wait_ge(pe_step, MIX_OUT)
            dve.tensor_tensor(xres[:, :, :], bank(2, 0, 512).rearrange("p (b d) -> p b d", b=B), xres[:, :, :], ALU.add)\
               .then_inc(mix_add, 1)
            dve.wait_ge(mix_add, 1)

            def integer_values(n):
                half = slice((n % 2) * KEYS // 2, (n % 2 + 1) * KEYS // 2)
                dve.wait_ge(v_round, n + 1)
                dve.tensor_scalar(vqb[:, n // 2, half], vT[:, n // 2, half], MAGIC, QMAX, ALU.subtract, ALU.min).then_inc(vq_ready, 1)

            normalise(2)
            key_columns(NC - 1)
            for n in range(4):
                integer_values(n)
                h2 = hq[:, 2 * n:2 * n + 2, :].rearrange("p m t -> p (m t)")
                dve.wait_ge(ff_h, n + 1)
                link(dve.tensor_scalar(h2, bank(n, 0, 512), 10.0, 32767.0, ALU.mult, ALU.min))
                link(dve.tensor_scalar(h2, h2, -32768.0, MAGIC, ALU.max, ALU.add))
                dve.tensor_scalar(h2, h2, MAGIC, None, ALU.subtract).then_inc(ff_q, 1)
            dve.wait_ge(vq_ready, 4)
            for m in range(CH):
                dve.tensor_scalar(vqb[:, m, :], vqb[:, m, :], -QMAX, None, ALU.max).then_inc(vq_clip, 1)
            dve.wait_ge(pe_step, FF_OUT)
            dve.tensor_tensor(xres[:, :, :], bank(4, 0, 512).rearrange("p (b d) -> p b d", b=B), xres[:, :, :], ALU.add)\
               .then_inc(ff_add, 1)
            dve.wait_ge(ff_add, 1)

            normalise(3)
            dve.wait_ge(ld_w3a, 16)
            dve.wait_ge(pe_step, Q_PS)
            link(dve.tensor_tensor(qb.rearrange("p (b h) d -> p b (h d)", b=B), bank(0, 0, 512).rearrange("p (b d) -> p b d", b=B),
                                   b_q.unsqueeze(1).broadcast_to([P, B, D]), ALU.add))
            link(dve.tensor_reduce(qmx[:, :], qb, AX.X, ALU.max, apply_absolute_value=True))
            link(dve.tensor_scalar(qsc[:, :], qmx[:, :], HW ** -0.5 / QMAX, 1e-8, ALU.mult, ALU.max))
            link(dve.reciprocal(qrs[:, :], qsc[:, :]))
            link(dve.scalar_tensor_tensor(out=qb, in0=qb, scalar=HW ** -0.5, in1=qrs.unsqueeze(2).broadcast_to([P, B * H, HW]),
                                          op0=ALU.mult, op1=ALU.mult))
            link(dve.tensor_scalar(qb, qb, MAGIC, MAGIC + QMAX, ALU.add, ALU.min))
            dve.tensor_scalar(q3, qb.unsqueeze(2).broadcast_to([P, B * H, 3, HW]), MAGIC - QMAX, MAGIC, ALU.max, ALU.subtract)\
               .then_inc(q3_ready, 1)
            for sgn, o in ((1.0, 0), (-1.0, 4)):
                ins = dve.tensor_scalar(sqa[:, :, o:o + 4].rearrange("q p (o b) -> q p o b", o=2),
                                        qsc.rearrange("q (b p o) -> q p o b", b=B, o=2), sgn, None, ALU.mult)
            ins.then_inc(sqa_ready, 1)
            dve.wait_ge(pe_step, Q_TR)
            dve.wait_ge(hmask_ready, 1)
            for o in range(2):
                dve.tensor_scalar(qz[:, :, o, :].rearrange("r p (b q) -> r b p q", b=B),
                                  ps[0:PR, 1:3, :].rearrange("r b n -> r (b n)").bitcast(BF16)
                                  .rearrange("r (b p q) -> r b p q", b=B, q=P),
                                  hmask[0:PR, o:o + 1], None, ALU.mult).then_inc(qz_ready, 1)
            link(dve.tensor_tensor(xres[:, :, :], xres[:, :, :], b_p.unsqueeze(1).broadcast_to([P, B, D]), ALU.add))
            dve.nop().then_inc(ptr_sb[0], 2)
            dve.nop().then_inc(s_read, 2)
            dve.nop().then_inc(o_read, 2)

            def maxima(it, j, c):
                u = 8 * it + j
                if c == 0:
                    dve.wait_ge(p_ready, 2 * u + 2)
                dve.wait_ge(s_ps, 4 * u + c + 1)
                dve.tensor_scalar(s_sb[:, j % 2, c * 1024:(c + 1) * 1024], ps[:, 2 * (c % 2):2 * (c % 2) + 2, :]
                                  .rearrange("p a n -> p (a n)"), 1.0, None, ALU.mult, ALU.max,
                                  accum_out=mxs[:, j % 2, c:c + 1]).then_inc(s_read, 1)
                if c == 3:
                    dve.wait_ge(s_read, 4 * u + 6)
                    dve.tensor_reduce(mx1[:, j % 2:j % 2 + 1], mxs[:, j % 2, :], AX.X, ALU.max).then_inc(mx_ready, 1)

            def columns16(it, j, c):
                u = 8 * it + j
                dve.wait_ge(t_ps, 4 * u + c + 9)
                dve.wait_ge(ptr_used, 4 * u + c + 1)
                dve.tensor_scalar(ptr[:, c, :], bank((4, 5, 6, 5)[c], 0, 512).bitcast(F16), -1024.0, None, ALU.add)\
                   .then_inc(ptr_sb[0], 1)

            def sums(it, g):
                n = 2 * it + g
                dve.wait_ge(ptr_used, 4 * (8 * it + 4 * g + 4) + 4)
                dve.tensor_tensor(zall[:, bass.ds(n, 1), :].rearrange("q o u -> q (o u)"), zs[:, g, 0, :], zs[:, g, 1, :], ALU.add)
                dve.tensor_copy(oall[:, bass.ds(n, 1), :, :].rearrange("q o u d -> q (o u d)"), bank(7, 0, 4 * HW)).then_inc(o_read, 1)

            def turn(it, j, ahead=True):
                for c in range(4):
                    if ahead:
                        maxima(*unit(it, j + 2), c)
                    if c % 2 == 0:
                        columns16(*unit(it, j), c)
                    if c == 1 and j % 4 == 0 and j:
                        sums(it, j // 4 - 1)

            for j in range(2):
                for c in range(4):
                    maxima(0, j, c)
            turn(0, 0)
            with dve.Fori(0, UNITS // 8 - 1) as it:
                for j in range(1, 9):
                    turn(it, j)
            for j in range(1, 8):
                turn(UNITS // 8 - 1, j, ahead=j < 6)
            sums(UNITS // 8 - 1, 1)
            dve.wait_ge(o_read, 2 + PAIRS)
            link(dve.reciprocal(rz[:, :], zall.rearrange("q p u -> q (p u)")))
            for b in range(B):
                ins = dve.tensor_tensor(onrm[:, b, :].rearrange("q (p o d) -> q p o d", p=PAIRS, o=2),
                                        oall.rearrange("q p (o b) d -> q b p o d", b=B)[:, b],
                                        rz.rearrange("q (p o b) -> q b p o", o=2, b=B)[:, b].unsqueeze(3)
                                        .broadcast_to([P, PAIRS, 2, HW]), ALU.mult)
            ins.then_inc(on_rows, 1)
            dve.wait_ge(pe_step, X_OUT)
            link(dve.tensor_tensor(xres[:, :, :], bank(5, 0, 512).rearrange("p (b d) -> p b d", b=B), xres[:, :, :], ALU.add))

            normalise(4)
            dve.wait_ge(oa_rows, 1)
            dve.tensor_tensor(prod[:, 0, :], bank(0, 0, D), q1[:, :], ALU.mult)
            link(dve.tensor_tensor(prod[:, 1, :], bank(1, 0, D), q1[:, :], ALU.mult))
            link(dve.tensor_reduce(s2[:, :, :].rearrange("p m h -> p (m h)"), prod.rearrange("p m (h d) -> p (m h) d", d=HW),
                                   AX.X, ALU.add))
            link(dve.tensor_tensor(m2[:, :], s2[:, 0, :], s2[:, 1, :], ALU.max))
            dve.tensor_tensor(s2[:, :, :], s2[:, :, :], m2.unsqueeze(1).broadcast_to([P, 2, H]), ALU.subtract).then_inc(e2_arg, 1)
            dve.wait_ge(e2_ready, 1)
            link(dve.tensor_tensor(z2[:, :], e2[:, 0, :], e2[:, 1, :], ALU.add))
            link(dve.reciprocal(z2[:, :], z2[:, :]))
            link(dve.tensor_tensor(e2[:, :, :], e2[:, :, :], z2.unsqueeze(1).broadcast_to([P, 2, H]), ALU.mult))
            for m in range(2):
                ins = dve.tensor_tensor(pv2[:, m, :].rearrange("p (h d) -> p h d", d=HW),
                                        bank(m, D, D).rearrange("p (h d) -> p h d", d=HW),
                                        e2[:, m, :].unsqueeze(2).broadcast_to([P, H, HW]), ALU.mult)
            link(ins)
            dve.nop().then_inc(qkv_used, 1)
            dve.tensor_tensor(orow[:, 1, :], pv2[:, 0, :], pv2[:, 1, :], ALU.add).then_inc(oa_rows, 1)
            dve.wait_ge(pe_step, SA_OUT)
            link(dve.tensor_tensor(xres[:, :, :], bank(4, 0, 512).rearrange("p (b d) -> p b d", b=B), xres[:, :, :], ALU.add))

            normalise(5)
            dve.wait_ge(pe_step, LOGITS)
            for b in range(B):
                ins = dve.max(top[:, b, :], bank(7, b * E, E))
            link(ins)
            dve.tensor_tensor(te[:, :, :], top[:, :, 0:2], top[:, :, 0:1].broadcast_to([P, B, 2]), ALU.subtract).then_inc(te_arg, 1)
            dve.wait_ge(te_ready, 1)
            link(dve.tensor_tensor(tz[:, :], te[:, :, 0], te[:, :, 1], ALU.add))
            link(dve.reciprocal(tz[:, :], tz[:, :]))
            link(dve.tensor_tensor(te[:, :, :], te[:, :, :], tz.unsqueeze(2).broadcast_to([P, B, 2]), ALU.mult))
            link(dve.tensor_tensor(comb[:, :], te[:, :, 0], te[:, :, 1], ALU.add))
            for m in range(FT + 1):
                dve.wait_ge(moe_t, m + 1)
                link(dve.scalar_tensor_tensor(out=ga[:, m % 2, :], in0=tg[:, m % 2, :], scalar=1.0, in1=bank(m % 4, 0, T),
                                              op0=ALU.add, op1=ALU.mult))
                dve.scalar_tensor_tensor(out=hT[:, m, :], in0=ga[:, m % 2, :], scalar=0.5, in1=bank(m % 4, T, T),
                                         op0=ALU.mult, op1=ALU.mult).then_inc(moe_h, 1)
            dve.wait_ge(moe_out, 1)
            link(dve.tensor_tensor(xres[:, :, :], bank(5, 0, 512).rearrange("p (b d) -> p b d", b=B), xres[:, :, :], ALU.add))
            dve.wait_ge(moe_out, 2)
            for b in range(B):
                dve.scalar_tensor_tensor(out=xres[:, b, :], in0=bank(6, b * D, D), scalar=comb[:, b:b + 1], in1=xres[:, b, :],
                                         op0=ALU.mult, op1=ALU.add).then_inc(y_ready, 1)

        @block.tensor
        def _(pe):
            def columns(k):
                pe.wait_ge(ln_rows, 2 * (k + 1))
                for c in range(CH):
                    for b in range(B):
                        mm = pe.transpose(bank(7, c * T + b * L, P), xn[:, b, c * P:(c + 1) * P], ident)
                mm.then_inc(ln_tr, 1)

            pe.wait_ge(ld_cst, 16)
            pe.wait_ge(ld_w0a, 16)
            for h in range(H):
                pe.matmul(bank(h // 8, (h % 8) * KVC, KVC, 0, QC), w_uqT[:, h, :], w_ukT[:, h, :], start=True, stop=True)
            for c in range(CH):
                mm = pe.matmul(bank(2, c * R, R), w_kvcT[0:KVC, c * P:(c + 1) * P], w_kr[0:KVC, :], start=True, stop=True)
            mm.then_inc(pe_step, 1)
            columns(0)
            pe.wait_ge(ld_w0q, 16)
            pe.wait_ge(ln_cols, 1)
            for c in range(CH):
                mm = pe.matmul(bank(7, 0, T, 0, QC), w_dq[:, c, :], xnT[:, c, :], start=(c == 0), stop=(c == CH - 1))
            mm.then_inc(pe_step, 1)

            def window_columns(b, f):
                if f == 0:
                    pe.wait_ge(got_rows[b], 16)
                n = 5 * b + f
                if n >= 2:
                    pe.wait_ge(gt_sb, n - 1)
                for j in range(2 * f, min(2 * f + 2, WIN)):
                    for c in range(CH):
                        mm = pe.transpose(bank(4 + n % 2, ((j % 2) * CH + c) * P, P), grow[:, b, j * D + c * P:j * D + (c + 1) * P],
                                          ident)
                mm.then_inc(gt_tr, 1)

            pe.wait_ge(qlat_sb, 1)
            pe.wait_ge(wq_made, 3)
            pe.wait_ge(wabs_sb, 3)
            for p in range(PAIRS):
                if p >= 2:
                    pe.wait_ge(qa_sb, p - 1)
                    pe.wait_ge(rq_ready, p - 1)
                for o in range(2):
                    pe.matmul(bank(p % 2, o * T, T), w_qall[0:QC, 2 * p + o, :], q_cT[0:QC, :], start=True, stop=True)
                for o in range(2):
                    mm = pe.matmul(bank(2 + p % 2, o * T, T, R, R), w_qrs[0:QC, 2 * p + o, :], q_cT[0:QC, :],
                                   start=True, stop=True)
                mm.then_inc(qpair, 1)
                if p >= 3:
                    window_columns(0, p - 3)
            for b in range(B):
                if b == 1:
                    for f in range(5):
                        window_columns(1, f)
                pe.wait_ge(gt_sb, 5 * b + 5)
                for f in range(3):
                    n = 3 * b + f
                    if n >= 2:
                        pe.wait_ge(kc_sb, n - 1)
                        pe.wait_ge(kr_ps, n - 1)
                    for j in range(3):
                        for c in range(CH):
                            mm = pe.matmul(bank(6 + n % 2, j * P, P), gT[:, c, 3 * f + j, :], w_kcat[:, c, :],
                                           start=(c == 0), stop=(c == CH - 1))
                    mm.then_inc(kpr, 1)
            for n in range(6):
                b, f = n // 3, n % 3
                pe.wait_ge(kc_sb, n + 1)
                pe.wait_ge(kr_sb, n + 1)
                pe.wait_ge(gt_sb, 10) if n < 2 else pe.wait_ge(kt_sb, n - 1)
                for j in range(3):
                    mm = pe.transpose(bank(4 + n % 2, j * P, P), krow[:, b, 3 * f + j, :], ident)
                mm.then_inc(kt_tr, 1)
            pe.wait_ge(qa_sb, PAIRS)
            pe.wait_ge(qr_sb, PAIRS)
            for n in range(8):
                pe.wait_ge(kt_sb, 3 if n < 4 else 6)
                if n >= 2:
                    pe.wait_ge(sc_ps, n - 1)
                for i in range(4):
                    g = 4 * n + i
                    q, b = g * GQ, g // GB
                    mm = pe.matmul(bank(n % 2, i * GK, GK), qT[:, g].rearrange("k h i -> k (h i)"), kcat[:, b, :, q % L:q % L + GQ],
                                   start=True, stop=True)
                mm.then_inc(scored, 1)
            pe.wait_ge(ld_w0b, 16)
            pe.wait_ge(kt_sb, 6)
            pe.wait_ge(kr_ps, 6)
            for p in range(PAIRS):
                for o in range(2):
                    mm = pe.matmul(bank(3 + p // 2, (p % 2) * D, D, o * KVC, KVC), w_uvT[:, 2 * p + o, :], w_o[:, 2 * p + o, :],
                                   start=True, stop=True)
            mm.then_inc(pe_step, 1)
            pe.wait_ge(csum, adds(NC - 1))
            for b in range(B):
                for c in range(CH):
                    for t in range(CT):
                        mm = pe.matmul(bank(7, 8 + CH * b + c, 1), csums[:, b, t, c * P:(c + 1) * P], ones[:, 0:1],
                                       start=(t == 0), stop=(t == CT - 1))
            mm.then_inc(pe_step, 1)
            pe.wait_ge(mtr_sb, 1)
            for b in range(B):
                for c in range(CH):
                    mm = pe.matmul(bank(7, 64 + KVC * b, KVC, 0, 1), mT[:, CH * b + c:CH * b + c + 1], w_kcat[:, c, 0:KVC],
                                   start=(c == 0), stop=(c == CH - 1))
            mm.then_inc(pe_step, 1)
            for n in range(8):
                pe.wait_ge(probs, 1 if n < 4 else 2)
                if n < 2:
                    pe.wait_ge(wvo_sb, 4)
                else:
                    pe.wait_ge(pt_sb, n - 1)
                for i in range(4):
                    mm = pe.transpose(bank(2 + n % 2, i * P, P, 0, GK1), sc[:, 4 * n + i, :], ident)
                mm.then_inc(pt_tr, 1)
            pe.wait_ge(ld_kvg, 16 * (WIN + 1))
            for n in range(4):
                pe.wait_ge(pt_sb, 2 * n + 2)
                if n >= 2:
                    pe.wait_ge(ot_sb, n - 1)
                for i in range(8):
                    g = 8 * n + i
                    for o in range(2):
                        pr = pT[0:GK1, g, :].rearrange("k (p o i) -> k o p i", o=2, i=GQ)[:, o]
                        mm = pe.matmul(bank(4 + n % 2, i * 64, 64, o * KVC, KVC), kvg[0:GK1, g, :], pr, start=True, stop=True)
                mm.then_inc(pv0, 1)
            pe.wait_ge(ot_sb, 4)
            pe.wait_ge(wvo_sb, 4)
            for b in range(B):
                for p in range(PAIRS):
                    mm = pe.matmul(bank(0, b * D, D), oT[:, p, b * L:(b + 1) * L], w_vo[:, p, :],
                                   start=(p == 0), stop=(p == PAIRS - 1))
            mm.then_inc(pe_step, 1)

            columns(1)
            pe.wait_ge(ld_w1, 16)
            pe.wait_ge(ln_cols, 2)
            for m in range(2 * ET):
                for c in range(CH):
                    mm = pe.matmul(bank(m // 2, (m % 2) * T, T), w_in[:, c, m * P:(m + 1) * P], xnT[:, c, :],
                                   start=(c == 0), stop=(c == CH - 1))
                if m % 2:
                    mm.then_inc(xz, 1)
            pe.nop().then_inc(cx_tr, 1)
            pe.nop().then_inc(v_ps, 2)
            pe.nop().then_inc(ktc_tr, 1)
            pe.nop().then_inc(hc_used, 2)

            def turned(i):
                pe.wait_ge(ld_cx, 16 * i + 16)
                pe.wait_ge(v_sb, 2 * i + 2)
                for t in range(CT):
                    for c in range(CH):
                        mm = pe.transpose(bank(c, t * P, P), cx[:, t, c * P:(c + 1) * P], ident)
                mm.then_inc(cx_tr, 1)

            def keys(i):
                pe.wait_ge(cT_sb, 2 * i + 2)
                pe.wait_ge(kb_sb, 2 * i + 2)
                for t in range(CT):
                    for c in range(CH):
                        mm = pe.matmul(bank(2 + t // 2, (t % 2) * D, D), cT[:, c, t * P:(t + 1) * P], w_kv[:, c, 0:D],
                                       start=(c == 0), stop=(c == CH - 1))
                    if t % 2:
                        mm.then_inc(k_ps, 1)

            def values_of(i, m):
                for c in range(CH):
                    mm = pe.matmul(bank(m, 0, CK), w_kv[:, c, D + m * P:D + (m + 1) * P], cT[:, c, :],
                                   start=(c == 0), stop=(c == CH - 1))
                mm.then_inc(v_ps, 1)

            pe.wait_ge(xz_sb, 4)
            turned(0)
            keys(0)
            pe.wait_ge(xc_ready, 1)
            for c in range(ET):
                pe.matmul(bank(4, 0, T), w_x[:, c, 0:DR], xc[:, c * T:(c + 1) * T], start=(c == 0), stop=(c == ET - 1))
            for c in range(ET):
                mm = pe.matmul(bank(4, T, T, 0, 2 * DS), w_x[:, c, DR:DR + 2 * DS], xc[:, c * T:(c + 1) * T],
                               start=(c == 0), stop=(c == ET - 1))
            mm.then_inc(pe_step, 1)
            pe.wait_ge(dt_sb, 1)
            for t in range(ET):
                mm = pe.matmul(bank(5 + t // 2, (t % 2) * T, T), w_dt[:, t * P:(t + 1) * P], dtT[:, :], start=True, stop=True)
            mm.then_inc(pe_step, 1)
            values_of(0, 0)
            values_of(0, 1)
            pe.wait_ge(skip, 1)
            for n in range(2):
                pe.matmul(bank(6 + n, 0, 512), ident, acc.rearrange("p t n -> p (t n)")[:, n * 512:(n + 1) * 512],
                          start=True, stop=True)
            pe.wait_ge(dt_sb, 2)

            def state(i, s):
                pe.wait_ge(hc_made, 2 * i + s + 3)
                for n in range(2):
                    mm = pe.matmul(bank(6 + n, 0, 512), ident, hc[:, s].rearrange("p t n -> p (t n)")[:, n * 512:(n + 1) * 512],
                                   start=False, stop=True, skip_group_check=True)
                mm.then_inc(hc_used, 1)

            def key_columns(i, half):
                pe.wait_ge(k3_ready, i + 1)
                for n in (2 * half, 2 * half + 1):
                    pe.wait_ge(ktc_sb[n % 2], 2 * i + n // 2 + 1)
                    for o in range(2):
                        p = 2 * n + o
                        for t in range(CT):
                            dst = bank(4 + n % 2, 0, 512, 0, PR).bitcast(BF16)[:, (o * CT + t) * P:(o * CT + t + 1) * P]
                            mm = pe.transpose(dst, k3[:, t, 2 * p:2 * p + 2].rearrange("k h a d -> k (h a d)"), identb[:, :])
                    mm.then_inc(ktc_tr, 1)

            with pe.Fori(0, NC - 1) as i:
                turned(i + 1)
                state(i, 0)
                keys(i + 1)
                key_columns(i, 0)
                values_of(i + 1, 0)
                key_columns(i, 1)
                values_of(i + 1, 1)
                state(i, 1)
            state(NC - 1, 0)
            state(NC - 1, 1)
            pe.wait_ge(gated, 1)
            pe.wait_ge(kb_sb, 2 * NC + 2)
            for b in range(B):
                for t in range(ET):
                    mm = pe.matmul(bank(2, b * D, D), acc[:, t, b * L:(b + 1) * L], w_out[:, t, :],
                                   start=(t == 0), stop=(t == ET - 1))
            mm.then_inc(pe_step, 1)
            key_columns(NC - 1, 0)
            key_columns(NC - 1, 1)

            columns(2)
            pe.wait_ge(ln_cols, 3)
            pe.wait_ge(ld_w2, 16)
            pe.wait_ge(v_sb, 2 * NC + 2)
            pe.wait_ge(mix_add, 1)
            for m in range(FT):
                for c in range(CH):
                    mm = pe.matmul(bank(m // 2, (m % 2) * T, T), w_f1[:, c, m * P:(m + 1) * P], xnT[:, c, :],
                                   start=(c == 0), stop=(c == CH - 1))
                if m % 2:
                    mm.then_inc(ff_h, 1)
            pe.wait_ge(ff_a, 4)
            pe.wait_ge(ktc_sb[0], 2 * NC + 1)
            for b in range(B):
                for m in range(FT):
                    mm = pe.matmul(bank(4, b * D, D), aT[:, m, b * L:(b + 1) * L], w_f2[:, m, :],
                                   start=(m == 0), stop=(m == FT - 1))
            mm.then_inc(pe_step, 1)

            columns(3)
            pe.wait_ge(ln_cols, 4)
            pe.wait_ge(ld_w3a, 16)
            for b in range(B):
                for c in range(CH):
                    mm = pe.matmul(bank(0, b * D, D), xnT[:, c, b * L:(b + 1) * L], w_q[:, c, :],
                                   start=(c == 0), stop=(c == CH - 1))
            mm.then_inc(pe_step, 1)
            for n in range(8):
                m, q = n // 4, n % 4
                pe.wait_ge(vq_clip, m + 1)
                if n >= 2:
                    pe.wait_ge(vr_sb, n - 1)
                else:
                    pe.wait_ge(ff_add, 1)
                for t in range(8):
                    k = (8 * q + t) * P
                    mm = pe.transpose(bank(5 + n % 2, 0, 512).bitcast(BF16)[:, t * P:(t + 1) * P], vqb[:, m, k:k + P], identb[:, :])
                mm.then_inc(vr_tr, 1)
            pe.wait_ge(q3_ready, 1)
            for b in range(B):
                for p in range(PAIRS):
                    dst = bank(1 + b, 0, 512, 0, PR).bitcast(BF16)[:, p * P:(p + 1) * P]
                    mm = pe.transpose(dst, q3[:, b * H + 2 * p:b * H + 2 * p + 2].rearrange("q h a d -> q (h a d)"), identb[:, :])
            mm.then_inc(pe_step, 1)
            pe.wait_ge(qz_ready, 2)
            pe.nop().then_inc(ptr_used, 4)
            pe.nop().then_inc(t_ps, 8)

            def scores(it, j, c):
                u, kk = 8 * it + j, j // 4
                if j % 4 == 0 and c == 0:
                    pe.wait_ge(ld_kqs[kk], 32 * it + 32)
                pe.wait_ge(s_read, 4 * u + c + 1)
                q = KEYS + (j // 2 % 2) * T + (j % 2) * L
                for m in range(2):
                    k = c * 1024 + m * 512
                    mm = pe.matmul(bank(2 * (c % 2) + m, 0, 512), kqs[:, kk, q:q + L], kqs[:, kk, k:k + 512],
                                   start=True, stop=True)
                mm.then_inc(s_ps, 1)

            def turned_over(it, j, c):
                u = 8 * it + j
                if c % 2 == 0:
                    pe.wait_ge(p_ready, 2 * u + c // 2 + 5)
                who, count = ((0, 1), (1, 2), (0, 2), (1, 3))[c]
                pe.wait_ge(ptr_sb[who], 2 * u + count)
                words = p8[:, j % 2].bitcast(F32)
                for n in range(4):
                    w = (4 * c + n) * P
                    mm = pe.transpose(bank((4, 5, 6, 5)[c], n * P, P), words[:, w:w + P], ident)
                mm.then_inc(t_ps, 1)

            def weighted(it, j, c):
                u, kk = 8 * it + j, j // 4
                pe.wait_ge(ptr_sb[c % 2], 2 * u + c // 2 + 3)
                if j % 4 == 0 and c == 0:
                    pe.wait_ge(ld_vss[kk], 16 * it + 16)
                    pe.wait_ge(o_read, 2 * it + j // 4 + 2)
                for n in range(4):
                    for par in range(2):
                        t = 2 * (4 * c + n) + par
                        v = t * 2 * HW + (j // 2 % 2) * HW
                        mm = pe.matmul(bank(7, (j % 4) * HW, HW), ptr[:, c, n * 2 * P + par:(n + 1) * 2 * P:2],
                                       vss[:, kk, v:v + HW], start=(t == 0), stop=(t == KT - 1))
                mm.then_inc(ptr_used, 1)

            def turn(it, j, ahead=True):
                for c in range(4):
                    if ahead:
                        scores(*unit(it, j + 2), c)
                    turned_over(*unit(it, j), c)
                    if c >= 2:
                        weighted(*unit(it, j), c - 2)
                    elif j:
                        weighted(*unit(it, j - 1), c + 2)

            for j in range(2):
                for c in range(4):
                    scores(0, j, c)
            pe.wait_ge(vr_sb, 8)
            turn(0, 0)
            with pe.Fori(0, UNITS // 8 - 1) as it:
                for j in range(1, 9):
                    turn(it, j)
            for j in range(1, 8):
                turn(UNITS // 8 - 1, j, ahead=j < 6)
            for c in range(2, 4):
                weighted(UNITS // 8 - 1, 7, c)

            pe.wait_ge(on_rows, 1)
            for c in range(CH):
                for b in range(B):
                    mm = pe.transpose(bank(4, c * T + b * L, P), onrm[:, b, c * P:(c + 1) * P], ident)
            mm.then_inc(pe_step, 1)
            pe.wait_ge(on_cols, CH)
            for b in range(B):
                for c in range(CH):
                    mm = pe.matmul(bank(5, b * D, D), onT[:, c, b * L:(b + 1) * L], w_p[:, c, :],
                                   start=(c == 0), stop=(c == CH - 1))
            mm.then_inc(pe_step, 1)

            columns(4)
            pe.wait_ge(ln_cols, 5)
            pe.wait_ge(ld_w3b, 16)
            for b, n0, bk in ((0, D, 0), (1, D, 1), (1, 0, 2)):
                n1 = 3 * D if n0 else D
                for c in range(CH):
                    mm = pe.matmul(bank(bk, 0, n1 - n0), xnT[:, c, b * L:(b + 1) * L], w_qkv[:, c, n0:n1],
                                   start=(c == 0), stop=(c == CH - 1))
            mm.then_inc(pe_step, 1)
            pe.wait_ge(oa_rows, B)
            for c in range(CH):
                for b in range(B):
                    mm = pe.transpose(bank(3, c * T + b * L, P), orow[:, b, c * P:(c + 1) * P], ident)
            mm.then_inc(pe_step, 1)
            pe.wait_ge(oa_cols, 1)
            for b in range(B):
                for c in range(CH):
                    mm = pe.matmul(bank(4, b * D, D), oaT[:, c, b * L:(b + 1) * L], w_ao[:, c, :],
                                   start=(c == 0), stop=(c == CH - 1))
            mm.then_inc(pe_step, 1)

            columns(5)
            pe.wait_ge(ln_cols, 6)
            pe.wait_ge(qkv_used, 1)
            for b in range(B):
                for c in range(CH):
                    mm = pe.matmul(bank(7, b * E, E), xnT[:, c, b * L:(b + 1) * L], w_rt[:, c, :],
                                   start=(c == 0), stop=(c == CH - 1))
            mm.then_inc(pe_step, 1)
            for m in range(FT + 1):
                if m >= 4:
                    pe.wait_ge(moe_h, m - 3)
                for n, w in ((0, w_sg), (1, w_su)):
                    for c in range(CH):
                        mm = pe.matmul(bank(m % 4, n * T, T), w[:, c, m * P:(m + 1) * P], xnT[:, c, :],
                                       start=(c == 0), stop=(c == CH - 1))
                mm.then_inc(moe_gu, 1)
            pe.wait_ge(moe_h, FT)
            for b in range(B):
                for m in range(FT):
                    mm = pe.matmul(bank(5, b * D, D), hT[:, m, b * L:(b + 1) * L], w_sd[:, m, :],
                                   start=(m == 0), stop=(m == FT - 1))
            mm.then_inc(moe_out, 1)
            pe.wait_ge(moe_h, FT + 1)
            for b in range(B):
                mm = pe.matmul(bank(6, b * D, D), hT[:, FT, b * L:(b + 1) * L], w_sd[:, FT, :], start=True, stop=True)
            mm.then_inc(moe_out, 1)


_CONST = {}


def constants():
    import numpy as np

    half = R // 2
    inv = (1.0 / 10000.0 ** (np.arange(half, dtype=np.float32) / np.float32(half))).astype(np.float32)
    ang = np.arange(NKEY, dtype=np.float32)[:, None] * inv
    cos, sin = np.cos(ang).astype(np.float32), np.sin(ang).astype(np.float32)
    rope = np.concatenate([cos, cos, -sin, sin], 1)
    cst = np.zeros((P, CST), np.float32)
    cst[:, 0:128] = np.eye(P)
    cst[R:, 128:256] = rope[:L, 0:R].T
    cst[R:, 256:384] = rope[:L, R:].T
    cst[:, 384:512] = 1.0
    cst[:, 512:520] = np.where(np.arange(P)[:, None] % GQ == np.arange(GQ), 0.0, NEG)
    cst[:, 520:529] = np.arange(WIN)
    cst[:, 529] = MAGIC
    return cst, rope


def kernel(**inputs):
    import numpy as np
    import concourse.bacc as bacc
    from concourse.bass_utils import run_bass_kernel_spmd

    a = {k: np.asarray(v) for k, v in inputs.items()}

    def rows(w, n=P):
        return w.reshape(-1, n, w.shape[-1]).transpose(1, 0, 2).reshape(n, -1)

    def full(w):
        out = np.zeros((P, w.shape[1]), w.dtype)
        out[:w.shape[0]] = w
        return out

    def over(v):
        return np.broadcast_to(v, (P, v.shape[-1]))

    uq = a["L0_xattn_W_uq"].reshape(QC, H, HD)
    uk = a["L0_xattn_W_uk"].reshape(KVC, H, HD)
    uv = a["L0_xattn_W_uv"].reshape(KVC, H, HD)
    qr = a["L0_xattn_W_qr"].reshape(QC, H, R)
    kvc = rows(a["L0_xattn_W_kvc"]).reshape(P, CH, KVC)
    w0a = np.concatenate([
        uq.transpose(2, 1, 0).reshape(P, -1),
        uk.transpose(2, 1, 0).reshape(P, -1),
        full(a["L0_xattn_W_kvc"].T),
        full(a["L0_xattn_W_kr"]),
    ], 1)
    w0q = np.concatenate([
        rows(a["L0_xattn_W_dq"]),
        np.concatenate([kvc, np.zeros_like(kvc)], 2).reshape(P, -1),
        full(qr.reshape(QC, -1)),
    ], 1)
    w0b = np.concatenate([uv.transpose(2, 1, 0).reshape(P, -1), rows(a["L0_xattn_W_o"])], 1)
    w1 = np.concatenate([
        rows(a["L0_attn_W_in"].T), rows(a["L0_attn_W_x"].T), a["L0_attn_W_dt"].T, rows(a["L0_attn_W_out"].T),
        rows(a["L0_attn_conv_w"]), rows(a["L0_attn_conv_b"][:, None]), rows(a["L0_attn_b_dt"][:, None]),
        rows(a["L0_attn_Dp"][:, None]), rows(a["L0_attn_A_log"]), rows(a["L1_xattn_Wkv"]),
        over(a["L1_xattn_bkv"][:D]), rows(a["L1_xattn_bkv"][D:, None]),
    ], 1)
    w2 = np.concatenate([rows(a["L0_ffn_W1"].T), rows(a["L0_ffn_W2"].T)], 1)

    def beside(s, r):
        return np.concatenate([rows(s).reshape(P, CH, -1), rows(r).reshape(P, CH, -1)], 2).reshape(P, -1)

    w3 = np.concatenate([
        rows(a["L1_xattn_Wq"]), over(a["L1_xattn_bq"]), rows(a["L1_xattn_Wp"]), over(a["L1_xattn_bp"]),
        rows(a["L1_attn_weight_qkv"].T), rows(a["L1_attn_weight_out"].T),
        beside(a["L1_ffn_sh_gate"].T, a["L1_ffn_r_gate"].T), beside(a["L1_ffn_sh_up"].T, a["L1_ffn_r_up"].T),
        rows(a["L1_ffn_sh_down"].T), rows(a["L1_ffn_r_down"].T), rows(a["L1_ffn_router_weight"].T),
    ], 1)
    seg = a["itok_BxS_0_1023"].reshape(NG, GQ)
    cst, rope = constants()
    arrays = {
        "x": a["x"].transpose(1, 0, 2),
        "seg": a["itok_BxS_0_1023"].T,
        "segg": np.broadcast_to(seg.T[None], (H, GQ, NG)).reshape(P, NG),
        "context": a["ctx_2048"].reshape(KEYS, D),
        "rope": rope, "cst": cst, "w0a": w0a, "w0q": w0q, "w0b": w0b, "w1": w1, "w2": w2, "w3": w3,
    }
    arrays = {f"in_{k}": np.ascontiguousarray(v) for k, v in arrays.items()}
    nc = bacc.Bacc("TRN2", target_bir_lowering=False, num_devices=1)
    args = [nc.dram_tensor(k, v.shape, mybir.dt.from_np(v.dtype), kind="ExternalInput").ap() for k, v in arrays.items()]
    out = nc.dram_tensor("out", (P, B, D), F32, kind="ExternalOutput").ap()
    perceiver_kernel(nc, *args, out)
    r = run_bass_kernel_spmd(nc, [arrays], core_ids=[0])
    return np.asarray(r.results[0]["out"]).transpose(1, 0, 2)
```

```python
from contextlib import ExitStack

import concourse.bass as bass
from concourse import mybir

ALU = mybir.AluOpType
ACT = mybir.ActivationFunctionType
AX = mybir.AxisListType
F32 = mybir.dt.float32
BF16 = mybir.dt.bfloat16
F16 = mybir.dt.float16
U8 = mybir.dt.uint8
I32 = mybir.dt.int32

P = 128
B, L, D = 2, 128, 256
T = B * L
CH = D // P
NKEY = 2048
KEYS = B * NKEY
EPS = 1e-5
NEG = -1e30
MAGIC = 12582912.0

H = 16
HD, KVC, QC, R = 128, 64, 96, 64
LOOKBACK = 8
WIN = LOOKBACK + 1
GQ = P // H
NG = T // GQ
GB = NG // B
GK = GQ * WIN
GK1 = GK + 1
MLA_SCALE = float((HD + R) ** -0.5)
DI, DS, DC, DR = 512, 16, 4, 128
ET = DI // P
LP = L + DC - 1
FF = 1024
FT = FF // P
HW = D // H
PAIRS = H // 2
PR = 2 * 3 * HW
CK = 512
CT = CK // P
NC = KEYS // CK
KT = KEYS // P
QMAX = 127.0
LN255 = 5.541263545158426
E = 8
CST = 530
W0A = H * QC + H * KVC + D + R
W0Q = CH * QC + CH * 2 * R + H * R
W0B = H * KVC + H * D
W1 = CH * 2 * DI + ET * (DR + 2 * DS) + DI + ET * D + ET * (DC + 3 + DS) + CH * 2 * D + D + CH
W2 = CH * FF + FT * D
W3 = 2 * (CH * D + D) + CH * 3 * D + CH * D + 2 * CH * (FF + P) + (FT + 1) * D + CH * E
ARENA = 40400
KV_LINKS = 3

UNITS = B * H


def unit(it, j):
    return it + j // 8, j % 8


def adds(c):
    per = NC // B
    return c // per * (per - 1) + max(c % per, 1)


class Chain:

    def __init__(self, engine, semaphore):
        self.engine, self.semaphore, self.n, self.off = engine, semaphore, 0, 0

    def __call__(self, ins):
        self.n += 1
        ins.then_inc(self.semaphore, 1)
        self.engine.wait_ge(self.semaphore, self.off + self.n)


def perceiver_kernel(nc, x_d, seg_d, segrep_d, ctx_d, rope_d, cst_d, w0a_d, w0q_d, w0b_d, w1_d, w2_d, w3_d, out_d):
    with ExitStack() as ctx:
        def sb(name, shape, dt=F32):
            return ctx.enter_context(nc.sbuf_tensor(name, shape, dt))

        def sem(name):
            return ctx.enter_context(nc.semaphore(name))

        def dram(name, shape, dt):
            return nc.dram_tensor(name, shape, dt).ap()

        ps = ctx.enter_context(nc.psum_tensor("ps", [P, 8, 512], F32))

        cst = sb("cst", [P, CST])
        ident, qcos, qsin = cst[:, 0:128], cst[:, 128:256], cst[:, 256:384]
        ones, negdiag, jidx = cst[:, 384:512], cst[:, 512:520], cst[:, 520:529]
        identb = sb("identb", [P, P], BF16)
        xres = sb("xres", [P, B, D])
        xn = sb("xn", [P, B, D])
        xnT = sb("xnT", [P, CH, T])
        ln_st = sb("ln_st", [P, B, 6])
        ln_mv = sb("ln_mv", [P, B, 2])
        ln_ve = sb("ln_ve", [P, B])
        ln_rs = sb("ln_rs", [P, B])
        neghalf = sb("neghalf", [P, B])
        w1 = sb("w1", [P, W1])
        vrow = sb("vrow", [P, PAIRS, KT * 2 * HW], F16)

        arena = sb("arena", [P, ARENA])
        at = [0]

        def phase(start=0):
            at[0] = start

        def take(shape, dt=F32, rows=P):
            n = 1
            for s in shape:
                n *= s
            words = n if dt in (F32, I32) else (n + 1) // 2 if dt in (BF16, F16) else n // 4
            a = arena[0:rows, at[0]:at[0] + words]
            at[0] += words
            assert at[0] <= ARENA, (at[0], ARENA)
            if dt != F32:
                a = a.bitcast(dt)
            if len(shape) > 1:
                names = "abcd"[:len(shape)]
                a = a.rearrange(f"p ({' '.join(names)}) -> p {' '.join(names)}",
                                **{k: s for k, s in zip(names[1:], shape[1:])})
            return a

        early = vrow.rearrange("k p n -> k (p n)").bitcast(F32)
        csums = early[:, 0:B * CT * D].rearrange("k (b t d) -> k b t d", b=B, t=CT)
        w0q = early[:, B * CT * D:B * CT * D + W0Q]
        w_dq = w0q[:, 0:CH * QC].rearrange("p (c n) -> p c n", c=CH)
        w_kcat = w0q[:, CH * QC:CH * (QC + 2 * R)].rearrange("p (c n) -> p c n", c=CH)
        w_qr = w0q[:, CH * (QC + 2 * R):W0Q].rearrange("p (h n) -> p h n", h=H)
        phase()
        w_uqT = take([H, QC])
        w_ukT = take([H, KVC])
        w_kvcT = take([D])
        w_kr = take([R])
        w0a = arena[:, 0:W0A]
        w_qall = take([H, 2 * R])
        w_qrs = take([H, R])
        w0b = take([W0B])
        at[0] -= W0B
        w_uvT = take([H, KVC])
        w_o = take([H, D])
        w_vo = take([PAIRS, D])
        g_at = at[0]
        grow = take([B, WIN * D])
        r_at = at[0]
        rrow = take([B, WIN * 2 * R])
        gT_at = at[0]
        gT = take([CH, WIN, P])
        krow = take([B, WIN, 2 * KVC])
        kcat = take([B, WIN, P])
        qT = take([NG, H, GQ])
        q_cT = take([T])
        rq = take([2, 2, 2, T])
        rk = take([2, 2, 3, R])
        seg_i = take([B], I32)
        segg_i = take([NG], I32)
        segf = take([B])
        base = take([B])
        idx = take([2 * B], I32)
        segh = take([NG])
        low = take([NG])
        baseg = take([NG])
        kid = take([NG, WIN])
        ge = take([NG, WIN])
        anyg = take([NG])
        mask = take([NG, GK1])
        sc = take([NG, GK1])
        mx = take([NG])
        mT = take([B * CH])
        phase(g_at)
        pT = take([NG, P])
        phase(r_at)
        oT = take([PAIRS, T])
        phase(gT_at)
        kvg = take([NG, KVC])
        phase()
        cs = take([2, CT, D])
        phase()
        kvm = take([NG, KVC], rows=1)
        taken = [0]

        def part(n):
            taken[0] += n
            return w1[:, taken[0] - n:taken[0]]

        w_in = part(CH * 2 * DI).rearrange("p (c n) -> p c n", c=CH)
        w_x = part(ET * (DR + 2 * DS)).rearrange("p (c n) -> p c n", c=ET)
        w_dt = part(DI)
        w_out = part(ET * D).rearrange("p (c n) -> p c n", c=ET)
        conv_w = part(ET * DC).rearrange("p (t k) -> p t k", t=ET)
        conv_b, b_dt, dskip = part(ET), part(ET), part(ET)
        a_log = part(ET * DS).rearrange("p (t s) -> p t s", t=ET)
        w_kv = part(CH * 2 * D).rearrange("p (c n) -> p c n", c=CH)
        b_k, b_v = part(D), part(CH)
        assert taken[0] == W1
        phase()
        xpad = take([ET, B, LP])
        zT = take([ET * T])
        acc = take([ET, T])
        th = take([ET * T])
        xc = take([ET * T])
        dtT = take([T])
        bcT = take([T], rows=2 * DS)
        delta = take([ET, T])
        u = take([ET, T])
        aneg = take([ET, DS])
        dA = take([2, ET, T])
        dbx = take([2, ET, T])
        hst = take([2, ET * T])
        hc = take([2, ET, T])
        bc = take([2, 2, T])
        w2_at = at[0]
        w2 = take([W2])
        cx = take([CT, D])
        cT = take([CH, CK])
        kmx = take([CT * H])
        ksc = take([CT * H])
        krs = take([CT * H])
        vq_at = at[0]
        kb = take([CT, D])
        tq = take([CT * H, HW])
        kq = take([CT * H, HW])
        r1 = take([CT * H, HW])
        k3_at = at[0]
        k3 = take([CT, H, 3, HW], BF16)
        ktc = take([PAIRS, CK], BF16, rows=PR)
        vT = take([CH, KEYS])
        vmx = take([CH, NC + 1])
        vsc = sb("vsc", [P, CH])
        vrs = take([CH])
        phase(vq_at)
        vqb = take([CH, KEYS], BF16)

        w_f1 = w2[:, 0:CH * FF].rearrange("p (c n) -> p c n", c=CH)
        w_f2 = w2[:, CH * FF:CH * FF + FT * D].rearrange("p (c n) -> p c n", c=FT)
        phase()
        hq = take([FT, T])
        aT = take([FT, T])
        assert at[0] <= w2_at

        phase()
        kqs = take([2, KEYS + 2 * T], BF16, rows=PR)
        vss = take([2, KT * 2 * HW], F16)
        sqs = take([2, 8])
        s_at = at[0]
        s_sb = take([2, KEYS])
        p8 = take([2, KEYS * 2], U8)
        ptr = take([4, 1024], F16)
        oall = take([PAIRS, 4, HW])
        zall = take([PAIRS, 4])
        mxs = take([2, 4])
        mx1 = take([2])
        scaled_mx = take([2])
        ln255 = take([1])
        nb = take([2])
        zs = take([2, 2, 4])
        tail_at = at[0]
        qz = take([PAIRS, 2, T], BF16, rows=PR)
        sqa = take([PAIRS, 8])
        hmask = take([2], rows=PR)
        phase(s_at)
        qb = take([B * H, HW])
        qmx = take([B * H])
        qsc = take([B * H])
        qrs = take([B * H])
        q3 = take([B * H, 3, HW], BF16)
        phase(tail_at)
        onrm = take([B, D])
        rz = take([PAIRS * 4])
        onT = take([CH, T])
        q1 = take([D])
        prod = take([2, D])
        s2 = take([2, H])
        m2 = take([H])
        e2 = take([2, H])
        z2 = take([H])
        orow = take([B, D])
        pv2 = take([2, D])
        oaT = take([CH, T])
        top = take([B, E])
        te = take([B, 2])
        tz = take([B])
        comb = take([B])
        tg = take([2, T])
        ga = take([2, T])
        hT = take([FT + 1, T])
        assert at[0] <= k3_at
        w3_at = k3_at
        phase(w3_at)
        w_q = take([CH, D])
        b_q = take([D])
        w_p = take([CH, D])
        b_p = take([D])
        w3a = at[0] - w3_at
        w_qkv = take([CH, 3 * D])
        w_ao = take([CH, D])
        w_sg = take([CH, FF + P])
        w_su = take([CH, FF + P])
        w_sd = take([FT + 1, D])
        w_rt = take([CH, E])
        assert at[0] == w3_at + W3, (at[0] - w3_at, W3)
        w3 = arena[:, w3_at:w3_at + W3]

        pe_step = sem("pe_step")
        (WABS, QLAT, MTR, MLAT, MLA_OUT, DLAT, DBC, DLIN, MIX_OUT, FF_OUT, Q_PS, Q_TR, ON_TR, X_OUT, Q_MADE,
         KEYS_MADE, VALUES_MADE, OA_TR, SA_OUT, LOGITS) = range(1, 21)
        ld_seg = sem("ld_seg")
        ld_x = sem("ld_x")
        ld_cst = sem("ld_cst")
        ld_segg = sem("ld_segg")
        ld_w0a = sem("ld_w0a")
        ld_w0q = sem("ld_w0q")
        csum = sem("csum")
        ld_cs = [sem(f"ld_cs{k}") for k in range(2)]
        got_rope = [sem(f"got_rope{k}") for k in range(2)]
        ld_w0b = sem("ld_w0b")
        kc_sb = sem("kc_sb")
        st_kv = sem("st_kv")
        ld_kvg = sem("ld_kvg")
        ld_w1 = sem("ld_w1")
        kvm_ready = sem("kvm_ready")
        mla_done = sem("mla_done")
        cx_tr = sem("cx_tr")
        ld_cx = sem("ld_cx")
        dbx_ready = sem("dbx_ready")
        ld_b = [sem(f"ld_b{k}") for k in range(2)]
        hc_made = sem("hc_made")
        ld_c = [sem(f"ld_c{k}") for k in range(2)]
        ld_w2 = sem("ld_w2")
        dt_sb = sem("dt_sb")
        st_bc = sem("st_bc")
        ktc_tr = sem("ktc_tr")
        ld_w3a = sem("ld_w3a")
        ld_keys = [sem(f"ld_keys{k}") for k in range(2)]
        ld_queries = [sem(f"ld_queries{k}") for k in range(2)]
        ld_sqs = [sem(f"ld_sqs{k}") for k in range(2)]
        ld_vss = [sem(f"ld_vss{k}") for k in range(2)]
        kt_stored = sem("kt_stored")
        sqa_ready = sem("sqa_ready")
        qz_ready = [sem(f"qz_ready{k}") for k in range(2)]
        vr_sb = sem("vr_sb")
        vq_ready = sem("vq_ready")
        ld_w3b = sem("ld_w3b")
        s_ps = sem("s_ps")
        ptr_used = sem("ptr_used")
        y_ready = sem("y_ready")
        st_out = sem("st_out")
        half = sem("half")
        ln_var = sem("ln_var")
        ln_rstd = sem("ln_rstd")
        idx_ready = sem("idx_ready")
        got_rows = [sem(f"got_rows{k}") for k in range(2)]
        rq_ready = sem("rq_ready")
        qr_sb = sem("qr_sb")
        h_ready = sem("h_ready")
        kq_ready = sem("kq_ready")
        krs_ready = sem("krs_ready")
        tq_ready = sem("tq_ready")
        k_int = sem("k_int")
        hc_used = [sem(f"hc_used{k}") for k in range(2)]
        delta_ready = sem("delta_ready")
        u_ready = sem("u_ready")
        hmask_set = sem("hmask_set")
        ln255_set = sem("ln255_set")
        p8_set = sem("p8_set")
        mx_ready = sem("mx_ready")
        mx_scaled = sem("mx_scaled")
        nb_ready = sem("nb_ready")
        ln_tr = sem("ln_tr")
        ln_cols = sem("ln_cols")
        identb_ready = sem("identb_ready")
        wq_made = sem("wq_made")
        wabs_sb = sem("wabs_sb")
        qlat_sb = sem("qlat_sb")
        kpr = sem("kpr")
        gt_tr = sem("gt_tr")
        gt_sb = sem("gt_sb")
        qpair = sem("qpair")
        qa_sb = sem("qa_sb")
        kt_tr = sem("kt_tr")
        kt_sb = sem("kt_sb")
        sc_ready = sem("sc_ready")
        sc_exp = sem("sc_exp")
        wvo = sem("wvo")
        wvo_sb = sem("wvo_sb")
        mtr_sb = sem("mtr_sb")
        pt_tr = sem("pt_tr")
        pt_sb = sem("pt_sb")
        v_sb = sem("v_sb")
        ktc_sb = sem("ktc_sb")
        v_ps = sem("v_ps")
        cT_sb = sem("cT_sb")
        xz = sem("xz")
        xz_sb = sem("xz_sb")
        conv = sem("conv")
        xc_tanh = sem("xc_tanh")
        z_tanh = sem("z_tanh")
        aneg_ready = sem("aneg_ready")
        dlin_abs = sem("dlin_abs")
        sp_ln = sem("sp_ln")
        dA_ready = sem("dA_ready")
        k_hi = sem("k_hi")
        r1_ready = sem("r1_ready")
        v_round = sem("v_round")
        vsc_ready = sem("vsc_ready")
        ff_q = sem("ff_q")
        ff_a = sem("ff_a")
        vr_tr = sem("vr_tr")
        p_ready = sem("p_ready")
        t_ps = sem("t_ps")
        o_read = sem("o_read")
        ptr_sb = [sem(f"ptr_sb{k}") for k in range(2)]
        on_cols = sem("on_cols")
        q1_sb = sem("q1_sb")
        e2_arg = sem("e2_arg")
        e2_ready = sem("e2_ready")
        oa_rows = sem("oa_rows")
        oa_cols = sem("oa_cols")
        te_arg = sem("te_arg")
        te_ready = sem("te_ready")
        moe_gu = sem("moe_gu")
        moe_h = sem("moe_h")
        moe_t = sem("moe_t")
        dve_chain = sem("dve_chain")
        ln_rows = sem("ln_rows")
        kr_sb = sem("kr_sb")
        kr_ps = sem("kr_ps")
        scored = sem("scored")
        sc_ps = sem("sc_ps")
        rsum = sem("rsum")
        probs = sem("probs")
        pv0 = sem("pv0")
        ot_sb = sem("ot_sb")
        kb_sb = sem("kb_sb")
        xc_ready = sem("xc_ready")
        k_ps = sem("k_ps")
        skip = sem("skip")
        k3_ready = sem("k3_ready")
        vmx_made = sem("vmx_made")
        gated = sem("gated")
        mix_add = sem("mix_add")
        ff_h = sem("ff_h")
        vq_clip = sem("vq_clip")
        ff_add = sem("ff_add")
        q3_ready = sem("q3_ready")
        s_read = sem("s_read")
        on_rows = sem("on_rows")
        qkv_used = sem("qkv_used")
        moe_out = sem("moe_out")
        act_chain = sem("act_chain")

        kt_scr = dram("kt_scr", (PR, PAIRS, KEYS), BF16)
        kv_scr = dram("kv_scr", (T, WIN, KVC), F32)
        bc_scr = dram("bc_scr", (DS, 2, T), F32)

        def bank(k, at_, n, row=0, rows=P):
            return ps[row:row + rows, k, at_:at_ + n]

        block = ctx.enter_context(nc.Block())

        @block.sync
        def _(sp):
            sp.dma_start(seg_i[:, :], seg_d).then_inc(ld_seg, 16)
            sp.dma_start(xres[:, :, :], x_d).then_inc(ld_x, 16)
            sp.dma_start(cst[:, :], cst_d).then_inc(ld_cst, 16)
            sp.dma_start(segg_i[:, :], segrep_d).then_inc(ld_segg, 16)
            sp.dma_start(w0a[:, :], w0a_d).then_inc(ld_w0a, 16)
            sp.dma_start(w0q[:, :], w0q_d).then_inc(ld_w0q, 16)

            def chunk(c):
                if c >= 2:
                    sp.wait_ge(csum, adds(c - 2))
                sp.dma_start(cs[:, c % 2], ctx_d[c * CK:(c + 1) * CK, :].rearrange("(p t) d -> p t d", t=CT))\
                  .then_inc(ld_cs[c % 2], 16)

            sp.wait_ge(pe_step, WABS)
            sp.wait_ge(got_rope[1], 16)
            chunk(0)
            chunk(1)
            sp.dma_start(w0b[:, :], w0b_d).then_inc(ld_w0b, 16)
            for b in range(B):
                chunk(2 * b + 2)
                sp.wait_ge(kc_sb, 3 * b + 3)
                sp.dma_start(kv_scr[b * L:(b + 1) * L, :, :], krow[:, b, :, 0:KVC]).then_inc(st_kv, 16)
                chunk(2 * b + 3)
            sp.wait_ge(st_kv, 32)
            for j in range(WIN):
                sp.dma_start(kvg[j * GQ:(j + 1) * GQ, :, :], kv_scr[:, j, :].rearrange("(g i) k -> i g k", i=GQ))\
                  .then_inc(ld_kvg, 16)
            chunk(6)
            chunk(7)
            sp.dma_start(w1[:, :], w1_d).then_inc(ld_w1, 16)
            sp.wait_ge(kvm_ready, 2)
            sp.dma_start(kvg[GK:GK1, :, :], kvm[:, :, :]).then_inc(ld_kvg, 16)

            sp.wait_ge(mla_done, 1)

            def context(i, key0):
                sp.wait_ge(cx_tr, i + 1)
                sp.dma_start(cx[:, :, :], ctx_d[bass.ds(key0, CK), :].rearrange("(p t) d -> p t d", t=CT)).then_inc(ld_cx, 16)

            def inputs(i, states):
                for s in range(2):
                    sp.wait_ge(dbx_ready, 2 * i + s + 1)
                    sp.dma_start(bc[:, s, 0], bc_scr[bass.ds(states[s], 1), 0, :].partition_broadcast(P)
                                 .rearrange("p o t -> p (o t)")).then_inc(ld_b[s], 16)
                for s in range(2):
                    sp.wait_ge(hc_made, 2 * i + s + 1)
                    sp.dma_start(bc[:, s, 1], bc_scr[bass.ds(states[s], 1), 1, :].partition_broadcast(P)
                                 .rearrange("p o t -> p (o t)")).then_inc(ld_c[s], 16)

            context(0, 0)
            sp.dma_start(w2[:, :], w2_d).then_inc(ld_w2, 16)
            sp.wait_ge(dt_sb, 2)
            sp.dma_start(bc_scr.rearrange("s a t -> a s t"), bcT[0:2 * DS, :]).then_inc(st_bc, 16)
            sp.wait_ge(st_bc, 16)
            with sp.Fori(0, NC - 1) as i:
                key0, states = sp.snap(i * CK + CK), [sp.snap(2 * i + s) for s in range(2)]
                inputs(i, states)
                context(i + 1, key0)
            inputs(NC - 1, [2 * (NC - 1) + s for s in range(2)])
            sp.wait_ge(ktc_tr, 4 * NC + 1)
            sp.dma_start(w3[:, 0:w3a], w3_d[:, 0:w3a]).then_inc(ld_w3a, 16)

            def pair_keys(slot, n):
                sp.dma_start(kqs[:, slot, 0:KEYS], kt_scr[:, bass.ds(n, 1), :].rearrange("r o k -> r (o k)")).then_inc(ld_keys[slot], 16)

            def pair_queries(slot, n):
                sp.dma_start(kqs[:, slot, KEYS:KEYS + 2 * T], qz[:, bass.ds(n, 1), :, :].rearrange("r o h t -> r (o h t)"))\
                  .then_inc(ld_queries[slot], 16)

            def pair_scales(slot, n):
                sp.dma_start(sqs[:, slot, :], sqa[:, bass.ds(n, 1), :].rearrange("q o n -> q (o n)")).then_inc(ld_sqs[slot], 16)

            def pair_values(slot, n):
                sp.dma_start(vss[:, slot, :], vrow[:, bass.ds(n, 1), :].rearrange("k o n -> k (o n)")).then_inc(ld_vss[slot], 16)

            sp.wait_ge(kt_stored, 16 * NC + 16)
            sp.wait_ge(pe_step, FF_OUT)
            for slot in range(2):
                pair_keys(slot, slot)
            sp.wait_ge(sqa_ready, 1)
            for slot in range(2):
                pair_scales(slot, slot)
            sp.wait_ge(qz_ready[0], 2)
            sp.wait_ge(qz_ready[1], 2)
            for slot in range(2):
                pair_queries(slot, slot)
            sp.wait_ge(vr_sb, 8)
            for slot in range(2):
                pair_values(slot, slot)
            sp.wait_ge(vq_ready, 4)
            sp.dma_start(w3[:, w3a:W3], w3_d[:, w3a:W3]).then_inc(ld_w3b, 16)
            with sp.Fori(0, 3) as it:
                nxt = [sp.snap(2 * it + 2 + slot) for slot in range(2)]
                for slot in range(2):
                    sp.wait_ge(s_ps, 4 * (8 * it + 4 * slot + 4))
                    pair_keys(slot, nxt[slot])
                    pair_queries(slot, nxt[slot])
                    sp.wait_ge(ptr_used, 4 * (8 * it + 4 * slot + 4) + 4)
                    pair_scales(slot, nxt[slot])
                    pair_values(slot, nxt[slot])
            sp.wait_ge(y_ready, 2)
            sp.dma_start(out_d, xres[:, :, :]).then_inc(st_out, 16)
            sp.wait_ge(st_out, 16)

        @block.gpsimd
        def _(pool):
            pool.memset(neghalf[:, :], -0.5).then_inc(half, 1)
            pool.wait_ge(half, 1)

            def root(k):
                pool.wait_ge(ln_var, k + 1)
                pool.tensor_tensor(ln_rs[:, :], ln_ve[:, :], neghalf[:, :], ALU.pow).then_inc(ln_rstd, 1)

            root(0)
            pool.wait_ge(idx_ready, 1)
            for b in range(B):
                pool.indirect_dma_start(grow[:, b, :], None, ctx_d, bass.IndirectOffsetOnAxis(ap=idx[:, b:b + 1], axis=0))\
                    .then_inc(got_rows[b], 16)
            for b in range(B):
                pool.indirect_dma_start(rrow[:, b, :], None, rope_d, bass.IndirectOffsetOnAxis(ap=idx[:, B + b:B + b + 1], axis=0))\
                    .then_inc(got_rope[b], 16)
            for b in range(B):
                pool.wait_ge(got_rows[b], 16)
                pool.wait_ge(got_rope[b], 16)
            for p in range(PAIRS):
                pool.wait_ge(rq_ready, p + 1)
                r = rq[R:2 * R, p % 2]
                pool.tensor_tensor(qT[R:2 * R, :, 2 * p:2 * p + 2, :], r[:, 0].rearrange("p o (g i) -> p g o i", i=GQ),
                                   r[:, 1].rearrange("p o (g i) -> p g o i", i=GQ), ALU.add).then_inc(qr_sb, 1)
            pool.wait_ge(qr_sb, PAIRS)
            for c in range(NC):
                b, k = c * B // NC, c % (NC // B)
                pool.wait_ge(ld_cs[c % 2], 16 * (c // 2 + 1))
                if k == 0:
                    continue
                if k > 1:
                    pool.wait_ge(csum, adds(c) - 1)
                pool.tensor_tensor(csums[:, b], cs[:, 0] if k == 1 else csums[:, b], cs[:, c % 2], ALU.add).then_inc(csum, 1)
            root(1)


            def input_of(i, s):
                pool.wait_ge(ld_b[s], 16 * i + 16)
                pool.wait_ge(h_ready, 2 * i + s + 1)
                pool.tensor_tensor(dbx[:, s], u[:, :, :], bc[:, s, 0, :].unsqueeze(1).broadcast_to([P, ET, T]), ALU.mult)\
                    .then_inc(dbx_ready, 1)

            pool.nop().then_inc(dbx_ready, 2)
            pool.nop().then_inc(kq_ready, 1)
            wide = [P, CT * H, HW]

            def scaled(i):
                pool.wait_ge(krs_ready, i + 1)
                pool.tensor_tensor(tq[:, :, :], kb.rearrange("p t (h d) -> p (t h) d", h=H),
                                   krs.unsqueeze(2).broadcast_to(wide), ALU.mult).then_inc(tq_ready, 1)

            def quantised(i):
                pool.wait_ge(k_int, i + 1)
                pool.tensor_tensor(kq[:, :, :], tq[:, :, :], ksc.unsqueeze(2).broadcast_to(wide), ALU.mult).then_inc(kq_ready, 1)

            def sum_of(i):
                pool.wait_ge(hc_made, 2 * i + 4)
                pool.wait_ge(hc_used[1], i + 1)
                pool.tensor_tensor(th[:, :], th[:, :], hc[:, 1].rearrange("p t n -> p (t n)"), ALU.add).then_inc(hc_used[1], 1)

            scaled(0)
            pool.wait_ge(delta_ready, 1)
            pool.memset(th[:, :], 0.0).then_inc(hc_used[1], 1)
            pool.wait_ge(u_ready, 1)
            input_of(0, 0)
            input_of(0, 1)
            with pool.Fori(0, NC - 1) as i:
                input_of(i + 1, 0)
                quantised(i)
                sum_of(i)
                input_of(i + 1, 1)
                scaled(i + 1)
            quantised(NC - 1)
            sum_of(NC - 1)
            root(2)
            root(3)
            pool.wait_ge(pe_step, FF_OUT)
            pool.memset(hmask[0:PR, :], 1.0).then_inc(hmask_set, 1)
            pool.wait_ge(hmask_set, 1)
            pool.affine_select(out=hmask[0:PR, 0:1], in_=hmask[0:PR, 0:1], compare_op=ALU.is_ge, fill=0.0, base=PR // 2 - 1,
                               pattern=[[0, 1]], channel_multiplier=-1).then_inc(hmask_set, 1)
            pool.affine_select(out=hmask[0:PR, 1:2], in_=hmask[0:PR, 1:2], compare_op=ALU.is_ge, fill=0.0, base=-(PR // 2),
                               pattern=[[0, 1]], channel_multiplier=1).then_inc(hmask_set, 1)
            pool.wait_ge(hmask_set, 3)
            pool.memset(ln255[:, :], LN255).then_inc(ln255_set, 1)
            pool.wait_ge(ln255_set, 1)
            pool.memset(p8.rearrange("p a n -> p (a n)").bitcast(F16), 1024.0).then_inc(p8_set, 1)

            def exponent(it, j):
                u, slot = 8 * it + j, j // 4
                if j % 4 == 0:
                    pool.wait_ge(ld_sqs[slot], 16 * it + 16)
                pool.wait_ge(mx_ready, u + 1)
                pool.tensor_tensor(scaled_mx[:, j % 2:j % 2 + 1], mx1[:, j % 2:j % 2 + 1], sqs[:, slot, 4 + j % 4:5 + j % 4], ALU.mult)\
                    .then_inc(mx_scaled, 1)
                pool.wait_ge(mx_scaled, u + 1)
                pool.tensor_tensor(nb[:, j % 2:j % 2 + 1], scaled_mx[:, j % 2:j % 2 + 1], ln255[:, 0:1], ALU.add).then_inc(nb_ready, 1)

            with pool.Fori(0, UNITS // 8) as it:
                for j in range(8):
                    exponent(it, j)
            root(4)
            root(5)

        @block.scalar
        def _(act):
            link = Chain(act, act_chain)

            def columns(k):
                act.wait_ge(ln_tr, k + 1)
                act.activation(xnT.rearrange("p c t -> p (c t)"), bank(7, 0, 512), ACT.Copy).then_inc(ln_cols, 1)

            act.wait_ge(ld_cst, 16)
            act.activation(identb[:, :], ident, ACT.Copy).then_inc(identb_ready, 1)
            act.wait_ge(ld_w0q, 16)
            act.activation(w_qall[0:QC, :, KVC:2 * KVC], w_qr[0:QC, :, :], ACT.Copy).then_inc(wq_made, 1)
            half = R // 2
            for k in range(2):
                act.activation(w_qrs[0:QC, :, k * half:(k + 1) * half], w_qr[0:QC, :, (1 - k) * half:(2 - k) * half], ACT.Copy)\
                   .then_inc(wq_made, 1)
            act.wait_ge(pe_step, WABS)
            for n in range(2):
                act.activation(w_qall[0:QC, 8 * n:8 * n + 8, 0:KVC],
                               bank(n, 0, 512, 0, QC).rearrange("p (h k) -> p h k", h=8), ACT.Copy).then_inc(wabs_sb, 1)
            act.activation(w_kcat[:, :, KVC:2 * KVC], bank(2, 0, CH * R).rearrange("p (c r) -> p c r", c=CH), ACT.Copy)\
               .then_inc(wabs_sb, 1)
            columns(0)
            act.wait_ge(pe_step, QLAT)
            act.activation(q_cT[0:QC, :], bank(7, 0, T, 0, QC), ACT.Copy).then_inc(qlat_sb, 1)

            def window_columns(b, f):
                if b == 1 and f == 0:
                    act.wait_ge(kpr, 3)
                act.wait_ge(gt_tr, 5 * b + f + 1)
                nj = 2 if f < 4 else 1
                act.activation(gT.rearrange("p c j q -> p j c q")[:, 2 * f:2 * f + nj],
                               bank(4 + (5 * b + f) % 2, 0, nj * 2 * P).rearrange("p (j c q) -> p j c q", j=nj, c=CH), ACT.Copy)\
                   .then_inc(gt_sb, 1)

            for p in range(PAIRS):
                act.wait_ge(qpair, p + 1)
                act.activation(qT[0:KVC, :, 2 * p:2 * p + 2, :],
                               bank(p % 2, 0, 512, 0, KVC).rearrange("p (o g i) -> p g o i", o=2, i=GQ),
                               ACT.Copy).then_inc(qa_sb, 1)
                if p >= 3:
                    window_columns(0, p - 3)
            for b in range(B):
                if b == 1:
                    for f in range(5):
                        window_columns(1, f)
                for f in range(3):
                    n = 3 * b + f
                    act.wait_ge(kpr, n + 1)
                    act.activation(krow[:, b, 3 * f:3 * f + 3, 0:KVC],
                                   bank(6 + n % 2, 0, 3 * P).rearrange("p (j k) -> p j k", j=3)[:, :, 0:KVC], ACT.Copy)\
                       .then_inc(kc_sb, 1)
            for n in range(6):
                act.wait_ge(kt_tr, n + 1)
                act.activation(kcat[:, n // 3, 3 * (n % 3):3 * (n % 3) + 3, :],
                               bank(4 + n % 2, 0, 3 * P).rearrange("p (j k) -> p j k", j=3), ACT.Copy).then_inc(kt_sb, 1)
            def exponentials(b):
                act.wait_ge(sc_ready, b + 1)
                act.activation(sc[:, b * GB:(b + 1) * GB, :], sc[:, b * GB:(b + 1) * GB, :], ACT.Exp, scale=MLA_SCALE)\
                   .then_inc(sc_exp, 1)

            exponentials(0)
            for n in range(4):
                act.wait_ge(wvo, n + 1)
                act.activation(w_vo[:, 2 * n:2 * n + 2, :], bank(3 + n, 0, 512).rearrange("p (a n) -> p a n", a=2), ACT.Copy)\
                   .then_inc(wvo_sb, 1)
            exponentials(1)
            for n in range(8):
                if n == 1:
                    act.wait_ge(pe_step, MTR)
                    act.activation(mT[:, :], bank(7, 8, B * CH), ACT.Copy, scale=1.0 / NKEY).then_inc(mtr_sb, 1)
                if n == 2:
                    act.wait_ge(pe_step, MLAT)
                    act.activation(kvm[:, 0:GB, :], bank(7, 64, KVC, 0, 1).unsqueeze(1).broadcast_to([1, GB, KVC]), ACT.Copy)\
                       .then_inc(kvm_ready, 1)
                act.wait_ge(pt_tr, n + 1)
                act.activation(pT[0:GK1, 4 * n:4 * n + 4, :], bank(2 + n % 2, 0, 512, 0, GK1)
                               .rearrange("p (g r) -> p g r", g=4), ACT.Copy).then_inc(pt_sb, 1)

            columns(1)
            act.nop().then_inc(v_sb, 2)
            act.nop().then_inc(ktc_sb, 2)
            act.nop().then_inc(kt_stored, 16)

            def context_columns(i):
                act.wait_ge(cx_tr, i + 2)
                act.wait_ge(v_ps, 2 * i + 2)
                for c in range(CH):
                    act.activation(cT[:, c, :], bank(c, 0, CK), ACT.Copy).then_inc(cT_sb, 1)

            act.wait_ge(ld_w1, 16)
            for m in range(4):
                if m == 3:
                    context_columns(0)
                act.wait_ge(xz, m + 1)
                if m < 2:
                    act.activation(xpad[:, 2 * m:2 * m + 2, :, DC - 1:LP], bank(m, 0, 512)
                                   .rearrange("p (t b l) -> p t b l", t=2, b=B), ACT.Copy).then_inc(xz_sb, 1)
                    for t in range(2 * m, 2 * m + 2):
                        ins = act.activation(acc[:, t, :], bank(m, (t % 2) * T, T), ACT.Identity, bias=conv_b[:, t:t + 1],
                                             scale=conv_w[:, t, DC - 1:DC])
                    ins.then_inc(xz_sb, 1)
                else:
                    act.activation(zT[:, (m - 2) * 512:(m - 1) * 512], bank(m, 0, 512), ACT.Copy).then_inc(xz_sb, 1)
            act.wait_ge(conv, 2)
            act.activation(th[:, :], acc.rearrange("p t n -> p (t n)"), ACT.Tanh, scale=0.5).then_inc(xc_tanh, 1)
            act.wait_ge(xz_sb, 6)
            act.activation(hst[:, 0, :], zT[:, :], ACT.Tanh, scale=0.5).then_inc(z_tanh, 1)
            link(act.activation(aneg[:, :, :], a_log, ACT.Exp))
            act.activation(aneg[:, :, :], aneg[:, :, :], ACT.Copy, scale=-1.0).then_inc(aneg_ready, 1)
            act.wait_ge(pe_step, DLAT)
            act.activation(dtT[:, :], bank(7, 0, T), ACT.Copy).then_inc(dt_sb, 1)
            act.wait_ge(pe_step, DBC)
            act.activation(bcT[0:2 * DS, :], bank(4, T, T, 0, 2 * DS), ACT.Copy).then_inc(dt_sb, 1)
            act.wait_ge(pe_step, DLIN)
            for t in range(ET):
                ins = act.activation(th[:, t * T:(t + 1) * T], bank(5 + t // 2, (t % 2) * T, T), ACT.Abs, bias=b_dt[:, t:t + 1])
                if t % 2:
                    ins.then_inc(dlin_abs, 1)
            act.wait_ge(dlin_abs, 2)
            link(act.activation(th[:, :], th[:, :], ACT.Exp, scale=-1.0))
            act.activation(th[:, :], th[:, :], ACT.Ln, bias=1.0).then_inc(sp_ln, 1)
            act.wait_ge(aneg_ready, 1)
            act.wait_ge(delta_ready, 1)

            def decay(i, s):
                act.wait_ge(h_ready, 2 * i + s + 1)
                for t in range(ET):
                    ins = act.activation(dA[:, s, t, :].rearrange("p (b l) -> p b l", b=B)[:, :, 1:L],
                                         delta[:, t, :].rearrange("p (b l) -> p b l", b=B)[:, :, 1:L], ACT.Exp,
                                         scale=aneg[:, t, bass.ds(2 * i + s, 1)])
                ins.then_inc(dA_ready, 1)


            def values_of(i, m):
                act.wait_ge(v_ps, 2 * i + m + 3)
                act.activation(vT[:, m, bass.ds(CK * i, CK)], bank(m, 0, CK), ACT.Identity, bias=b_v[:, m:m + 1])\
                   .then_inc(v_sb, 1)

            def first_part(i):
                act.wait_ge(kq_ready, i + 2)
                act.wait_ge(ktc_tr, 4 * i + 1)
                act.activation(k3.rearrange("k t h a d -> k (t h) a d")[:, :, 0, :], kq[:, :, :], ACT.Copy).then_inc(k_hi, 1)

            def second_part(i):
                act.wait_ge(r1_ready, i + 1)
                act.activation(k3.rearrange("k t h a d -> k (t h) a d")[:, :, 1, :], r1[:, :, :], ACT.Copy).then_inc(k_hi, 1)

            def key_columns(i, half):
                for n in (2 * half, 2 * half + 1):
                    act.wait_ge(ktc_tr, 4 * i + n + 2)
                    if n == 0:
                        act.wait_ge(kt_stored, 16 * i + 16)
                    act.activation(ktc[:, 2 * n:2 * n + 2, :].rearrange("p a k -> p (a k)"),
                                   bank(4 + n % 2, 0, 512, 0, PR).bitcast(BF16), ACT.Copy).then_inc(ktc_sb, 1)

            def keys_out(i):
                act.wait_ge(ktc_sb, 4 * i + 6)
                act.dma_start(kt_scr[:, :, bass.ds(i * CK, CK)], ktc[:, :, :]).then_inc(kt_stored, 16)

            decay(0, 0)
            decay(0, 1)
            for m in range(CH):
                values_of(0, m)
            with act.Fori(0, NC - 1) as i:
                context_columns(i + 1)
                first_part(i)
                decay(i + 1, 0)
                second_part(i)
                decay(i + 1, 1)
                values_of(i + 1, 0)
                key_columns(i, 0)
                values_of(i + 1, 1)
                key_columns(i, 1)
                keys_out(i)

            def rounded(n):
                v = vT[:, n // 2, (n % 2) * KEYS // 2:(n % 2 + 1) * KEYS // 2]
                act.activation(v, v, ACT.Identity, bias=cst[:, 529:530], scale=vrs[:, n // 2:n // 2 + 1]).then_inc(v_round, 1)

            first_part(NC - 1)
            second_part(NC - 1)
            act.wait_ge(vsc_ready, 1)
            rounded(0)
            key_columns(NC - 1, 0)
            key_columns(NC - 1, 1)

            columns(2)
            keys_out(NC - 1)
            rounded(1)
            for n in range(4):
                act.wait_ge(ff_q, n + 1)
                act.activation(aT[:, 2 * n:2 * n + 2, :], hq[:, 2 * n:2 * n + 2, :], ACT.Gelu_apprx_tanh, scale=0.1)\
                   .then_inc(ff_a, 1)
            rounded(2)
            rounded(3)

            columns(3)

            def value_rows(n):
                m, q = n // 4, n % 4
                act.wait_ge(vr_tr, n + 1)
                act.activation(vrow.rearrange("k p (t n) -> k t p n", n=2 * HW)[:, 8 * q:8 * q + 8, 4 * m:4 * m + 4, :],
                               bank(5 + n % 2, 0, 512).bitcast(BF16).rearrange("k (t p n) -> k t p n", t=8, p=4), ACT.Copy)\
                   .then_inc(vr_sb, 1)

            for n in range(4):
                value_rows(n)
            act.nop().then_inc(p_ready, 4)
            act.wait_ge(pe_step, Q_TR)
            act.wait_ge(hmask_set, 3)
            for o in range(2):
                act.activation(qz[:, :, o, L:T], bank(7, 0, 512, 0, PR).bitcast(BF16).rearrange("r (p q) -> r p q", q=P), ACT.Copy,
                               scale=hmask[0:PR, o:o + 1]).then_inc(qz_ready[1], 1)
            for n in range(4, 8):
                value_rows(n)

            def probabilities(it, j, half):
                u, slot = 8 * it + j, j // 4
                if half == 0:
                    act.wait_ge(nb_ready, u + 1)
                    act.wait_ge(t_ps, 4 * u + 4)
                    if j % 4 == 0:
                        act.wait_ge(ld_sqs[slot], 16 * it + 16)
                        act.wait_ge(o_read, 2 * it + j // 4 + 1)
                keys = slice(half * KEYS // 2, (half + 1) * KEYS // 2)
                out8 = p8[:, j % 2, half * KEYS:(half + 1) * KEYS].rearrange("q (n w a e) -> q n a w e", w=P, a=2, e=2)
                act.activation(out8[:, :, :, :, 0], s_sb[:, j % 2, keys].rearrange("q (n a w) -> q n a w", a=2, w=P), ACT.Exp,
                               bias=nb[:, j % 2:j % 2 + 1], scale=sqs[:, slot, j % 4:j % 4 + 1],
                               accum_out=zs[:, slot, half, j % 4:j % 4 + 1]).then_inc(p_ready, 1)

            def columns16(it, j, c):
                u = 8 * it + j
                act.wait_ge(t_ps, 4 * u + c + 9)
                act.wait_ge(ptr_used, 4 * u + c + 1)
                act.activation(ptr[:, c, :], bank((4, 5, 6, 5)[c], 0, 512).bitcast(F16), ACT.Copy, bias=-1024.0)\
                   .then_inc(ptr_sb[1], 1)

            def turn(it, j, ahead=True):
                for half in range(2):
                    if ahead:
                        probabilities(*unit(it, j + 1), half)
                    columns16(*unit(it, j), 2 * half + 1)

            act.nop().then_inc(ptr_sb[1], 2)
            act.wait_ge(p8_set, 1)
            for half in range(2):
                probabilities(0, 0, half)
            turn(0, 0)
            with act.Fori(0, UNITS // 8 - 1) as it:
                for j in range(1, 9):
                    turn(it, j)
            for j in range(1, 8):
                turn(UNITS // 8 - 1, j, ahead=j < 7)
            act.wait_ge(pe_step, ON_TR)
            for c in range(CH):
                act.activation(onT[:, c, :], bank(4, c * T, T), ACT.Copy, scale=vsc[:, c:c + 1]).then_inc(on_cols, 1)

            columns(4)
            act.wait_ge(pe_step, Q_MADE)
            act.activation(q1[:, :], bank(2, 0, D), ACT.Copy, scale=HW ** -0.5).then_inc(q1_sb, 1)
            act.wait_ge(e2_arg, 1)
            act.activation(e2[:, :, :], s2[:, :, :], ACT.Exp).then_inc(e2_ready, 1)
            act.wait_ge(pe_step, VALUES_MADE)
            act.activation(orow[:, 0, :], bank(5, 0, D), ACT.Copy).then_inc(oa_rows, 1)
            act.wait_ge(pe_step, OA_TR)
            act.activation(oaT.rearrange("p c t -> p (c t)"), bank(3, 0, 512), ACT.Copy).then_inc(oa_cols, 1)

            columns(5)
            act.wait_ge(te_arg, 1)
            act.activation(te[:, :, :], te[:, :, :], ACT.Exp).then_inc(te_ready, 1)
            for m in range(FT + 1):
                act.wait_ge(moe_gu, m + 1)
                if m >= 2:
                    act.wait_ge(moe_h, m - 1)
                act.activation(tg[:, m % 2, :], bank(m % 4, 0, T), ACT.Tanh, scale=0.5).then_inc(moe_t, 1)

        @block.vector
        def _(dve):
            link = Chain(dve, dve_chain)

            def normalise(k):
                for b in range(B):
                    dve.bn_stats(ln_st[:, b, :], xres[:, b, :]).then_inc(dve_chain, 1)
                    link.n += 1
                dve.wait_ge(dve_chain, link.n)
                for b in range(B):
                    dve.bn_aggr(ln_mv[:, b, :], ln_st[:, b, :]).then_inc(dve_chain, 1)
                    link.n += 1
                dve.wait_ge(dve_chain, link.n)
                dve.tensor_scalar(ln_ve[:, :], ln_mv[:, :, 1], EPS, None, ALU.add).then_inc(ln_var, 1)
                dve.wait_ge(ln_rstd, k + 1)
                for b in range(B):
                    dve.tensor_scalar(xn[:, b, :], xres[:, b, :], ln_mv[:, b, 0:1], ln_rs[:, b:b + 1], ALU.subtract, ALU.mult)\
                       .then_inc(ln_rows, 1)

            dve.wait_ge(ld_x, 16)
            normalise(0)
            dve.wait_ge(ld_seg, 16)
            link(dve.tensor_copy(segf[:, :], seg_i[:, :]))
            link(dve.tensor_scalar(base[:, :], segf[:, :], float(-LOOKBACK), float(NKEY - WIN), ALU.add, ALU.min))
            link(dve.tensor_scalar(base[:, :], base[:, :], 0.0, None, ALU.max))
            dve.tensor_copy(idx[:, B:2 * B], base[:, :])
            for b in range(B):
                ins = dve.tensor_scalar(idx[:, b:b + 1], base[:, b:b + 1], float(b * NKEY), None, ALU.add)
            ins.then_inc(idx_ready, 1)
            dve.wait_ge(ld_segg, 16)
            dve.wait_ge(ld_cst, 16)
            link(dve.tensor_copy(segh[:, :], segg_i[:, :]))
            link(dve.tensor_scalar(low[:, :], segh[:, :], float(-LOOKBACK), None, ALU.add))
            link(dve.tensor_scalar(baseg[:, :], low[:, :], float(NKEY - WIN), 0.0, ALU.min, ALU.max))
            wide = [P, NG, WIN]
            link(dve.tensor_tensor(kid, baseg.unsqueeze(2).broadcast_to(wide), jidx.unsqueeze(1).broadcast_to(wide), ALU.add))
            link(dve.tensor_tensor(ge, kid, low.unsqueeze(2).broadcast_to(wide), ALU.is_ge))
            link(dve.tensor_tensor(kid, kid, segh.unsqueeze(2).broadcast_to(wide), ALU.is_le))
            link(dve.tensor_tensor(ge, ge, kid, ALU.mult))
            link(dve.tensor_reduce(anyg[:, :], ge, AX.X, ALU.max))
            dve.tensor_scalar(mask[:, :, GK:GK1].rearrange("p g o -> p (g o)"), anyg[:, :], NEG, None, ALU.mult)
            link(dve.tensor_scalar(ge, ge, -1.0, -NEG, ALU.add, ALU.mult))
            full = [P, NG, WIN, GQ]
            link(dve.tensor_tensor(mask[:, :, 0:GK].rearrange("p g (j i) -> p g j i", j=WIN),
                                   ge.unsqueeze(3).broadcast_to(full),
                                   negdiag.unsqueeze(1).unsqueeze(1).broadcast_to(full), ALU.add))
            dve.tensor_copy(sc[:, :, GK:GK1], mask[:, :, GK:GK1])
            for p in range(PAIRS):
                dve.wait_ge(qpair, p + 1)
                four = [R, 2, B, L]
                cosb = qcos[R:2 * R, :].unsqueeze(1).unsqueeze(1).broadcast_to(four)
                sinb = qsin[R:2 * R, :].unsqueeze(1).unsqueeze(1).broadcast_to(four)
                r = rq[R:2 * R, p % 2]
                if p >= 2:
                    dve.wait_ge(qr_sb, p - 1)
                split = "p (o b l) -> p o b l"
                dve.tensor_tensor(r[:, 0].rearrange("p o (b l) -> p o b l", b=B),
                                  bank(p % 2, 0, 512, R, R).rearrange(split, o=2, b=B), cosb, ALU.mult)
                dve.tensor_tensor(r[:, 1].rearrange("p o (b l) -> p o b l", b=B),
                                  bank(2 + p % 2, 0, 512, R, R).rearrange(split, o=2, b=B), sinb, ALU.mult).then_inc(rq_ready, 1)
            for n in range(6):
                b, f = n // 3, n % 3
                if f == 0:
                    dve.wait_ge(got_rope[b], 16)
                dve.wait_ge(kc_sb, n + 1)
                if n >= 2:
                    dve.wait_ge(kr_sb, n - 1)
                r = rk[:, n % 2]
                raw = bank(6 + n % 2, 0, 3 * P).rearrange("p (j k) -> p j k", j=3)[:, :, KVC:2 * KVC]
                angles = rrow[:, b, :].rearrange("p (j k) -> p j k", j=WIN)[:, 3 * f:3 * f + 3, :]
                dve.tensor_tensor(r[:, 0], raw, angles[:, :, 0:R], ALU.mult)
                dve.tensor_tensor(r[:, 1, :, 0:R // 2], raw[:, :, R // 2:R], angles[:, :, R:R + R // 2], ALU.mult)
                ins = dve.tensor_tensor(r[:, 1, :, R // 2:R], raw[:, :, 0:R // 2], angles[:, :, R + R // 2:2 * R], ALU.mult)
                ins.then_inc(kr_ps, 1)
                dve.wait_ge(kr_ps, n + 1)
                dve.tensor_tensor(krow[:, b, 3 * f:3 * f + 3, KVC:2 * KVC], r[:, 0], r[:, 1], ALU.add).then_inc(kr_sb, 1)
            for n in range(8):
                dve.wait_ge(scored, n + 1)
                dve.tensor_tensor(sc[:, 4 * n:4 * n + 4, 0:GK], bank(n % 2, 0, 4 * GK).rearrange("p (g k) -> p g k", g=4),
                                  mask[:, 4 * n:4 * n + 4, 0:GK], ALU.add).then_inc(sc_ps, 1)
                if n == 5:
                    dve.wait_ge(sc_exp, 1)
                    link(dve.tensor_reduce(mx[:, 0:GB], sc[:, 0:GB, :], AX.X, ALU.add))
                    dve.reciprocal(mx[:, 0:GB], mx[:, 0:GB]).then_inc(rsum, 1)
                if n % 4 == 3:
                    b = n // 4
                    s = sc[:, b * GB:(b + 1) * GB, :]
                    dve.wait_ge(sc_ps, n + 1)
                    link(dve.tensor_reduce(mx[:, b * GB:(b + 1) * GB], s, AX.X, ALU.max))
                    dve.tensor_tensor(s, s, mx[:, b * GB:(b + 1) * GB].unsqueeze(2).broadcast_to([P, GB, GK1]), ALU.subtract)\
                       .then_inc(sc_ready, 1)
            for b in range(B):
                s, m = sc[:, b * GB:(b + 1) * GB, :], mx[:, b * GB:(b + 1) * GB]
                if b == 0:
                    dve.wait_ge(rsum, 1)
                else:
                    dve.wait_ge(sc_exp, b + 1)
                    link(dve.tensor_reduce(m, s, AX.X, ALU.add))
                    link(dve.reciprocal(m, m))
                dve.tensor_tensor(s, s, m.unsqueeze(2).broadcast_to([P, GB, GK1]), ALU.mult).then_inc(probs, 1)
            dve.wait_ge(pe_step, MLAT)
            dve.tensor_copy(kvm[:, GB:2 * GB, :], bank(6, 0, KVC, 0, 1).unsqueeze(1).broadcast_to([1, GB, KVC]))\
               .then_inc(kvm_ready, 1)
            for n in range(4):
                dve.wait_ge(pv0, n + 1)
                dve.tensor_copy(oT.rearrange("k p (g i) -> k g p i", i=GQ)[:, 8 * n:8 * n + 8],
                                bank(4 + n % 2, 0, 512).rearrange("k (g p i) -> k g p i", g=8, p=PAIRS)).then_inc(ot_sb, 1)
            dve.wait_ge(pe_step, MLA_OUT)
            dve.tensor_tensor(xres[:, :, :], bank(0, 0, 512).rearrange("p (b d) -> p b d", b=B), xres[:, :, :], ALU.add)\
               .then_inc(mla_done, 1)
            dve.wait_ge(mla_done, 1)

            normalise(1)
            link(dve.memset(xpad[:, :, :, 0:DC - 1], 0.0))
            dve.memset(dA[:, :, :, :], 0.0)
            dve.nop().then_inc(kb_sb, 2)
            dve.wait_ge(ld_w1, 16)
            for m in range(2):
                dve.wait_ge(xz_sb, 2 * m + 2)
                for k in range(DC - 1):
                    for t in range(2 * m, 2 * m + 2):
                        a = acc[:, t, :].rearrange("p (b l) -> p b l", b=B)
                        ins = dve.scalar_tensor_tensor(out=a, in0=xpad[:, t, :, k:k + L], scalar=conv_w[:, t, k:k + 1], in1=a,
                                                       op0=ALU.mult, op1=ALU.add)
                    if k < DC - 2:
                        link(ins)
                ins.then_inc(conv, 1)
            acc_f = acc.rearrange("p t n -> p (t n)")
            dve.wait_ge(xc_tanh, 1)
            link(dve.scalar_tensor_tensor(out=xc[:, :], in0=th[:, :], scalar=1.0, in1=acc_f, op0=ALU.add, op1=ALU.mult))
            dve.tensor_scalar(xc[:, :], xc[:, :], 0.5, None, ALU.mult).then_inc(xc_ready, 1)
            dve.wait_ge(xc_ready, 1)
            tq_f = tq.rearrange("p a b -> p (a b)")
            dve.nop().then_inc(h_ready, 2)
            dve.nop().then_inc(hc_made, 2)

            def biased(i):
                dve.wait_ge(kq_ready, i + 1)
                for n in range(2):
                    dve.wait_ge(k_ps, 2 * i + n + 1)
                    dve.tensor_tensor(kb[:, 2 * n:2 * n + 2, :], bank(2 + n, 0, 512).rearrange("p (t d) -> p t d", t=2),
                                      b_k.unsqueeze(1).broadcast_to([P, 2, D]), ALU.add).then_inc(kb_sb, 1)

            def scale_of(i):
                dve.wait_ge(kb_sb, 2 * i + 4)
                link(dve.tensor_reduce(kmx[:, :], kb.rearrange("p t (h d) -> p (t h) d", h=H), AX.X, ALU.max,
                                       apply_absolute_value=True))
                link(dve.tensor_scalar(ksc[:, :], kmx[:, :], 1.0 / QMAX, 1e-8, ALU.mult, ALU.max))
                dve.reciprocal(krs[:, :], ksc[:, :]).then_inc(krs_ready, 1)

            biased(0)
            scale_of(0)
            dve.wait_ge(z_tanh, 1)
            link(dve.scalar_tensor_tensor(out=zT[:, :], in0=hst[:, 0, :], scalar=1.0, in1=zT[:, :], op0=ALU.add, op1=ALU.mult))
            for t in range(ET):
                if t % 2 == 0:
                    dve.wait_ge(dlin_abs, t // 2 + 1)
                ins = dve.tensor_scalar(acc[:, t, :], bank(5 + t // 2, (t % 2) * T, T), b_dt[:, t:t + 1], None, ALU.add)
            link(ins)
            dve.wait_ge(sp_ln, 1)
            delta_f, u_f = delta.rearrange("p t n -> p (t n)"), u.rearrange("p t n -> p (t n)")
            dve.scalar_tensor_tensor(out=delta_f, in0=acc_f, scalar=0.0, in1=th[:, :], op0=ALU.max, op1=ALU.add)\
               .then_inc(delta_ready, 1)
            dve.wait_ge(delta_ready, 1)
            dve.tensor_tensor(u_f, delta_f, xc[:, :], ALU.mult).then_inc(u_ready, 1)
            for t in range(ET):
                ins = dve.tensor_scalar(acc_f[:, t * T:(t + 1) * T], xc[:, t * T:(t + 1) * T], dskip[:, t:t + 1], None, ALU.mult)
            ins.then_inc(skip, 1)

            def state(i, s):
                dve.wait_ge(dA_ready, 2 * i + s + 1)
                dve.wait_ge(dbx_ready, 2 * i + s + 3)
                dve.tensor_tensor_scan(hst[:, s, :], dA[:, s].rearrange("p t n -> p (t n)"),
                                       dbx[:, s].rearrange("p t n -> p (t n)"), 0.0, ALU.mult, ALU.add).then_inc(h_ready, 1)
                dve.wait_ge(h_ready, 2 * i + s + 3)
                dve.wait_ge(hc_used[s], i + 1)
                dve.wait_ge(ld_c[s], 16 * i + 16)
                dve.tensor_tensor(hc[:, s], hst[:, s, :].rearrange("p (t n) -> p t n", t=ET),
                                  bc[:, s, 1, :].unsqueeze(1).broadcast_to([P, ET, T]), ALU.mult).then_inc(hc_made, 1)

            k3v = k3.rearrange("k t h a d -> k (t h) a d")

            def integers(i):
                dve.wait_ge(tq_ready, i + 1)
                link(dve.tensor_scalar(tq_f, tq_f, MAGIC, MAGIC + QMAX, ALU.add, ALU.min))
                dve.tensor_scalar(tq_f, tq_f, MAGIC - QMAX, MAGIC, ALU.max, ALU.subtract).then_inc(k_int, 1)

            def second_part(i):
                dve.wait_ge(k_hi, 2 * i + 1)
                dve.tensor_tensor(r1[:, :, :], kq[:, :, :], k3v[:, :, 0, :], ALU.subtract).then_inc(r1_ready, 1)

            def third_part(i):
                dve.wait_ge(r1_ready, i + 1)
                dve.wait_ge(k_hi, 2 * i + 2)
                dve.tensor_tensor(k3v[:, :, 2, :], r1[:, :, :], k3v[:, :, 1, :], ALU.subtract).then_inc(k3_ready, 1)

            def largest(i):
                dve.wait_ge(v_sb, 2 * i + 4)
                dve.tensor_reduce(vmx[:, :, bass.ds(i, 1)], vT[:, :, bass.ds(CK * i, CK)], AX.X, ALU.max,
                                  apply_absolute_value=True).then_inc(vmx_made, 1)

            state(0, 0)
            start = link.n
            with dve.Fori(0, NC - 1) as i:
                link.n, link.off = start, KV_LINKS * i
                integers(i)
                state(i, 1)
                second_part(i)
                biased(i + 1)
                third_part(i)
                scale_of(i + 1)
                largest(i)
                state(i + 1, 0)
            assert link.n == start + KV_LINKS
            link.n, link.off = start + KV_LINKS * (NC - 1), 0
            integers(NC - 1)
            state(NC - 1, 1)
            largest(NC - 1)
            dve.wait_ge(vmx_made, NC)
            link(dve.tensor_reduce(vmx[:, :, NC:NC + 1], vmx[:, :, 0:NC], AX.X, ALU.max))
            link(dve.tensor_scalar(vsc[:, :], vmx[:, :, NC], 1.0 / QMAX, 1e-8, ALU.mult, ALU.max))
            dve.reciprocal(vrs[:, :], vsc[:, :]).then_inc(vsc_ready, 1)
            second_part(NC - 1)
            dve.wait_ge(hc_used[0], NC + 1)
            dve.wait_ge(hc_used[1], NC + 1)
            th_f = th.rearrange("p (n k) -> p n k", n=2)
            link(dve.tensor_tensor(th_f, ps[:, 6:8, :], th_f, ALU.add))
            for n in range(2):
                ins = dve.scalar_tensor_tensor(out=acc_f[:, n * 512:(n + 1) * 512], in0=th[:, n * 512:(n + 1) * 512], scalar=0.5,
                                               in1=zT[:, n * 512:(n + 1) * 512], op0=ALU.mult, op1=ALU.mult)
            ins.then_inc(gated, 1)
            third_part(NC - 1)
            dve.wait_ge(pe_step, MIX_OUT)
            dve.tensor_tensor(xres[:, :, :], bank(2, 0, 512).rearrange("p (b d) -> p b d", b=B), xres[:, :, :], ALU.add)\
               .then_inc(mix_add, 1)
            dve.wait_ge(mix_add, 1)

            def integer_values(n):
                half = slice((n % 2) * KEYS // 2, (n % 2 + 1) * KEYS // 2)
                dve.wait_ge(v_round, n + 1)
                dve.tensor_scalar(vqb[:, n // 2, half], vT[:, n // 2, half], MAGIC, QMAX, ALU.subtract, ALU.min).then_inc(vq_ready, 1)

            normalise(2)
            integer_values(0)
            for n in range(4):
                h2 = hq[:, 2 * n:2 * n + 2, :].rearrange("p m t -> p (m t)")
                dve.wait_ge(ff_h, n + 1)
                link(dve.tensor_scalar(h2, bank(n, 0, 512), 10.0, 32767.0, ALU.mult, ALU.min))
                link(dve.tensor_scalar(h2, h2, -32768.0, MAGIC, ALU.max, ALU.add))
                dve.tensor_scalar(h2, h2, MAGIC, None, ALU.subtract).then_inc(ff_q, 1)

            def clipped_values(m):
                dve.wait_ge(vq_ready, 2 * m + 2)
                dve.tensor_scalar(vqb[:, m, :], vqb[:, m, :], -QMAX, None, ALU.max).then_inc(vq_clip, 1)

            integer_values(1)
            clipped_values(0)
            dve.wait_ge(pe_step, FF_OUT)
            dve.tensor_tensor(xres[:, :, :], ps[:, 4:6, 0:D], xres[:, :, :], ALU.add).then_inc(ff_add, 1)
            dve.wait_ge(ff_add, 1)

            normalise(3)
            integer_values(2)
            integer_values(3)
            clipped_values(1)
            dve.wait_ge(ld_w3a, 16)
            dve.wait_ge(pe_step, Q_PS)
            link(dve.tensor_tensor(qb.rearrange("p (b h) d -> p b (h d)", b=B), bank(0, 0, 512).rearrange("p (b d) -> p b d", b=B),
                                   b_q.unsqueeze(1).broadcast_to([P, B, D]), ALU.add))
            link(dve.tensor_reduce(qmx[:, :], qb, AX.X, ALU.max, apply_absolute_value=True))
            link(dve.tensor_scalar(qsc[:, :], qmx[:, :], HW ** -0.5 / QMAX, 1e-8, ALU.mult, ALU.max))
            link(dve.reciprocal(qrs[:, :], qsc[:, :]))
            link(dve.scalar_tensor_tensor(out=qb, in0=qb, scalar=HW ** -0.5, in1=qrs.unsqueeze(2).broadcast_to([P, B * H, HW]),
                                          op0=ALU.mult, op1=ALU.mult))
            link(dve.tensor_scalar(qb, qb, MAGIC, MAGIC + QMAX, ALU.add, ALU.min))
            dve.tensor_scalar(q3, qb.unsqueeze(2).broadcast_to([P, B * H, 3, HW]), MAGIC - QMAX, MAGIC, ALU.max, ALU.subtract)\
               .then_inc(q3_ready, 1)
            for sgn, o in ((1.0, 0), (-1.0, 4)):
                ins = dve.tensor_scalar(sqa[:, :, o:o + 4].rearrange("q p (o b) -> q p o b", o=2),
                                        qsc.rearrange("q (b p o) -> q p o b", b=B, o=2), sgn, None, ALU.mult)
            ins.then_inc(sqa_ready, 1)
            link(dve.tensor_tensor(xres[:, :, :], xres[:, :, :], b_p.unsqueeze(1).broadcast_to([P, B, D]), ALU.add))
            dve.nop().then_inc(ptr_sb[0], 2)
            dve.nop().then_inc(s_read, 2)
            dve.nop().then_inc(o_read, 2)
            dve.wait_ge(pe_step, Q_TR)
            dve.wait_ge(hmask_set, 3)
            for o in range(2):
                dve.tensor_scalar(qz[:, :, o, 0:L], bank(4, 0, 512, 0, PR).bitcast(BF16).rearrange("r (p q) -> r p q", q=P),
                                  hmask[0:PR, o:o + 1], None, ALU.mult).then_inc(qz_ready[0], 1)

            def maxima(it, j, c):
                u = 8 * it + j
                if c == 0:
                    dve.wait_ge(p_ready, 2 * u + 2)
                dve.wait_ge(s_ps, 4 * u + c + 1)
                dve.tensor_scalar(s_sb[:, j % 2, c * 1024:(c + 1) * 1024], ps[:, 2 * (c % 2):2 * (c % 2) + 2, :]
                                  .rearrange("p a n -> p (a n)"), 1.0, None, ALU.mult, ALU.max,
                                  accum_out=mxs[:, j % 2, c:c + 1]).then_inc(s_read, 1)
                if c == 3:
                    dve.wait_ge(s_read, 4 * u + 6)
                    dve.tensor_reduce(mx1[:, j % 2:j % 2 + 1], mxs[:, j % 2, :], AX.X, ALU.max).then_inc(mx_ready, 1)

            def columns16(it, j, c):
                u = 8 * it + j
                dve.wait_ge(t_ps, 4 * u + c + 9)
                dve.wait_ge(ptr_used, 4 * u + c + 1)
                dve.tensor_scalar(ptr[:, c, :], bank((4, 5, 6, 5)[c], 0, 512).bitcast(F16), -1024.0, None, ALU.add)\
                   .then_inc(ptr_sb[0], 1)

            def sums(it, g):
                n = 2 * it + g
                dve.wait_ge(ptr_used, 4 * (8 * it + 4 * g + 4) + 4)
                dve.tensor_tensor(zall[:, bass.ds(n, 1), :].rearrange("q o u -> q (o u)"), zs[:, g, 0, :], zs[:, g, 1, :], ALU.add)
                dve.tensor_copy(oall[:, bass.ds(n, 1), :, :].rearrange("q o u d -> q (o u d)"), bank(7, 0, 4 * HW)).then_inc(o_read, 1)

            def turn(it, j, ahead=True):
                for c in range(4):
                    if ahead:
                        maxima(*unit(it, j + 2), c)
                    if c % 2 == 0:
                        columns16(*unit(it, j), c)
                    if c == 1 and j % 4 == 0 and j:
                        sums(it, j // 4 - 1)

            for j in range(2):
                for c in range(4):
                    maxima(0, j, c)
            turn(0, 0)
            with dve.Fori(0, UNITS // 8 - 1) as it:
                for j in range(1, 9):
                    turn(it, j)
            for j in range(1, 8):
                turn(UNITS // 8 - 1, j, ahead=j < 6)
            sums(UNITS // 8 - 1, 1)
            dve.wait_ge(o_read, 2 + PAIRS)
            link(dve.reciprocal(rz[:, :], zall.rearrange("q p u -> q (p u)")))
            for b in range(B):
                ins = dve.tensor_tensor(onrm[:, b, :].rearrange("q (p o d) -> q p o d", p=PAIRS, o=2),
                                        oall.rearrange("q p (o b) d -> q b p o d", b=B)[:, b],
                                        rz.rearrange("q (p o b) -> q b p o", o=2, b=B)[:, b].unsqueeze(3)
                                        .broadcast_to([P, PAIRS, 2, HW]), ALU.mult)
            ins.then_inc(on_rows, 1)
            dve.wait_ge(pe_step, X_OUT)
            link(dve.tensor_tensor(xres[:, :, :], bank(5, 0, 512).rearrange("p (b d) -> p b d", b=B), xres[:, :, :], ALU.add))

            normalise(4)
            dve.wait_ge(q1_sb, 1)
            dve.wait_ge(pe_step, KEYS_MADE)
            dve.tensor_tensor(prod[:, 0, :], bank(0, 0, D), q1[:, :], ALU.mult)
            link(dve.tensor_tensor(prod[:, 1, :], bank(1, 0, D), q1[:, :], ALU.mult))
            link(dve.tensor_reduce(s2[:, :, :].rearrange("p m h -> p (m h)"), prod.rearrange("p m (h d) -> p (m h) d", d=HW),
                                   AX.X, ALU.add))
            link(dve.tensor_tensor(m2[:, :], s2[:, 0, :], s2[:, 1, :], ALU.max))
            dve.tensor_tensor(s2[:, :, :], s2[:, :, :], m2.unsqueeze(1).broadcast_to([P, 2, H]), ALU.subtract).then_inc(e2_arg, 1)
            dve.wait_ge(e2_ready, 1)
            link(dve.tensor_tensor(z2[:, :], e2[:, 0, :], e2[:, 1, :], ALU.add))
            link(dve.reciprocal(z2[:, :], z2[:, :]))
            link(dve.tensor_tensor(e2[:, :, :], e2[:, :, :], z2.unsqueeze(1).broadcast_to([P, 2, H]), ALU.mult))
            dve.wait_ge(pe_step, VALUES_MADE)
            dve.wait_ge(oa_rows, 1)
            for m in range(2):
                ins = dve.tensor_tensor(pv2[:, m, :].rearrange("p (h d) -> p h d", d=HW),
                                        bank(5 + m, 0, D).rearrange("p (h d) -> p h d", d=HW),
                                        e2[:, m, :].unsqueeze(2).broadcast_to([P, H, HW]), ALU.mult)
            link(ins)
            dve.nop().then_inc(qkv_used, 1)
            dve.tensor_tensor(orow[:, 1, :], pv2[:, 0, :], pv2[:, 1, :], ALU.add).then_inc(oa_rows, 1)
            dve.wait_ge(pe_step, SA_OUT)
            link(dve.tensor_tensor(xres[:, :, :], bank(4, 0, 512).rearrange("p (b d) -> p b d", b=B), xres[:, :, :], ALU.add))

            normalise(5)
            dve.wait_ge(pe_step, LOGITS)
            for b in range(B):
                ins = dve.max(top[:, b, :], bank(7, b * E, E))
            link(ins)
            dve.tensor_tensor(te[:, :, :], top[:, :, 0:2], top[:, :, 0:1].broadcast_to([P, B, 2]), ALU.subtract).then_inc(te_arg, 1)
            dve.wait_ge(te_ready, 1)
            link(dve.tensor_tensor(tz[:, :], te[:, :, 0], te[:, :, 1], ALU.add))
            link(dve.reciprocal(tz[:, :], tz[:, :]))
            link(dve.tensor_tensor(te[:, :, :], te[:, :, :], tz.unsqueeze(2).broadcast_to([P, B, 2]), ALU.mult))
            link(dve.tensor_tensor(comb[:, :], te[:, :, 0], te[:, :, 1], ALU.add))
            for m in range(FT + 1):
                dve.wait_ge(moe_t, m + 1)
                link(dve.scalar_tensor_tensor(out=ga[:, m % 2, :], in0=tg[:, m % 2, :], scalar=1.0, in1=bank(m % 4, 0, T),
                                              op0=ALU.add, op1=ALU.mult))
                dve.scalar_tensor_tensor(out=hT[:, m, :], in0=ga[:, m % 2, :], scalar=0.5, in1=bank(m % 4, T, T),
                                         op0=ALU.mult, op1=ALU.mult).then_inc(moe_h, 1)
            dve.wait_ge(moe_out, 1)
            link(dve.tensor_tensor(xres[:, :, :], bank(5, 0, 512).rearrange("p (b d) -> p b d", b=B), xres[:, :, :], ALU.add))
            dve.wait_ge(moe_out, 2)
            for b in range(B):
                dve.scalar_tensor_tensor(out=xres[:, b, :], in0=bank(6, b * D, D), scalar=comb[:, b:b + 1], in1=xres[:, b, :],
                                         op0=ALU.mult, op1=ALU.add).then_inc(y_ready, 1)

        @block.tensor
        def _(pe):
            def columns(k):
                pe.wait_ge(ln_rows, 2 * (k + 1))
                for c in range(CH):
                    for b in range(B):
                        mm = pe.transpose(bank(7, c * T + b * L, P), xn[:, b, c * P:(c + 1) * P], ident)
                mm.then_inc(ln_tr, 1)

            pe.wait_ge(ld_cst, 16)
            pe.wait_ge(ld_w0a, 16)
            for h in range(H):
                pe.matmul(bank(h // 8, (h % 8) * KVC, KVC, 0, QC), w_uqT[:, h, :], w_ukT[:, h, :], start=True, stop=True)
            for c in range(CH):
                mm = pe.matmul(bank(2, c * R, R), w_kvcT[0:KVC, c * P:(c + 1) * P], w_kr[0:KVC, :], start=True, stop=True)
            mm.then_inc(pe_step, 1)
            columns(0)
            pe.wait_ge(ld_w0q, 16)
            pe.wait_ge(ln_cols, 1)
            for c in range(CH):
                mm = pe.matmul(bank(7, 0, T, 0, QC), w_dq[:, c, :], xnT[:, c, :], start=(c == 0), stop=(c == CH - 1))
            mm.then_inc(pe_step, 1)

            def window_columns(b, f):
                if f == 0:
                    pe.wait_ge(got_rows[b], 16)
                n = 5 * b + f
                if n >= 2:
                    pe.wait_ge(gt_sb, n - 1)
                for j in range(2 * f, min(2 * f + 2, WIN)):
                    for c in range(CH):
                        mm = pe.transpose(bank(4 + n % 2, ((j % 2) * CH + c) * P, P), grow[:, b, j * D + c * P:j * D + (c + 1) * P],
                                          ident)
                mm.then_inc(gt_tr, 1)

            pe.wait_ge(qlat_sb, 1)
            pe.wait_ge(wq_made, 3)
            pe.wait_ge(wabs_sb, 3)
            for p in range(PAIRS):
                if p >= 2:
                    pe.wait_ge(qa_sb, p - 1)
                    pe.wait_ge(rq_ready, p - 1)
                for o in range(2):
                    pe.matmul(bank(p % 2, o * T, T), w_qall[0:QC, 2 * p + o, :], q_cT[0:QC, :], start=True, stop=True)
                for o in range(2):
                    mm = pe.matmul(bank(2 + p % 2, o * T, T, R, R), w_qrs[0:QC, 2 * p + o, :], q_cT[0:QC, :],
                                   start=True, stop=True)
                mm.then_inc(qpair, 1)
                if p >= 3:
                    window_columns(0, p - 3)
            for b in range(B):
                if b == 1:
                    for f in range(5):
                        window_columns(1, f)
                pe.wait_ge(gt_sb, 5 * b + 5)
                for f in range(3):
                    n = 3 * b + f
                    if n >= 2:
                        pe.wait_ge(kc_sb, n - 1)
                        pe.wait_ge(kr_ps, n - 1)
                    for j in range(3):
                        for c in range(CH):
                            mm = pe.matmul(bank(6 + n % 2, j * P, P), gT[:, c, 3 * f + j, :], w_kcat[:, c, :],
                                           start=(c == 0), stop=(c == CH - 1))
                    mm.then_inc(kpr, 1)
            for n in range(6):
                b, f = n // 3, n % 3
                pe.wait_ge(kc_sb, n + 1)
                pe.wait_ge(kr_sb, n + 1)
                pe.wait_ge(gt_sb, 10) if n < 2 else pe.wait_ge(kt_sb, n - 1)
                for j in range(3):
                    mm = pe.transpose(bank(4 + n % 2, j * P, P), krow[:, b, 3 * f + j, :], ident)
                mm.then_inc(kt_tr, 1)
            pe.wait_ge(qa_sb, PAIRS)
            pe.wait_ge(qr_sb, PAIRS)
            def weights_vo(n):
                for p in range(2 * n, 2 * n + 2):
                    for o in range(2):
                        mm = pe.matmul(bank(3 + n, (p % 2) * D, D, o * KVC, KVC), w_uvT[:, 2 * p + o, :], w_o[:, 2 * p + o, :],
                                       start=True, stop=True)
                mm.then_inc(wvo, 1)

            def mean_column(b):
                pe.wait_ge(csum, adds((b + 1) * NC // B - 1))
                for c in range(CH):
                    for t in range(CT):
                        mm = pe.matmul(bank(7, 8 + CH * b + c, 1), csums[:, b, t, c * P:(c + 1) * P], ones[:, 0:1],
                                       start=(t == 0), stop=(t == CT - 1))
                return mm

            for n in range(8):
                if n == 6:
                    pe.wait_ge(ld_w0b, 16)
                    pe.wait_ge(kr_ps, 6)
                    weights_vo(0)
                    weights_vo(1)
                pe.wait_ge(kt_sb, 3 if n < 4 else 6)
                if n >= 2:
                    pe.wait_ge(sc_ps, n - 1)
                for i in range(4):
                    g = 4 * n + i
                    q, b = g * GQ, g // GB
                    mm = pe.matmul(bank(n % 2, i * GK, GK), qT[:, g].rearrange("k h i -> k (h i)"), kcat[:, b, :, q % L:q % L + GQ],
                                   start=True, stop=True)
                mm.then_inc(scored, 1)
            weights_vo(2)
            weights_vo(3)
            mean_column(0)
            for n in range(8):
                if n == 0:
                    mean_column(1).then_inc(pe_step, 1)
                if n == 2:
                    pe.wait_ge(mtr_sb, 1)
                    pe.wait_ge(wvo_sb, 4)
                    for b in range(B):
                        for c in range(CH):
                            mm = pe.matmul(bank(7 - b, 64 * (1 - b), KVC, 0, 1), mT[:, CH * b + c:CH * b + c + 1], w_kcat[:, c, 0:KVC],
                                           start=(c == 0), stop=(c == CH - 1))
                    mm.then_inc(pe_step, 1)
                pe.wait_ge(probs, 1 if n < 4 else 2)
                if n == 1:
                    pe.wait_ge(wvo_sb, 1)
                if n >= 2:
                    pe.wait_ge(pt_sb, n - 1)
                for i in range(4):
                    mm = pe.transpose(bank(2 + n % 2, i * P, P, 0, GK1), sc[:, 4 * n + i, :], ident)
                mm.then_inc(pt_tr, 1)
            pe.wait_ge(ld_kvg, 16 * (WIN + 1))
            for n in range(4):
                pe.wait_ge(pt_sb, 2 * n + 2)
                if n >= 2:
                    pe.wait_ge(ot_sb, n - 1)
                for i in range(8):
                    g = 8 * n + i
                    for o in range(2):
                        pr = pT[0:GK1, g, :].rearrange("k (p o i) -> k o p i", o=2, i=GQ)[:, o]
                        mm = pe.matmul(bank(4 + n % 2, i * 64, 64, o * KVC, KVC), kvg[0:GK1, g, :], pr, start=True, stop=True)
                mm.then_inc(pv0, 1)
            for b in range(B):
                pe.wait_ge(ot_sb, 2 * b + 2)
                for p in range(PAIRS):
                    mm = pe.matmul(bank(0, b * D, D), oT[:, p, b * L:(b + 1) * L], w_vo[:, p, :],
                                   start=(p == 0), stop=(p == PAIRS - 1))
            mm.then_inc(pe_step, 1)

            pe.nop().then_inc(cx_tr, 1)
            pe.nop().then_inc(v_ps, 2)
            pe.nop().then_inc(ktc_tr, 1)
            pe.nop().then_inc(hc_used[0], 1)
            columns(1)

            def turned(i):
                pe.wait_ge(ld_cx, 16 * i + 16)
                pe.wait_ge(v_sb, 2 * i + 2)
                for t in range(CT):
                    for c in range(CH):
                        mm = pe.transpose(bank(c, t * P, P), cx[:, t, c * P:(c + 1) * P], ident)
                mm.then_inc(cx_tr, 1)

            pe.wait_ge(ld_w1, 16)
            pe.wait_ge(ln_cols, 2)
            for m in range(2 * ET):
                if m == 3 * ET // 2:
                    pe.wait_ge(xz_sb, 4)
                    turned(0)
                for c in range(CH):
                    mm = pe.matmul(bank(m // 2, (m % 2) * T, T), w_in[:, c, m * P:(m + 1) * P], xnT[:, c, :],
                                   start=(c == 0), stop=(c == CH - 1))
                if m % 2:
                    mm.then_inc(xz, 1)

            def keys(i, tiles=range(CT)):
                pe.wait_ge(cT_sb, 2 * i + 2)
                pe.wait_ge(kb_sb, 2 * i + 2)
                for t in tiles:
                    for c in range(CH):
                        mm = pe.matmul(bank(2 + t // 2, (t % 2) * D, D), cT[:, c, t * P:(t + 1) * P], w_kv[:, c, 0:D],
                                       start=(c == 0), stop=(c == CH - 1))
                    if t % 2:
                        mm.then_inc(k_ps, 1)

            def values_of(i, m):
                for c in range(CH):
                    mm = pe.matmul(bank(m, 0, CK), w_kv[:, c, D + m * P:D + (m + 1) * P], cT[:, c, :],
                                   start=(c == 0), stop=(c == CH - 1))
                mm.then_inc(v_ps, 1)

            pe.wait_ge(xz_sb, 5)
            keys(0, range(CT // 2))
            pe.wait_ge(xz_sb, 6)
            keys(0, range(CT // 2, CT))
            pe.wait_ge(xc_ready, 1)
            for c in range(ET):
                mm = pe.matmul(bank(7, 0, T), w_x[:, c, 0:DR], xc[:, c * T:(c + 1) * T], start=(c == 0), stop=(c == ET - 1))
            mm.then_inc(pe_step, 1)
            for c in range(ET):
                mm = pe.matmul(bank(4, T, T, 0, 2 * DS), w_x[:, c, DR:DR + 2 * DS], xc[:, c * T:(c + 1) * T],
                               start=(c == 0), stop=(c == ET - 1))
            mm.then_inc(pe_step, 1)
            pe.wait_ge(dt_sb, 1)
            for t in range(ET):
                mm = pe.matmul(bank(5 + t // 2, (t % 2) * T, T), w_dt[:, t * P:(t + 1) * P], dtT[:, :], start=True, stop=True)
            mm.then_inc(pe_step, 1)
            values_of(0, 0)
            values_of(0, 1)
            pe.wait_ge(skip, 1)
            for n in range(2):
                pe.matmul(bank(6 + n, 0, 512), ident, acc.rearrange("p t n -> p (t n)")[:, n * 512:(n + 1) * 512],
                          start=True, stop=True)
            pe.wait_ge(dt_sb, 2)

            def state(i):
                pe.wait_ge(hc_made, 2 * i + 3)
                for n in range(2):
                    mm = pe.matmul(bank(6 + n, 0, 512), ident, hc[:, 0].rearrange("p t n -> p (t n)")[:, n * 512:(n + 1) * 512],
                                   start=False, stop=True, skip_group_check=True)
                mm.then_inc(hc_used[0], 1)

            def key_columns(i, half):
                pe.wait_ge(k3_ready, i + 1)
                for n in (2 * half, 2 * half + 1):
                    pe.wait_ge(ktc_sb, 4 * i + n + 1)
                    for o in range(2):
                        p = 2 * n + o
                        for t in range(CT):
                            dst = bank(4 + n % 2, 0, 512, 0, PR).bitcast(BF16)[:, (o * CT + t) * P:(o * CT + t + 1) * P]
                            mm = pe.transpose(dst, k3[:, t, 2 * p:2 * p + 2].rearrange("k h a d -> k (h a d)"), identb[:, :])
                    mm.then_inc(ktc_tr, 1)

            with pe.Fori(0, NC - 1) as i:
                turned(i + 1)
                state(i)
                keys(i + 1)
                values_of(i + 1, 0)
                key_columns(i, 0)
                values_of(i + 1, 1)
                key_columns(i, 1)
            state(NC - 1)
            pe.wait_ge(gated, 1)
            pe.wait_ge(kb_sb, 2 * NC + 2)
            for b in range(B):
                for t in range(ET):
                    mm = pe.matmul(bank(2, b * D, D), acc[:, t, b * L:(b + 1) * L], w_out[:, t, :],
                                   start=(t == 0), stop=(t == ET - 1))
            mm.then_inc(pe_step, 1)
            key_columns(NC - 1, 0)
            key_columns(NC - 1, 1)

            columns(2)
            pe.wait_ge(ln_cols, 3)
            pe.wait_ge(ld_w2, 16)
            pe.wait_ge(v_sb, 2 * NC + 2)
            pe.wait_ge(mix_add, 1)
            for m in range(FT):
                for c in range(CH):
                    mm = pe.matmul(bank(m // 2, (m % 2) * T, T), w_f1[:, c, m * P:(m + 1) * P], xnT[:, c, :],
                                   start=(c == 0), stop=(c == CH - 1))
                if m % 2:
                    mm.then_inc(ff_h, 1)
            pe.wait_ge(ktc_sb, 4 * NC + 2)
            for m in range(FT):
                if m % 2 == 0:
                    pe.wait_ge(ff_a, m // 2 + 1)
                for b in range(B):
                    mm = pe.matmul(bank(4 + b, 0, D), aT[:, m, b * L:(b + 1) * L], w_f2[:, m, :],
                                   start=(m == 0), stop=(m == FT - 1))
            mm.then_inc(pe_step, 1)

            columns(3)
            pe.wait_ge(ln_cols, 4)
            pe.wait_ge(ld_w3a, 16)
            for b in range(B):
                for c in range(CH):
                    mm = pe.matmul(bank(0, b * D, D), xnT[:, c, b * L:(b + 1) * L], w_q[:, c, :],
                                   start=(c == 0), stop=(c == CH - 1))
            mm.then_inc(pe_step, 1)

            def value_rows(n):
                m, q = n // 4, n % 4
                pe.wait_ge(vq_clip, m + 1)
                if n >= 2:
                    pe.wait_ge(vr_sb, n - 1)
                else:
                    pe.wait_ge(ff_add, 1)
                for t in range(8):
                    k = (8 * q + t) * P
                    mm = pe.transpose(bank(5 + n % 2, 0, 512).bitcast(BF16)[:, t * P:(t + 1) * P], vqb[:, m, k:k + P], identb[:, :])
                mm.then_inc(vr_tr, 1)

            for n in range(4):
                value_rows(n)
            pe.wait_ge(q3_ready, 1)
            for b in range(B):
                for p in range(PAIRS):
                    dst = bank((4, 7)[b], 0, 512, 0, PR).bitcast(BF16)[:, p * P:(p + 1) * P]
                    mm = pe.transpose(dst, q3[:, b * H + 2 * p:b * H + 2 * p + 2].rearrange("q h a d -> q (h a d)"), identb[:, :])
            mm.then_inc(pe_step, 1)
            pe.nop().then_inc(ptr_used, 4)
            pe.nop().then_inc(t_ps, 8)

            def scores(it, j, c, early=False):
                u, slot = 8 * it + j, j // 4
                q = KEYS + (j // 2 % 2) * T + (j % 2) * L
                queries = kqs[:, slot, q:q + L]
                if early:
                    pe.wait_ge(qz_ready[j % 2], j // 2 + 1)
                    queries = qz[:, 0, j // 2 % 2, (j % 2) * L:(j % 2 + 1) * L]
                if j % 4 == 0 and c == 0:
                    pe.wait_ge(ld_keys[slot], 16 * it + 16)
                    if not early:
                        pe.wait_ge(ld_queries[slot], 16 * it + 16)
                pe.wait_ge(s_read, 4 * u + c + 1)
                for m in range(2):
                    k = c * 1024 + m * 512
                    mm = pe.matmul(bank(2 * (c % 2) + m, 0, 512), queries, kqs[:, slot, k:k + 512],
                                   start=True, stop=True)
                mm.then_inc(s_ps, 1)

            def turned_over(it, j, c):
                u = 8 * it + j
                if c % 2 == 0:
                    pe.wait_ge(p_ready, 2 * u + c // 2 + 5)
                who, count = ((0, 1), (1, 2), (0, 2), (1, 3))[c]
                pe.wait_ge(ptr_sb[who], 2 * u + count)
                words = p8[:, j % 2].bitcast(F32)
                for n in range(4):
                    w = (4 * c + n) * P
                    mm = pe.transpose(bank((4, 5, 6, 5)[c], n * P, P), words[:, w:w + P], ident)
                mm.then_inc(t_ps, 1)

            def weighted(it, j, c):
                u, slot = 8 * it + j, j // 4
                pe.wait_ge(ptr_sb[c % 2], 2 * u + c // 2 + 3)
                if j % 4 == 0 and c == 0:
                    pe.wait_ge(ld_vss[slot], 16 * it + 16)
                    pe.wait_ge(o_read, 2 * it + j // 4 + 2)
                for n in range(4):
                    for par in range(2):
                        t = 2 * (4 * c + n) + par
                        v = t * 2 * HW + (j // 2 % 2) * HW
                        mm = pe.matmul(bank(7, (j % 4) * HW, HW), ptr[:, c, n * 2 * P + par:(n + 1) * 2 * P:2],
                                       vss[:, slot, v:v + HW], start=(t == 0), stop=(t == KT - 1))
                mm.then_inc(ptr_used, 1)

            def turn(it, j, ahead=True, early=False):
                for c in range(4):
                    if ahead:
                        scores(*unit(it, j + 2), c, early)
                    turned_over(*unit(it, j), c)
                    if c >= 2:
                        weighted(*unit(it, j), c - 2)
                    elif j:
                        weighted(*unit(it, j - 1), c + 2)

            for j in range(2):
                for c in range(4):
                    scores(0, j, c, early=True)
                    if j == 0:
                        value_rows(4 + c)
            pe.wait_ge(vr_sb, 8)
            pe.wait_ge(qz_ready[0], 2)
            pe.wait_ge(qz_ready[1], 2)
            turn(0, 0, early=True)
            pe.wait_ge(ld_queries[0], 16)
            with pe.Fori(0, UNITS // 8 - 1) as it:
                for j in range(1, 9):
                    turn(it, j)
            for j in range(1, 8):
                turn(UNITS // 8 - 1, j, ahead=j < 6)
            for c in range(2, 4):
                weighted(UNITS // 8 - 1, 7, c)

            pe.wait_ge(on_rows, 1)
            for c in range(CH):
                for b in range(B):
                    mm = pe.transpose(bank(4, c * T + b * L, P), onrm[:, b, c * P:(c + 1) * P], ident)
            mm.then_inc(pe_step, 1)
            pe.wait_ge(on_cols, CH)
            for b in range(B):
                for c in range(CH):
                    mm = pe.matmul(bank(5, b * D, D), onT[:, c, b * L:(b + 1) * L], w_p[:, c, :],
                                   start=(c == 0), stop=(c == CH - 1))
            mm.then_inc(pe_step, 1)

            columns(4)
            pe.wait_ge(ln_cols, 5)
            pe.wait_ge(ld_w3b, 16)
            def projected(b, part, bk):
                for c in range(CH):
                    mm = pe.matmul(bank(bk, 0, D), xnT[:, c, b * L:(b + 1) * L], w_qkv[:, c, part * D:(part + 1) * D],
                                   start=(c == 0), stop=(c == CH - 1))
                return mm

            projected(1, 0, 2).then_inc(pe_step, 1)
            projected(0, 1, 0)
            projected(1, 1, 1).then_inc(pe_step, 1)
            projected(0, 2, 5)
            projected(1, 2, 6).then_inc(pe_step, 1)
            pe.wait_ge(oa_rows, B)
            for c in range(CH):
                for b in range(B):
                    mm = pe.transpose(bank(3, c * T + b * L, P), orow[:, b, c * P:(c + 1) * P], ident)
            mm.then_inc(pe_step, 1)
            pe.wait_ge(oa_cols, 1)
            for b in range(B):
                for c in range(CH):
                    mm = pe.matmul(bank(4, b * D, D), oaT[:, c, b * L:(b + 1) * L], w_ao[:, c, :],
                                   start=(c == 0), stop=(c == CH - 1))
            mm.then_inc(pe_step, 1)

            columns(5)
            pe.wait_ge(ln_cols, 6)
            pe.wait_ge(qkv_used, 1)
            for b in range(B):
                for c in range(CH):
                    mm = pe.matmul(bank(7, b * E, E), xnT[:, c, b * L:(b + 1) * L], w_rt[:, c, :],
                                   start=(c == 0), stop=(c == CH - 1))
            mm.then_inc(pe_step, 1)
            for m in range(FT + 1):
                if m >= 4:
                    pe.wait_ge(moe_h, m - 3)
                for n, w in ((0, w_sg), (1, w_su)):
                    for c in range(CH):
                        mm = pe.matmul(bank(m % 4, n * T, T), w[:, c, m * P:(m + 1) * P], xnT[:, c, :],
                                       start=(c == 0), stop=(c == CH - 1))
                mm.then_inc(moe_gu, 1)
            pe.wait_ge(moe_h, FT)
            for b in range(B):
                for m in range(FT):
                    mm = pe.matmul(bank(5, b * D, D), hT[:, m, b * L:(b + 1) * L], w_sd[:, m, :],
                                   start=(m == 0), stop=(m == FT - 1))
            mm.then_inc(moe_out, 1)
            pe.wait_ge(moe_h, FT + 1)
            for b in range(B):
                mm = pe.matmul(bank(6, b * D, D), hT[:, FT, b * L:(b + 1) * L], w_sd[:, FT, :], start=True, stop=True)
            mm.then_inc(moe_out, 1)




def constants():
    import numpy as np

    half = R // 2
    inv = (1.0 / 10000.0 ** (np.arange(half, dtype=np.float32) / np.float32(half))).astype(np.float32)
    ang = np.arange(NKEY, dtype=np.float32)[:, None] * inv
    cos, sin = np.cos(ang).astype(np.float32), np.sin(ang).astype(np.float32)
    rope = np.concatenate([cos, cos, -sin, sin], 1)
    cst = np.zeros((P, CST), np.float32)
    cst[:, 0:128] = np.eye(P)
    cst[R:, 128:256] = rope[:L, 0:R].T
    cst[R:, 256:384] = rope[:L, R:].T
    cst[:, 384:512] = 1.0
    cst[:, 512:520] = np.where(np.arange(P)[:, None] % GQ == np.arange(GQ), 0.0, NEG)
    cst[:, 520:529] = np.arange(WIN)
    cst[:, 529] = MAGIC
    return cst, rope


def kernel(**inputs):
    import numpy as np
    import concourse.bacc as bacc
    from concourse.bass_utils import run_bass_kernel_spmd

    a = {k: np.asarray(v) for k, v in inputs.items()}

    def rows(w, n=P):
        return w.reshape(-1, n, w.shape[-1]).transpose(1, 0, 2).reshape(n, -1)

    def full(w):
        out = np.zeros((P, w.shape[1]), w.dtype)
        out[:w.shape[0]] = w
        return out

    def over(v):
        return np.broadcast_to(v, (P, v.shape[-1]))

    uq = a["L0_xattn_W_uq"].reshape(QC, H, HD)
    uk = a["L0_xattn_W_uk"].reshape(KVC, H, HD)
    uv = a["L0_xattn_W_uv"].reshape(KVC, H, HD)
    qr = a["L0_xattn_W_qr"].reshape(QC, H, R)
    kvc = rows(a["L0_xattn_W_kvc"]).reshape(P, CH, KVC)
    w0a = np.concatenate([
        uq.transpose(2, 1, 0).reshape(P, -1),
        uk.transpose(2, 1, 0).reshape(P, -1),
        full(a["L0_xattn_W_kvc"].T),
        full(a["L0_xattn_W_kr"]),
    ], 1)
    w0q = np.concatenate([
        rows(a["L0_xattn_W_dq"]),
        np.concatenate([kvc, np.zeros_like(kvc)], 2).reshape(P, -1),
        full(qr.reshape(QC, -1)),
    ], 1)
    w0b = np.concatenate([uv.transpose(2, 1, 0).reshape(P, -1), rows(a["L0_xattn_W_o"])], 1)
    w1 = np.concatenate([
        rows(a["L0_attn_W_in"].T), rows(a["L0_attn_W_x"].T), a["L0_attn_W_dt"].T, rows(a["L0_attn_W_out"].T),
        rows(a["L0_attn_conv_w"]), rows(a["L0_attn_conv_b"][:, None]), rows(a["L0_attn_b_dt"][:, None]),
        rows(a["L0_attn_Dp"][:, None]), rows(a["L0_attn_A_log"]), rows(a["L1_xattn_Wkv"]),
        over(a["L1_xattn_bkv"][:D]), rows(a["L1_xattn_bkv"][D:, None]),
    ], 1)
    w2 = np.concatenate([rows(a["L0_ffn_W1"].T), rows(a["L0_ffn_W2"].T)], 1)

    def beside(s, r):
        return np.concatenate([rows(s).reshape(P, CH, -1), rows(r).reshape(P, CH, -1)], 2).reshape(P, -1)

    w3 = np.concatenate([
        rows(a["L1_xattn_Wq"]), over(a["L1_xattn_bq"]), rows(a["L1_xattn_Wp"]), over(a["L1_xattn_bp"]),
        rows(a["L1_attn_weight_qkv"].T), rows(a["L1_attn_weight_out"].T),
        beside(a["L1_ffn_sh_gate"].T, a["L1_ffn_r_gate"].T), beside(a["L1_ffn_sh_up"].T, a["L1_ffn_r_up"].T),
        rows(a["L1_ffn_sh_down"].T), rows(a["L1_ffn_r_down"].T), rows(a["L1_ffn_router_weight"].T),
    ], 1)
    seg = a["itok_BxS_0_1023"].reshape(NG, GQ)
    cst, rope = constants()
    arrays = {
        "x": a["x"].transpose(1, 0, 2),
        "seg": a["itok_BxS_0_1023"].T,
        "segg": np.broadcast_to(seg.T[None], (H, GQ, NG)).reshape(P, NG),
        "context": a["ctx_2048"].reshape(KEYS, D),
        "rope": rope, "cst": cst, "w0a": w0a, "w0q": w0q, "w0b": w0b, "w1": w1, "w2": w2, "w3": w3,
    }
    arrays = {f"in_{k}": np.ascontiguousarray(v) for k, v in arrays.items()}
    nc = bacc.Bacc("TRN2", target_bir_lowering=False, num_devices=1)
    args = [nc.dram_tensor(k, v.shape, mybir.dt.from_np(v.dtype), kind="ExternalInput").ap() for k, v in arrays.items()]
    out = nc.dram_tensor("out", (P, B, D), F32, kind="ExternalOutput").ap()
    perceiver_kernel(nc, *args, out)
    r = run_bass_kernel_spmd(nc, [arrays], core_ids=[0])
    return np.asarray(r.results[0]["out"]).transpose(1, 0, 2)
```
